# Optimizing a Trainium2 kernel written in Bass

```python
import numpy as np
import jax
import jax.numpy as jnp

def _softmax(x, axis=-1):
    return jax.nn.softmax(x, axis=axis)

def _gelu(x):
    return jax.nn.gelu(x, approximate=True)

def _silu(x):
    return jax.nn.silu(x)

def _sigmoid(x):
    return jax.nn.sigmoid(x)

def _layernorm(x, axis=-1, eps=1e-05):
    m = jnp.mean(x, axis=axis, keepdims=True)
    v = jnp.var(x, axis=axis, keepdims=True)
    return (x - m) / jnp.sqrt(v + eps)

def _scatter_add(tgt, idx, src, axis=0):
    return tgt.at[idx].add(src)

def _segment_sum(src, seg, n):
    return jax.ops.segment_sum(src, seg, n)
kernel_name = 'mk_seq_preln_d2_jaxref_r4_0e266a'

def setup_inputs(seed: int=0):
    np.random.seed(seed)
    _w = jnp.asarray

    def _L0_attn_setup():
        import jax, jax.numpy as jnp
        import numpy as np
        B, S, D, DS = (8, 512, 256, 64)
        TEMP = 1.0
        IMP_TH, SUR_TH = (0.5, 0.7)

        def _l2norm(x):
            return x / jnp.maximum(jnp.linalg.norm(x, axis=-1, keepdims=True), 1e-12)
        key = jax.random.key(seed)
        ks = jax.random.split(key, 12)
        s = 0.02
        return {'x': jax.random.normal(ks[0], (B, S, D), jnp.float32), 'Wk': jax.random.normal(ks[1], (DS, D), jnp.float32) * s, 'Wv': jax.random.normal(ks[2], (DS, D), jnp.float32) * s, 'Wq': jax.random.normal(ks[3], (DS, D), jnp.float32) * s, 'fast_alpha': jnp.float32(0.8), 'slow_alpha': jnp.float32(0.99), 'nm_w1': jax.random.normal(ks[4], (2 * DS, DS), jnp.float32) * s, 'nm_b1': jnp.zeros((2 * DS,), jnp.float32), 'nm_w2': jax.random.normal(ks[5], (DS, 2 * DS), jnp.float32) * s, 'nm_b2': jnp.zeros((DS,), jnp.float32), 'ir_w1': jax.random.normal(ks[6], (DS, D), jnp.float32) * s, 'ir_b1': jnp.zeros((DS,), jnp.float32), 'ir_w2': jax.random.normal(ks[7], (1, DS), jnp.float32) * s, 'ir_b2': jnp.zeros((1,), jnp.float32), 'pw': jax.random.normal(ks[8], (3, D), jnp.float32) * s, 'Wo': jax.random.normal(ks[9], (D, DS), jnp.float32) * s, 'norm_w': jnp.ones((DS,), jnp.float32)}
    _L0_attn_in = _L0_attn_setup()

    def _L0_ffn_setup():
        import jax, jax.numpy as jnp
        import numpy as np
        EMBED_DIM = 256
        HIDDEN_DIM = 1024
        NUM_EXPERTS = 8
        TOP_K = 2
        key = jax.random.key(seed)
        ks = jax.random.split(key, 4)
        std1 = float(np.sqrt(2.0 / EMBED_DIM))
        std2 = float(np.sqrt(2.0 / HIDDEN_DIM))
        x = jax.random.normal(ks[0], (1, 512, EMBED_DIM), dtype=jnp.float32)
        w_router = jax.random.normal(ks[1], (EMBED_DIM, NUM_EXPERTS), dtype=jnp.float32) * 0.02
        w1 = jax.random.normal(ks[2], (NUM_EXPERTS, EMBED_DIM, HIDDEN_DIM), dtype=jnp.float32) * std1
        b1 = jnp.zeros((NUM_EXPERTS, HIDDEN_DIM), dtype=jnp.float32)
        w2 = jax.random.normal(ks[3], (NUM_EXPERTS, HIDDEN_DIM, EMBED_DIM), dtype=jnp.float32) * std2
        b2 = jnp.zeros((NUM_EXPERTS, EMBED_DIM), dtype=jnp.float32)
        return {'x': x, 'w_router': w_router, 'w1': w1, 'b1': b1, 'w2': w2, 'b2': b2}
    _L0_ffn_in = _L0_ffn_setup()

    def _L1_attn_setup():
        import jax, jax.numpy as jnp
        import numpy as np
        LN_EPS = 1e-05
        WKV_EPS = 1e-08
        NEG_INF = -1e+38

        def _layernorm(x, g, b):
            m = jnp.mean(x, axis=-1, keepdims=True)
            v = jnp.mean(jnp.square(x - m), axis=-1, keepdims=True)
            return (x - m) * jax.lax.rsqrt(v + LN_EPS) * g + b

        def _wkv(w, u, k, v):
            B, T, C = k.shape
            aa0 = jnp.zeros((B, C), k.dtype)
            bb0 = jnp.full((B, C), NEG_INF, k.dtype)

            def step(carry, kv_t):
                aa, bb = carry
                kk, vv = kv_t
                ww = u + kk
                p = jnp.maximum(bb, ww)
                e1 = jnp.exp(bb - p)
                e2 = jnp.exp(ww - p)
                y_t = (e1 * aa + e2 * vv) / (e1 + e2 + WKV_EPS)
                ww = w + bb
                p = jnp.maximum(ww, kk)
                e1 = jnp.exp(ww - p)
                e2 = jnp.exp(kk - p)
                aa = e1 * aa + e2 * vv
                bb = p + jnp.log(e1 + e2 + WKV_EPS)
                return ((aa, bb), y_t)
            (aa, bb), ys = jax.lax.scan(step, (aa0, bb0), (jnp.swapaxes(k, 0, 1), jnp.swapaxes(v, 0, 1)))
            y = jnp.swapaxes(ys, 0, 1)
            new_state = jnp.stack([aa, bb], axis=-1)
            return (y, new_state)

        def _reference_tuple_inner(x, time_decay, time_first, W_tm, g1, b1, tmk, tmv, tmr, W_cm, W_cp, g2, b2, cmk, cmr):
            x_prev = jnp.concatenate([x[:, :1], x[:, :-1]], axis=1)
            kvr = _layernorm(x, g1, b1) @ W_tm
            k, v, r = jnp.split(kvr, 3, axis=-1)
            k = k * tmk + x_prev * (1.0 - tmk)
            v = v * tmv + x_prev * (1.0 - tmv)
            r = jax.nn.sigmoid(r * tmr + x_prev * (1.0 - tmr))
            y, new_state = _wkv(time_decay, time_first, k, v)
            x = x + r * y
            xp = jnp.concatenate([x[:, -1:], x[:, :-1]], axis=1)
            xn = _layernorm(x, g2, b2)
            kk = xn @ W_cm
            cmk4 = jnp.tile(cmk, (1, 1, 4))
            xp4 = jnp.tile(xp, (1, 1, 4))
            kk = kk * cmk4 + xp4 * (1.0 - cmk4)
            rr = jax.nn.sigmoid(xn * cmr + xp * (1.0 - cmr))
            vv = jnp.square(jax.nn.relu(kk)) @ W_cp
            x = x + rr * vv
            return (x, new_state)
        key = jax.random.key(seed)
        ks = jax.random.split(key, 12)
        B, T, C = (8, 512, 256)
        scale = 0.02
        return {'x': jax.random.normal(ks[0], (B, T, C), jnp.float32), 'time_decay': jax.random.uniform(ks[1], (C,), jnp.float32, -1.0, 1.0), 'time_first': jax.random.uniform(ks[2], (C,), jnp.float32, -1.0, 1.0), 'W_tm': jax.random.normal(ks[3], (C, 3 * C), jnp.float32) * scale, 'g1': jnp.ones((C,), jnp.float32), 'b1': jnp.zeros((C,), jnp.float32), 'tmk': jax.random.uniform(ks[4], (1, 1, C), jnp.float32), 'tmv': jax.random.uniform(ks[5], (1, 1, C), jnp.float32), 'tmr': jax.random.uniform(ks[6], (1, 1, C), jnp.float32), 'W_cm': jax.random.normal(ks[7], (C, 4 * C), jnp.float32) * scale, 'W_cp': jax.random.normal(ks[8], (4 * C, C), jnp.float32) * scale, 'g2': jnp.ones((C,), jnp.float32), 'b2': jnp.zeros((C,), jnp.float32), 'cmk': jax.random.uniform(ks[9], (1, 1, C), jnp.float32), 'cmr': jax.random.uniform(ks[10], (1, 1, C), jnp.float32)}
    _L1_attn_in = _L1_attn_setup()

    def _L1_ffn_setup():
        import jax, jax.numpy as jnp
        import numpy as np
        D_IN, D_HID = (256, 1024)

        def _ternary(key, shape):
            return jax.random.randint(key, shape, -1, 2).astype(jnp.float32)

        def _tlin(x, w, s):
            return jnp.einsum('bsi,oi->bso', x, w) * s
        key = jax.random.key(seed)
        ks = jax.random.split(key, 12)
        inv = lambda fan: 1.0 / np.sqrt(fan).astype(np.float32)
        return {'x': jax.random.normal(ks[0], (4, 512, D_IN), dtype=jnp.float32), 'w1_w': _ternary(ks[1], (D_HID, D_IN)), 'w1_s': jax.random.uniform(ks[2], (D_HID,), dtype=jnp.float32) * inv(D_IN), 'w2_w': _ternary(ks[3], (D_HID, D_IN)), 'w2_s': jax.random.uniform(ks[4], (D_HID,), dtype=jnp.float32) * inv(D_IN), 'h1_w': _ternary(ks[5], (D_HID, D_HID)), 'h1_s': jax.random.uniform(ks[6], (D_HID,), dtype=jnp.float32) * inv(D_HID), 'h2_w': _ternary(ks[7], (D_HID, D_HID)), 'h2_s': jax.random.uniform(ks[8], (D_HID,), dtype=jnp.float32) * inv(D_HID), 'w3_w': _ternary(ks[9], (D_IN, D_HID)), 'w3_s': jax.random.uniform(ks[10], (D_IN,), dtype=jnp.float32) * inv(D_HID)}
    _L1_ffn_in = _L1_ffn_setup()
    _d = {'L0_attn_x': _L0_attn_in['x'], 'L0_attn_Wk': _L0_attn_in['Wk'], 'L0_attn_Wv': _L0_attn_in['Wv'], 'L0_attn_Wq': _L0_attn_in['Wq'], 'L0_attn_fast_alpha': _L0_attn_in['fast_alpha'], 'L0_attn_slow_alpha': _L0_attn_in['slow_alpha'], 'L0_attn_nm_w1': _L0_attn_in['nm_w1'], 'L0_attn_nm_b1': _L0_attn_in['nm_b1'], 'L0_attn_nm_w2': _L0_attn_in['nm_w2'], 'L0_attn_nm_b2': _L0_attn_in['nm_b2'], 'L0_attn_ir_w1': _L0_attn_in['ir_w1'], 'L0_attn_ir_b1': _L0_attn_in['ir_b1'], 'L0_attn_ir_w2': _L0_attn_in['ir_w2'], 'L0_attn_ir_b2': _L0_attn_in['ir_b2'], 'L0_attn_pw': _L0_attn_in['pw'], 'L0_attn_Wo': _L0_attn_in['Wo'], 'L0_attn_norm_w': _L0_attn_in['norm_w'], 'L0_ffn_w_router': _L0_ffn_in['w_router'], 'L0_ffn_w1': _L0_ffn_in['w1'], 'L0_ffn_b1': _L0_ffn_in['b1'], 'L0_ffn_w2': _L0_ffn_in['w2'], 'L0_ffn_b2': _L0_ffn_in['b2'], 'L1_attn_time_decay': _L1_attn_in['time_decay'], 'L1_attn_time_first': _L1_attn_in['time_first'], 'L1_attn_W_tm': _L1_attn_in['W_tm'], 'L1_attn_g1': _L1_attn_in['g1'], 'L1_attn_b1': _L1_attn_in['b1'], 'L1_attn_tmk': _L1_attn_in['tmk'], 'L1_attn_tmv': _L1_attn_in['tmv'], 'L1_attn_tmr': _L1_attn_in['tmr'], 'L1_attn_W_cm': _L1_attn_in['W_cm'], 'L1_attn_W_cp': _L1_attn_in['W_cp'], 'L1_attn_g2': _L1_attn_in['g2'], 'L1_attn_b2': _L1_attn_in['b2'], 'L1_attn_cmk': _L1_attn_in['cmk'], 'L1_attn_cmr': _L1_attn_in['cmr'], 'L1_ffn_w1_w': _L1_ffn_in['w1_w'], 'L1_ffn_w1_s': _L1_ffn_in['w1_s'], 'L1_ffn_w2_w': _L1_ffn_in['w2_w'], 'L1_ffn_w2_s': _L1_ffn_in['w2_s'], 'L1_ffn_h1_w': _L1_ffn_in['h1_w'], 'L1_ffn_h1_s': _L1_ffn_in['h1_s'], 'L1_ffn_h2_w': _L1_ffn_in['h2_w'], 'L1_ffn_h2_s': _L1_ffn_in['h2_s'], 'L1_ffn_w3_w': _L1_ffn_in['w3_w'], 'L1_ffn_w3_s': _L1_ffn_in['w3_s']}
    _x0 = _d['L0_attn_x']
    _d['L0_attn_x'] = jax.random.normal(jax.random.fold_in(jax.random.key(seed), 1), (1, 4096, 256), dtype=_x0.dtype)
    del _x0
    return _d

def reference(L0_attn_x, L0_attn_Wk, L0_attn_Wv, L0_attn_Wq, L0_attn_fast_alpha, L0_attn_slow_alpha, L0_attn_nm_w1, L0_attn_nm_b1, L0_attn_nm_w2, L0_attn_nm_b2, L0_attn_ir_w1, L0_attn_ir_b1, L0_attn_ir_w2, L0_attn_ir_b2, L0_attn_pw, L0_attn_Wo, L0_attn_norm_w, L0_ffn_w_router, L0_ffn_w1, L0_ffn_b1, L0_ffn_w2, L0_ffn_b2, L1_attn_time_decay, L1_attn_time_first, L1_attn_W_tm, L1_attn_g1, L1_attn_b1, L1_attn_tmk, L1_attn_tmv, L1_attn_tmr, L1_attn_W_cm, L1_attn_W_cp, L1_attn_g2, L1_attn_b2, L1_attn_cmk, L1_attn_cmr, L1_ffn_w1_w, L1_ffn_w1_s, L1_ffn_w2_w, L1_ffn_w2_s, L1_ffn_h1_w, L1_ffn_h1_s, L1_ffn_h2_w, L1_ffn_h2_s, L1_ffn_w3_w, L1_ffn_w3_s):

    def _L0_attn_ref(x, Wk, Wv, Wq, fast_alpha, slow_alpha, nm_w1, nm_b1, nm_w2, nm_b2, ir_w1, ir_b1, ir_w2, ir_b2, pw, Wo, norm_w):
        import jax, jax.numpy as jnp
        import numpy as np
        B, S, D, DS = (8, 512, 256, 64)
        TEMP = 1.0
        IMP_TH, SUR_TH = (0.5, 0.7)

        def _l2norm(x):
            return x / jnp.maximum(jnp.linalg.norm(x, axis=-1, keepdims=True), 1e-12)
        Bb = x.shape[0]
        k = _l2norm(x @ Wk.T)
        v = x @ Wv.T
        q = _l2norm(x @ Wq.T)
        imp = jax.nn.sigmoid(jax.nn.gelu(x @ ir_w1.T + ir_b1, approximate=False) @ ir_w2.T + ir_b2)
        nu = jax.nn.gelu(v @ nm_w1.T + nm_b1, approximate=False) @ nm_w2.T + nm_b2
        pwt = jax.nn.softmax(x @ pw.T, axis=-1)

        def step(carry, inp):
            fH, sH, ns = carry
            k_t, v_t, q_t, i_t, nu_t, p_t = inp
            pred = (jnp.einsum('bk,bkv->bv', q_t, fH) + jnp.einsum('bk,bkv->bv', q_t, sH)) * 0.5
            err = jnp.sum((v_t - pred) ** 2, axis=-1, keepdims=True)
            surprise = jax.nn.sigmoid(err / (TEMP + 1e-06))
            kv = k_t[:, :, None] * v_t[:, None, :]
            d_fast = kv - k_t[:, :, None] * jnp.einsum('bk,bkv->bv', k_t, fH)[:, None, :]
            fH = fast_alpha * fH + (1 - fast_alpha) * d_fast
            u_slow = (i_t > IMP_TH).astype(x.dtype)
            d_slow = kv - k_t[:, :, None] * jnp.einsum('bk,bkv->bv', k_t, sH)[:, None, :]
            sH = slow_alpha * sH + (1 - slow_alpha) * u_slow[:, :, None] * d_slow
            u_neu = (surprise > SUR_TH).astype(x.dtype)
            ns = ns + u_neu * (nu_t - ns) * 0.1
            o = p_t[:, 0:1] * jnp.einsum('bk,bkv->bv', q_t, fH) + p_t[:, 1:2] * jnp.einsum('bk,bkv->bv', q_t, sH) + p_t[:, 2:3] * ns
            return ((fH, sH, ns), o)
        ds = Wk.shape[0]
        init = (jnp.zeros((Bb, ds, ds), x.dtype), jnp.zeros((Bb, ds, ds), x.dtype), jnp.zeros((Bb, ds), x.dtype))
        xs = (k.transpose(1, 0, 2), v.transpose(1, 0, 2), q.transpose(1, 0, 2), imp.transpose(1, 0, 2), nu.transpose(1, 0, 2), pwt.transpose(1, 0, 2))
        _, out = jax.lax.scan(step, init, xs)
        out = out.transpose(1, 0, 2)
        of = out.astype(jnp.float32)
        of = of * jax.lax.rsqrt(jnp.mean(of * of, axis=-1, keepdims=True) + 1e-06)
        out = (of * norm_w).astype(out.dtype)
        return out @ Wo.T

    def _L0_ffn_ref(x, w_router, w1, b1, w2, b2):
        import jax, jax.numpy as jnp
        import numpy as np
        EMBED_DIM = 256
        HIDDEN_DIM = 1024
        NUM_EXPERTS = 8
        TOP_K = 2
        orig_shape = x.shape
        xf = x.reshape(-1, EMBED_DIM)
        logits = xf @ w_router
        probs = jax.nn.softmax(logits, axis=-1)
        topk_w, topk_idx = jax.lax.top_k(probs, TOP_K)
        mask = jax.nn.one_hot(topk_idx, NUM_EXPERTS, dtype=xf.dtype)
        weights = jnp.sum(topk_w[..., None] * mask, axis=1)
        h = jnp.einsum('te,ieh->tih', xf, w1) + b1
        h = jax.nn.gelu(h)
        out = jnp.einsum('tih,ihe->tie', h, w2) + b2
        out = jnp.sum(out * weights[..., None], axis=1)
        return out.reshape(orig_shape)

    def _L1_attn_ref(x, time_decay, time_first, W_tm, g1, b1, tmk, tmv, tmr, W_cm, W_cp, g2, b2, cmk, cmr):
        import jax, jax.numpy as jnp
        import numpy as np
        LN_EPS = 1e-05
        WKV_EPS = 1e-08
        NEG_INF = -1e+38

        def _layernorm(x, g, b):
            m = jnp.mean(x, axis=-1, keepdims=True)
            v = jnp.mean(jnp.square(x - m), axis=-1, keepdims=True)
            return (x - m) * jax.lax.rsqrt(v + LN_EPS) * g + b

        def _wkv(w, u, k, v):
            B, T, C = k.shape
            aa0 = jnp.zeros((B, C), k.dtype)
            bb0 = jnp.full((B, C), NEG_INF, k.dtype)

            def step(carry, kv_t):
                aa, bb = carry
                kk, vv = kv_t
                ww = u + kk
                p = jnp.maximum(bb, ww)
                e1 = jnp.exp(bb - p)
                e2 = jnp.exp(ww - p)
                y_t = (e1 * aa + e2 * vv) / (e1 + e2 + WKV_EPS)
                ww = w + bb
                p = jnp.maximum(ww, kk)
                e1 = jnp.exp(ww - p)
                e2 = jnp.exp(kk - p)
                aa = e1 * aa + e2 * vv
                bb = p + jnp.log(e1 + e2 + WKV_EPS)
                return ((aa, bb), y_t)
            (aa, bb), ys = jax.lax.scan(step, (aa0, bb0), (jnp.swapaxes(k, 0, 1), jnp.swapaxes(v, 0, 1)))
            y = jnp.swapaxes(ys, 0, 1)
            new_state = jnp.stack([aa, bb], axis=-1)
            return (y, new_state)

        def _reference_tuple_inner(x, time_decay, time_first, W_tm, g1, b1, tmk, tmv, tmr, W_cm, W_cp, g2, b2, cmk, cmr):
            x_prev = jnp.concatenate([x[:, :1], x[:, :-1]], axis=1)
            kvr = _layernorm(x, g1, b1) @ W_tm
            k, v, r = jnp.split(kvr, 3, axis=-1)
            k = k * tmk + x_prev * (1.0 - tmk)
            v = v * tmv + x_prev * (1.0 - tmv)
            r = jax.nn.sigmoid(r * tmr + x_prev * (1.0 - tmr))
            y, new_state = _wkv(time_decay, time_first, k, v)
            x = x + r * y
            xp = jnp.concatenate([x[:, -1:], x[:, :-1]], axis=1)
            xn = _layernorm(x, g2, b2)
            kk = xn @ W_cm
            cmk4 = jnp.tile(cmk, (1, 1, 4))
            xp4 = jnp.tile(xp, (1, 1, 4))
            kk = kk * cmk4 + xp4 * (1.0 - cmk4)
            rr = jax.nn.sigmoid(xn * cmr + xp * (1.0 - cmr))
            vv = jnp.square(jax.nn.relu(kk)) @ W_cp
            x = x + rr * vv
            return (x, new_state)
        return _reference_tuple_inner(x, time_decay, time_first, W_tm, g1, b1, tmk, tmv, tmr, W_cm, W_cp, g2, b2, cmk, cmr)[0]

    def _L1_ffn_ref(x, w1_w, w1_s, w2_w, w2_s, h1_w, h1_s, h2_w, h2_s, w3_w, w3_s):
        import jax, jax.numpy as jnp
        import numpy as np
        D_IN, D_HID = (256, 1024)

        def _ternary(key, shape):
            return jax.random.randint(key, shape, -1, 2).astype(jnp.float32)

        def _tlin(x, w, s):
            return jnp.einsum('bsi,oi->bso', x, w) * s
        h = jax.nn.silu(_tlin(x, w1_w, w1_s)) * _tlin(x, w2_w, w2_s)
        h = jax.nn.gelu(_tlin(h, h1_w, h1_s), approximate=False)
        h = jax.nn.gelu(_tlin(h, h2_w, h2_s), approximate=False)
        return _tlin(h, w3_w, w3_s)
    x = L0_attn_x
    x = x + _L0_attn_ref(_layernorm(x, axis=-1), L0_attn_Wk, L0_attn_Wv, L0_attn_Wq, L0_attn_fast_alpha, L0_attn_slow_alpha, L0_attn_nm_w1, L0_attn_nm_b1, L0_attn_nm_w2, L0_attn_nm_b2, L0_attn_ir_w1, L0_attn_ir_b1, L0_attn_ir_w2, L0_attn_ir_b2, L0_attn_pw, L0_attn_Wo, L0_attn_norm_w)
    x = x + _L0_ffn_ref(_layernorm(x, axis=-1), L0_ffn_w_router, L0_ffn_w1, L0_ffn_b1, L0_ffn_w2, L0_ffn_b2)
    x = x + _L1_attn_ref(_layernorm(x, axis=-1), L1_attn_time_decay, L1_attn_time_first, L1_attn_W_tm, L1_attn_g1, L1_attn_b1, L1_attn_tmk, L1_attn_tmv, L1_attn_tmr, L1_attn_W_cm, L1_attn_W_cp, L1_attn_g2, L1_attn_b2, L1_attn_cmk, L1_attn_cmr)
    x = x + _L1_ffn_ref(_layernorm(x, axis=-1), L1_ffn_w1_w, L1_ffn_w1_s, L1_ffn_w2_w, L1_ffn_w2_s, L1_ffn_h1_w, L1_ffn_h1_s, L1_ffn_h2_w, L1_ffn_h2_s, L1_ffn_w3_w, L1_ffn_w3_s)
    return x

_drawn_inputs = setup_inputs


def setup_inputs(seed=0):
    import zlib

    import numpy as np

    out = dict(_drawn_inputs(seed))
    spreads = {'L0_attn_nm_b1': (0.0, 0.1),
     'L0_attn_nm_b2': (0.0, 0.1),
     'L0_attn_ir_b1': (0.0, 0.1),
     'L0_attn_norm_w': (1.0, 0.2),
     'L0_ffn_b1': (0.0, 0.1),
     'L0_ffn_b2': (0.0, 0.1),
     'L1_attn_g1': (1.0, 0.2),
     'L1_attn_b1': (0.0, 0.1),
     'L1_attn_g2': (1.0, 0.2),
     'L1_attn_b2': (0.0, 0.1)}
    factors = {}
    for name, (base, spread) in spreads.items():
        noise = np.random.default_rng([zlib.crc32(name.encode()), seed]).standard_normal(out[name].shape)
        drawn = base * np.exp(spread * noise) if base else spread * noise
        out[name] = jnp.asarray(drawn.astype(out[name].dtype))
    for name, factor in factors.items():
        out[name] = (out[name] * factor).astype(out[name].dtype)
    return out
```

```python
import concourse.bass as bass
from concourse import mybir
from contextlib import ExitStack

S, D, DS, HID, NE = 4096, 256, 64, 1024, 8
CH = 128
NC = S // CH
KT = D // 128
BT = 512
NB = S // BT
CPB = BT // CH
PJ = 3 * DS + 3
LOGIT = 0.8472978603872034
LEVELS = 7
TT = 256
MT = 2 * S // TT + NE


class Steps:

    def __init__(self, eng, sem):
        self.eng, self.sem, self.done, self.here, self.at = eng, sem, 0, 0, None

    def turn(self, i, per):
        self.at, self.per, self.here = i, per, 0

    def end(self, turns):
        assert self.here == self.per, (self.here, self.per)
        self.done += turns * self.per
        self.at, self.here = None, 0

    def __call__(self, ins):
        ins.then_inc(self.sem, 1)
        if self.at is None:
            self.done += 1
            self.eng.wait_ge(self.sem, self.done)
        else:
            self.here += 1
            self.eng.wait_ge(self.sem, self.at * self.per + (self.done + self.here))


def build(nc, A):
    fp32, f32r, i32, u32 = mybir.dt.float32, mybir.dt.float32r, mybir.dt.int32, mybir.dt.uint32
    ALU, ACT, AX = mybir.AluOpType, mybir.ActivationFunctionType, mybir.AxisListType
    ds = bass.ds

    ctx = ExitStack()
    with ctx:
        def sem(name):
            return ctx.enter_context(nc.semaphore(name))

        def bank(name):
            return ctx.enter_context(nc.psum_tensor(name, [128, 512], fp32))

        raw = {}
        for n, rows, cols in (("w1", D, HID), ("w2", D, HID), ("h1", HID, HID), ("h2", HID, HID), ("w3", HID, D)):
            raw[n] = nc.dram_tensor("ffn_copy_" + n, (rows, cols), fp32, kind="Internal").ap()
        x_tok_d = A["x"].rearrange("o (c p) d -> p (o c) d", p=CH)
        z1_d = nc.dram_tensor("z1_sorted", (MT * TT, D), fp32, kind="Internal").ap()
        ym_d = nc.dram_tensor("moe_sorted", (MT * TT, D), fp32, kind="Internal").ap()

        def sb(name, shape, dt=fp32, to=None):
            return (to or ctx).enter_context(nc.sbuf_tensor(name, shape, dt))

        ident = sb("ident", [128, 128])
        one_m = sb("one_m", [128, 128])
        slot1 = sb("slot1", [128, NC], i32)
        slot2 = sb("slot2", [128, NC], i32)
        gate1 = sb("gate1", [128, NC])
        gate2 = sb("gate2", [128, NC])
        tiles = sb("tiles", [1, NE], i32)
        tiles0 = sb("tiles0", [1, NE + 1], i32)
        small = sb("small", [128, 16, NC])
        sc8 = sb("sc8", [128, 8])

        NV = 15
        (W_, U_, TMK, TMV, TMR, G1, B1, G2, B2, CMK, CMR, QMK, QMV, QMR, QCK) = range(NV)
        QCR = NV
        vec = sb("vec", [128, NV + 1, KT])
        epsv = sb("epsv", [128, 2])
        avg = sb("avg", [128, 128])
        px = ctx.enter_context(ExitStack())
        x_tok = sb("x_tok", [128, NC, D], to=px)

        pa = ctx.enter_context(ExitStack())
        PR = sb("PR", [128, NC, 200], to=pa)
        WP = sb("WP", [128, NC, 256], to=pa)
        NU = sb("NU", [DS, S], to=pa)
        wcat = sb("wcat", [128, KT, PJ], to=pa)
        wvT = sb("wvT", [128, KT, DS], to=pa)
        ir1T = sb("ir1T", [128, KT, DS], to=pa)
        ir2T = sb("ir2T", [DS, 1], to=pa)
        nm1T = sb("nm1T", [DS, 2 * DS], to=pa)
        nm2T = sb("nm2T", [2 * DS, DS], to=pa)
        wroT = sb("wroT", [128, KT, NE], to=pa)
        woT = sb("woT", [DS, D], to=pa)
        woN = sb("woN", [DS, D], to=pa)
        b_ir1 = sb("b_ir1", [DS, 1], to=pa)
        b_nm1 = sb("b_nm1", [2 * DS, 1], to=pa)
        b_nm2 = sb("b_nm2", [DS, 1], to=pa)
        normw = sb("normw", [DS, 1], to=pa)
        scal = sb("scal", [128, 4], to=pa)
        st = sb("st", [128, NC, 6], to=pa)
        mv = sb("mv", [128, NC, 2], to=pa)
        zt = sb("zt", [128, 2, D], to=pa)
        zT = sb("zT", [128, KT, BT], to=pa)
        vT = sb("vT", [DS, BT], to=pa)
        gT = sb("gT", [DS, BT], to=pa)
        hT = sb("hT", [128, BT], to=pa)
        maskL = sb("maskL", [128, 2, 2, 128], to=pa)
        maskQ = sb("maskQ", [128, 2, 128], to=pa)
        pw_s = sb("pw_s", [128, 2, 132], to=pa)
        lam = sb("lam", [128, 2], to=pa)
        rev = sb("rev", [128, 2], to=pa)
        beta = sb("beta", [128, 2], to=pa)
        blam = sb("blam", [128, 2], to=pa)
        alC = sb("alC", [128, 2], to=pa)
        state = sb("state", [DS, 2, DS], to=pa)
        KQ = sb("KQ", [128, 2, 5, DS], to=pa)
        KR = sb("KR", [128, 2, 2, DS], to=pa)
        KQT = sb("KQT", [DS, 2, 5, 128], to=pa)
        X = sb("X", [128, 2, 2, 128], to=pa)
        L = sb("L", [128, 2, 2, 4, 128], to=pa)
        QM = sb("QM", [128, 2, 2, 128], to=pa)
        YT = sb("YT", [DS, 2, 2, 128], to=pa)
        ubc = sb("ubc", [128, 2, DS], to=pa)
        aN = sb("aN", [DS, 2, 128], to=pa)
        bN = sb("bN", [DS, 2, 128], to=pa)
        nsT = sb("nsT", [DS, 2, 128], to=pa)
        oT = sb("oT", [DS, 2, 128], to=pa)
        ot = sb("ot", [128, 2, DS], to=pa)
        ts = sb("ts", [128, 2, DS], to=pa)
        z1T = sb("z1T", [128, 2, KT, 128], to=pa)
        LG = sb("LG", [128, NC, NE], to=pa)
        big = sb("big", [128, NC, DS], to=pa)
        rt = sb("rt", [128, 6, NC, NE], to=pa)
        top8 = sb("top8", [128, NC, 8], to=pa)
        idx8 = sb("idx8", [128, NC, 8], u32, to=pa)
        iota8 = sb("iota8", [128, NC, NE], to=pa)
        base8 = sb("base8", [128, NE], to=pa)
        tri = sb("tri", [128, 128], to=pa)
        cnt8 = sb("cnt8", [128, 4, NE], to=pa)
        zero = sb("zero", [128, 8 * D], to=pa)

        B = [bank(f"bank{i}") for i in range(8)]

        ld_x, ld_w, ld_s = sem("x_loaded"), sem("weights_loaded"), sem("scalars_loaded")
        consts = sem("constants_ready")
        d_st, a_st, p_st = sem("vector_steps"), sem("scalar_steps"), sem("pool_steps")
        z_rdy, zps_rdy, zT_rdy = sem("z_ready"), sem("zT_in_psum"), sem("zT_ready")
        pj_ps, pj_out = sem("projection_in_psum"), sem("projection_taken")
        ti_ps, gT_rdy, vT_rdy = sem("vT_irT_in_psum"), sem("gT_ready"), sem("vT_ready")
        hd_ps, hd_rdy, nu_ps, nu_out = sem("nm_hidden_in_psum"), sem("nm_hidden_ready"), sem("nu_imp_in_psum"), sem("nu_imp_taken")
        sq_rdy, sq_done = sem("sqrt_wanted"), sem("sqrt_done")
        kq_rdy, kqt_ps, kqt_rdy = sem("kq_ready"), sem("kqT_in_psum"), sem("kqT_ready")
        g_ps, l_rdy = sem("gram_in_psum"), sem("L_ready")
        sq_ps, sq_cp = sem("square_in_psum"), sem("square_taken")
        ap_ps, ap_rdy = sem("LX_in_psum"), sem("X_ready")
        yt_ps, yt_rdy = sem("YT_in_psum"), sem("YT_ready")
        w_ps, w_rdy, f_ps, f_rdy, pp_ps, pp_rdy = (sem("Yf_in_psum"), sem("w_ready"), sem("Kw_in_psum"),
                                                   sem("state_ready"), sem("pred_in_psum"), sem("pred_taken"))
        ub_rdy, ub_ps, ns_rdy, nst_ps, o_rdy, ot_ps, oT_rdy, wo_ps, wo_out = (
            sem("u_copied"), sem("u_rows_in_psum"), sem("ns_ready"), sem("nsT_back_in_psum"), sem("o_ready"),
            sem("oT_in_psum"), sem("oT_ready"), sem("attn_out_in_psum"), sem("x1_ready"))
        z1_rdy, z1_ps, z1T_rdy, lg_ps, lg_out = (sem("z1_ready"), sem("z1T_in_psum"), sem("z1T_ready"),
                                                sem("logits_in_psum"), sem("logits_taken"))
        rk_rdy, rk_ps, route_rdy, scat = sem("mask_ready"), sem("ranks_in_psum"), sem("routes_ready"), sem("rows_scattered")
        cp_w = sem("ffn_weights_copied")
        zf = sem("zeros_stored")
        ZF = MT * TT // (128 * 8)
        zt_free, mk_rdy, mk_ps = sem("z_buffer_free"), sem("masks_ready"), sem("mask_transposes_in_psum")

        def pj(o, n=1):
            return slice(o, o + n * DS)

        pblk = ctx.enter_context(ExitStack())
        block = pblk.enter_context(nc.Block())

        @block.sync
        def _(sp):
            sp.dma_start(x_tok[:, :, :], x_tok_d).then_inc(ld_x, 16)
            col = lambda a: a.rearrange("(p o) -> p o", o=1)
            for dst, src in ((wcat, A["wcatT"]), (wvT, A["wvT"]), (ir1T, A["ir1T"]), (wroT, A["wroT"])):
                sp.dma_start(dst[:, :, :], src.rearrange("(k p) n -> p k n", p=128)).then_inc(ld_w, 16)
            for dst, src in ((ir2T, A["ir2T"]), (nm1T, A["nm1T"]), (nm2T, A["nm2T"]), (woT, A["woT"]),
                             (b_ir1, col(A["ir_b1"])), (b_nm1, col(A["nm_b1"])), (b_nm2, col(A["nm_b2"])),
                             (normw, col(A["norm_w"]))):
                sp.dma_start(dst[:, :], src).then_inc(ld_w, 16)
            for n, a in enumerate((A["fast_alpha"], A["slow_alpha"], A["ir_b2"])):
                sp.dma_start(scal[:, n:n + 1], a.rearrange("(o n) -> o n", o=1).broadcast_to([128, 1])).then_inc(ld_s, 16)
            for n in raw:
                sp.dma_start(raw[n], A["ffn_" + n]).then_inc(cp_w, 16)
            sp.wait_ge(consts, 2)
            for d_ in (z1_d, ym_d):
                v = d_.rearrange("(a p r) d -> a p (r d)", p=128, r=8)
                for a in range(ZF):
                    sp.dma_start(v[a], zero[:, :]).then_inc(zf, 16)
        RSTD, RK, RQ, US, P0, P1, P2, UN, QKD, RO, IMP, T0, T1, T2, T3, RST1 = range(16)

        @block.gpsimd
        def _(pool):
            go = Steps(pool, p_st)
            go(nc.gpsimd.memset(ident[:, :], 0.0))
            nc.gpsimd.memset(one_m[:, :], 1.0)
            go(nc.gpsimd.memset(tri[:, :], 1.0))
            go(nc.gpsimd.affine_select(out=ident[:, :], in_=ident[:, :], compare_op=ALU.not_equal, fill=1.0,
                                       base=0, pattern=[[-1, 128]], channel_multiplier=1))
            go(nc.gpsimd.affine_select(out=tri[:, :], in_=tri[:, :], compare_op=ALU.is_gt, fill=0.0,
                                       base=0, pattern=[[1, 128]], channel_multiplier=-1))
            go(nc.gpsimd.iota(idx8[:, :, :].bitcast(i32), pattern=[[0, NC], [1, NE]], base=0, channel_multiplier=0))
            go(nc.gpsimd.tensor_copy(iota8[:, :, :], idx8[:, :, :].bitcast(i32)))
            nc.gpsimd.memset(sc8[:, :], 0.0).then_inc(consts, 1)
            nc.gpsimd.memset(zero[:, :], 0.0).then_inc(consts, 1)
            pool.wait_ge(route_rdy, 1)
            pool.wait_ge(zf, 16 * 2 * ZF)
            n = 0
            for c in range(NC):
                for s_ in (slot1, slot2):
                    pool.indirect_dma_start(z1_d, bass.IndirectOffsetOnAxis(s_[:, c:c + 1].bitcast(u32), 0),
                                            WP[:, c, :], None).then_inc(scat, 16)
                    n += 1
            pool.wait_ge(scat, 16 * n)
        @block.vector
        def _(dve):
            V = nc.vector
            go = Steps(dve, d_st)
            def row(t, c):
                return t[:, ds(c, 1), :].rearrange("p o d -> p (o d)")

            def ln_stats():
                with dve.Fori(0, NC) as c:
                    V.bn_stats(row(st, c), row(x_tok, c)).then_inc(d_st, 1)
                go.done += NC
                dve.wait_ge(d_st, go.done)
                for c in range(NC):
                    last = V.bn_aggr(mv[:, c, :], st[:, c, :])
                go(last)
                V.tensor_scalar(small[:, T0, :], mv[:, :, 1], 1e-5, None, ALU.add).then_inc(sq_rdy, 1)

            dve.sem_inc(nu_out, 2)
            dve.sem_inc(pj_out, 2)
            dve.wait_ge(ld_x, 16)
            ln_stats()
            dve.wait_ge(ld_s, 48)
            dve.wait_ge(consts, 2)
            for m in range(2):
                al = scal[:, m:m + 1]
                go(V.tensor_scalar(beta[:, m:m + 1], al, -1.0, 1.0, ALU.mult, ALU.add))
                V.memset(pw_s[:, m, 0:1], 0.0)
                go(V.tensor_tensor_scan(pw_s[:, m, 1:129], al.broadcast_to([128, 128]), ident[:, :], 0.0,
                                        ALU.mult, ALU.add))
                V.tensor_copy(maskQ[:, m, :], pw_s[:, m, 0:128])
                V.tensor_copy(rev[:, m:m + 1], pw_s[:, m, 128:129])
                V.tensor_scalar(maskL[:, m, 1, :], pw_s[:, m, 0:128], beta[:, m:m + 1], None,
                                ALU.mult).then_inc(mk_rdy, 1)
            dve.wait_ge(mk_ps, 1)
            for m in range(2):
                V.tensor_copy(maskL[:, m, 0, :], B[0][:, m * 128:(m + 1) * 128])
                go(V.tensor_copy(lam[:, m:m + 1], B[1][:, m:m + 1]))
                V.tensor_scalar(alC[:, m:m + 1], B[1][:, 2 + m:3 + m], scal[:, m:m + 1], None, ALU.mult)
                go(V.tensor_tensor(blam[:, m:m + 1], beta[:, m:m + 1], lam[:, m:m + 1], ALU.mult))
            dve.wait_ge(ld_w, 16 * 12)
            go(V.tensor_scalar(woN[:, :], woT[:, :], normw[:, :], None, ALU.mult))
            dve.wait_ge(sq_done, 1)
            go(V.reciprocal(small[:, RSTD, :], small[:, T0, :]))
            with dve.Fori(0, NB) as b:
                for j in range(CPB):
                    c = b * CPB + j
                    dve.wait_ge(zt_free, c + 1)
                    V.tensor_scalar(zt[:, j % 2, :], row(x_tok, c), row(mv, c)[:, 0:1],
                                    small[:, RSTD, ds(c, 1)], ALU.subtract, ALU.mult).then_inc(z_rdy, 1)
                dve.wait_ge(ti_ps, b + 1)
                V.tensor_copy(vT[:, :], B[4][0:DS, :]).then_inc(vT_rdy, 1)
                for h in range(2):
                    dve.wait_ge(pj_ps, 2 * b + (h + 1))
                    V.tensor_copy(PR[:, ds(b * CPB + 2 * h, 2), 0:PJ],
                                  B[2 + h][:, 0:400].rearrange("p (j n) -> p j n", j=2)[:, :, 0:PJ]).then_inc(pj_out, 1)
                dve.wait_ge(nu_ps, b + 1)
                V.tensor_scalar(NU[:, ds(b * BT, BT)], B[4][0:DS, :], b_nm2[:, :], None, ALU.add).then_inc(nu_out, 1)
                V.tensor_copy(small[:, IMP, ds(b * CPB, CPB)], B[5][:, 0:CPB]).then_inc(nu_out, 1)
            dve.wait_ge(pj_out, 2 * NB + 2)
            dve.wait_ge(nu_out, 2 * NB + 2)
            go(V.tensor_scalar(small[:, US, :], small[:, IMP, :], scal[:, 2:3], 0.0, ALU.add, ALU.is_gt))
            for dst, o in ((RK, 0), (RQ, 2 * DS)):
                go(V.tensor_tensor(big[:, :, :], PR[:, :, pj(o)], PR[:, :, pj(o)], ALU.mult))
                go(V.tensor_reduce(small[:, dst, :], big[:, :, :], AX.X, ALU.add))
            go(V.tensor_tensor(small[:, T2, :], PR[:, :, PJ - 3], PR[:, :, PJ - 2], ALU.max))
            go(V.tensor_tensor(small[:, T2, :], small[:, T2, :], PR[:, :, PJ - 1], ALU.max))
            for n in range(3):
                last = V.tensor_tensor(small[:, P0 + n, :], PR[:, :, PJ - 3 + n], small[:, T2, :], ALU.subtract)
            last.then_inc(sq_rdy, 1)
            dve.wait_ge(sq_done, 2)
            go(V.tensor_tensor(small[:, T2, :], small[:, P0, :], small[:, P1, :], ALU.add))
            go(V.tensor_tensor(small[:, T2, :], small[:, T2, :], small[:, P2, :], ALU.add))
            go(V.reciprocal(small[:, T3, :], small[:, T2, :]))
            for n in range(3):
                V.tensor_tensor(small[:, P0 + n, :], small[:, P0 + n, :], small[:, T3, :], ALU.mult)
            for dst, o in ((RK, 0), (RQ, 2 * DS)):
                go(V.tensor_scalar(small[:, dst, :], small[:, dst, :], 1e-12, None, ALU.max))
                go(V.reciprocal(small[:, dst, :], small[:, dst, :]))
                go(V.tensor_tensor(PR[:, :, pj(o)], PR[:, :, pj(o)],
                                   small[:, dst, :].rearrange("p (c o) -> p c o", o=1).broadcast_to([128, NC, DS]), ALU.mult))
            go(V.tensor_tensor(big[:, :, :], PR[:, :, pj(0)], PR[:, :, pj(2 * DS)], ALU.mult))
            go(V.tensor_reduce(small[:, QKD, :], big[:, :, :], AX.X, ALU.add))
            V.memset(nsT[:, :, :], 0.0)
            go(V.memset(state[:, :, :], 0.0))
            dve.sem_inc(f_rdy, 1)

            with dve.Fori(0, NC // 2) as t:
                go.turn(t, 2)
                for j in range(2):
                    c = t * 2 + j
                    pr = row(PR, c)
                    u = small[:, US, ds(c, 1)]
                    k_, v_, q_ = pr[:, pj(0)], pr[:, pj(DS)], pr[:, pj(2 * DS)]
                    V.tensor_copy(KQ[:, j, 0, :], k_)
                    go(V.tensor_scalar(KQ[:, j, 1, :], k_, u, None, ALU.mult))
                    for m in range(2):
                        V.tensor_scalar(KQ[:, j, 3 + m, :], q_, lam[:, m:m + 1], None, ALU.mult)
                        V.tensor_scalar(KR[:, j, m, :], KQ[:, j, m, :], rev[:, m:m + 1], None, ALU.mult)
                        V.tensor_scalar(X[:, j, m, DS:2 * DS], KQ[:, j, m, :], blam[:, m:m + 1], None, ALU.mult)
                    V.tensor_scalar(X[:, j, 0, 0:DS], v_, beta[:, 0:1], None, ALU.mult)
                    V.tensor_scalar(X[:, j, 1, 0:DS], v_, beta[:, 1:2], u, ALU.mult, ALU.mult)
                    V.tensor_copy(KQ[:, j, 2, :], q_).then_inc(kq_rdy, 1)
                for j in range(2):
                    dve.wait_ge(g_ps, t * 2 + (j + 1))
                    for m in range(2):
                        gm = B[4 + j][:, m * 128:(m + 1) * 128].rearrange("p (o n) -> p o n", o=1)
                        V.tensor_tensor(L[:, j, 0, 2 * m:2 * m + 2, :], gm.broadcast_to([128, 2, 128]),
                                        maskL[:, m, :, :], ALU.mult)
                    qk = B[4 + j][:, 256:384].rearrange("p (o n) -> p o n", o=1)
                    V.tensor_tensor(QM[:, j, :, :], qk.broadcast_to([128, 2, 128]), maskQ[:, :, :],
                                    ALU.mult).then_inc(l_rdy, 1)
                for n in range(LEVELS):
                    for j in range(2):
                        dve.wait_ge(ap_ps, t * (2 * LEVELS) + (2 * n + j + 1))
                        V.tensor_tensor(X[:, j, :, :], X[:, j, :, :],
                                        B[2 + j][:, 0:256].rearrange("p (m n) -> p m n", m=2),
                                        ALU.subtract if n == 0 else ALU.add).then_inc(ap_rdy, 1)
                dve.wait_ge(ap_rdy, (t + 1) * (2 * LEVELS))
                for j in range(2):
                    c = t * 2 + j
                    dve.wait_ge(w_ps, c + 1)
                    V.tensor_tensor(row(WP, c)[:, 0:128].rearrange("p (m n) -> p m n", m=2), X[:, j, :, 0:DS],
                                    B[6][:, 0:128].rearrange("p (m n) -> p m n", m=2), ALU.subtract).then_inc(w_rdy, 1)
                    dve.wait_ge(pp_ps, c + 1)
                    V.tensor_copy(row(WP, c)[:, 128:256], B[7][:, 0:128])
                    for m in range(2):
                        last = V.scalar_tensor_tensor(state[:, m, :], state[:, m, :], alC[0:DS, m:m + 1],
                                                      B[6][0:DS, 256 + m * DS:256 + (m + 1) * DS], ALU.mult, ALU.add)
                    last.then_inc(f_rdy, 1)
                    dve.wait_ge(f_rdy, c + 2)
                go.end(NC // 2)

            dve.wait_ge(w_rdy, NC)
            go(V.tensor_tensor(big[:, :, :], WP[:, :, 128:128 + DS], WP[:, :, 128 + DS:256], ALU.add))
            go(V.scalar_tensor_tensor(big[:, :, :], big[:, :, :], -0.5, PR[:, :, pj(DS)], ALU.mult, ALU.add))
            go(V.tensor_tensor(big[:, :, :], big[:, :, :], big[:, :, :], ALU.mult))
            go(V.tensor_reduce(small[:, UN, :], big[:, :, :], AX.X, ALU.add))
            go(V.tensor_scalar(small[:, UN, :], small[:, UN, :], 1.0 / (1.0 + 1e-6), LOGIT, ALU.mult, ALU.is_gt))
            go(V.tensor_scalar(small[:, UN, :], small[:, UN, :], 0.1, None, ALU.mult))
            for m in range(2):
                V.tensor_scalar(small[:, T0 + 2 * m, :], small[:, P0 + m, :], scal[:, m:m + 1], None, ALU.mult)
                last = V.tensor_tensor(small[:, T1 + 2 * m, :], small[:, P0 + m, :], small[:, QKD, :], ALU.mult)
            go(last)
            with dve.Fori(0, NC // 2) as t:
                go.turn(t, 14)
                for j in range(2):
                    c = t * 2 + j
                    V.tensor_copy(ubc[:, j, :], small[:, UN, ds(c, 1)].broadcast_to([128, DS])).then_inc(ub_rdy, 1)
                for j in range(2):
                    c = t * 2 + j
                    dve.wait_ge(ub_ps, c + 1)
                    V.tensor_scalar(aN[:, j, :], B[j][0:DS, 0:128], -1.0, 1.0, ALU.mult, ALU.add)
                    go(V.tensor_tensor(bN[:, j, :], B[j][0:DS, 0:128], NU[:, ds(c * CH, CH)], ALU.mult))
                    V.tensor_tensor_scan(nsT[:, j, :], aN[:, j, :], bN[:, j, :], nsT[:, 1 - j, 127:128],
                                         ALU.mult, ALU.add).then_inc(ns_rdy, 1)
                    dve.wait_ge(ns_rdy, c + 1)
                for j in range(2):
                    c = t * 2 + j
                    wp = row(WP, c)
                    dve.wait_ge(nst_ps, c + 1)
                    go(V.tensor_scalar(ot[:, j, :], B[j][:, 128:128 + DS], small[:, P2, ds(c, 1)], None, ALU.mult))
                    for s_, o in ((T0, 128), (T1, 0), (T2, 128 + DS), (T3, DS)):
                        go(V.scalar_tensor_tensor(ot[:, j, :], wp[:, o:o + DS], small[:, s_, ds(c, 1)], ot[:, j, :],
                                                  ALU.mult, ALU.add))
                    go(V.tensor_tensor(ts[:, j, :], ot[:, j, :], ot[:, j, :], ALU.mult))
                    V.tensor_reduce(small[:, RO, ds(c, 1)], ts[:, j, :], AX.X, ALU.add).then_inc(o_rdy, 1)
                go.end(NC // 2)
            dve.wait_ge(wo_out, NC + 2)
            dve.wait_ge(o_rdy, NC)
            V.tensor_scalar(small[:, RO, :], small[:, RO, :], 1.0 / DS, 1e-6, ALU.mult, ALU.add).then_inc(sq_rdy, 1)
            dve.wait_ge(sq_done, 3)
            go(V.reciprocal(small[:, RO, :], small[:, RO, :]))
            with dve.Fori(0, NC) as c:
                V.scalar_tensor_tensor(row(x_tok, c), row(WP, c), small[:, RO, ds(c, 1)], row(x_tok, c),
                                       ALU.mult, ALU.add).then_inc(d_st, 1)
            go.done += NC
            dve.wait_ge(d_st, go.done)
            ln_stats()
            dve.wait_ge(sq_done, 4)
            go(V.reciprocal(small[:, RST1, :], small[:, T0, :]))
            with dve.Fori(0, NC // 2) as t:
                for j in range(2):
                    c = t * 2 + j
                    V.tensor_scalar(zt[:, j, :], row(x_tok, c), row(mv, c)[:, 0:1],
                                    small[:, RST1, ds(c, 1)], ALU.subtract, ALU.mult).then_inc(z1_rdy, 1)
                for j in range(2):
                    c = t * 2 + j
                    dve.wait_ge(lg_ps, c + 1)
                    V.tensor_copy(row(LG, c), B[2 + j][:, 0:NE]).then_inc(lg_out, 1)
            dve.wait_ge(lg_out, NC)
            bc = lambda a: a.rearrange("p (c o) -> p c o", o=1).broadcast_to([128, NC, NE])
            for n, (src, m_, oh) in enumerate(((LG[:, :, :], T1, 0), (rt[:, 2, :, :], T2, 1))):
                go(V.tensor_reduce(small[:, m_, :], src, AX.X, ALU.max))
                go(V.tensor_tensor(rt[:, 3, :, :], src, bc(small[:, m_, :]), ALU.is_equal))
                go(V.scalar_tensor_tensor(rt[:, 3, :, :], rt[:, 3, :, :], -64.0, iota8[:, :, :], ALU.mult, ALU.add))
                go(V.tensor_reduce(small[:, T3, :], rt[:, 3, :, :], AX.X, ALU.min))
                go(V.tensor_tensor(rt[:, oh, :, :], rt[:, 3, :, :], bc(small[:, T3, :]), ALU.is_equal))
                if n == 0:
                    go(V.scalar_tensor_tensor(rt[:, 2, :, :], rt[:, 0, :, :], -3e38, LG[:, :, :], ALU.mult, ALU.add))
            V.tensor_tensor(rt[:, 3, :, :], rt[:, 0, :, :], rt[:, 1, :, :], ALU.add).then_inc(rk_rdy, 1)
            go(V.tensor_tensor(small[:, T2, :], small[:, T2, :], small[:, T1, :], ALU.subtract))
            V.tensor_tensor(LG[:, :, :], LG[:, :, :], bc(small[:, T1, :]), ALU.subtract).then_inc(sq_rdy, 1)
            dve.wait_ge(sq_done, 5)
            go(V.tensor_reduce(small[:, T3, :], LG[:, :, :], AX.X, ALU.add))
            go(V.reciprocal(gate1[:, :], small[:, T3, :]))
            go(V.tensor_tensor(gate2[:, :], gate1[:, :], small[:, T2, :], ALU.mult))
            dve.wait_ge(rk_ps, 1)
            go(V.tensor_copy(rt[:, 4, :, :], B[1][:, 0:NC * NE].rearrange("p (c e) -> p c e", e=NE)))
            for e in range(NE):
                last = V.tensor_tensor_scan(rt[:, 2, :, e], one_m[:, 0:NC], rt[:, 4, :, e], 0.0, ALU.mult, ALU.add)
            go(last)
            go(V.tensor_copy(cnt8[:, 0, :], rt[:, 2, NC - 1, :]))
            go(V.tensor_scalar(cnt8[:, 3, :], cnt8[:, 0, :], 0.0, None, ALU.is_gt))
            for j in range(1, S // TT):
                go(V.scalar_tensor_tensor(cnt8[:, 3, :], cnt8[:, 0, :], float(TT * j), cnt8[:, 3, :], ALU.is_gt, ALU.add))
            go(V.tensor_scalar(cnt8[:, 3, :], cnt8[:, 3, :], 1.0, None, ALU.max))
            go(V.tensor_tensor_scan(cnt8[:, 2, :], one_m[:, 0:NE], cnt8[:, 3, :], 0.0, ALU.mult, ALU.add))
            go(V.tensor_tensor(base8[:, :], cnt8[:, 2, :], cnt8[:, 3, :], ALU.subtract))
            go(V.tensor_scalar(base8[:, :], base8[:, :], float(TT), None, ALU.mult))
            go(V.tensor_tensor(rt[:, 4, :, :], rt[:, 2, :, :], rt[:, 4, :, :], ALU.subtract))
            go(V.tensor_tensor(rt[:, 4, :, :], rt[:, 4, :, :], B[0][:, 0:NC * NE].rearrange("p (c e) -> p c e", e=NE), ALU.add))
            go(V.tensor_tensor(rt[:, 4, :, :], rt[:, 4, :, :],
                               base8[:, :].rearrange("p (o e) -> p o e", o=1).broadcast_to([128, NC, NE]), ALU.add))
            for oh, dst in ((0, slot1), (1, slot2)):
                go(V.tensor_tensor(rt[:, 5, :, :], rt[:, 4, :, :], rt[:, oh, :, :], ALU.mult))
                go(V.tensor_reduce(small[:, T3, :], rt[:, 5, :, :], AX.X, ALU.add))
                go(V.tensor_copy(dst[:, :], small[:, T3, :]))
            V.memset(tiles0[:, 0:1], 0)
            V.tensor_copy(tiles0[0:1, 1:NE + 1], cnt8[0:1, 2, :])
            V.tensor_copy(tiles[0:1, :], cnt8[0:1, 3, :]).then_inc(route_rdy, 1)

        @block.scalar
        def _(act):
            A_ = nc.scalar
            act.sem_inc(wo_out, 2)
            act.wait_ge(sq_rdy, 1)
            A_.activation(small[:, T0, :], small[:, T0, :], ACT.Sqrt).then_inc(sq_done, 1)
            act.wait_ge(ld_w, 16 * 12)
            with act.Fori(0, NB) as b:
                act.wait_ge(zt_free, b * CPB + (CPB + 2))
                for k in range(KT):
                    A_.activation(zT[:, k, :], B[k][:, :], ACT.Copy).then_inc(zT_rdy, 1)
                act.wait_ge(ti_ps, b + 1)
                A_.activation(gT[:, :], B[5][0:DS, :], ACT.Gelu, bias=b_ir1[:, :]).then_inc(gT_rdy, 1)
                act.wait_ge(hd_ps, b + 1)
                A_.activation(hT[:, :], B[6][:, :], ACT.Gelu, bias=b_nm1[:, :]).then_inc(hd_rdy, 1)
            act.wait_ge(sq_rdy, 2)
            A_.activation(small[:, RK, :], small[:, RK, :], ACT.Sqrt)
            A_.activation(small[:, RQ, :], small[:, RQ, :], ACT.Sqrt)
            A_.activation(small[:, P0:P0 + 3, :], small[:, P0:P0 + 3, :], ACT.Exp).then_inc(sq_done, 1)
            with act.Fori(0, NC // 2) as t:
                for j in range(2):
                    act.wait_ge(kqt_ps, t * 2 + (j + 1))
                    A_.activation(KQT[:, j, 0:4, :], B[4 + j][0:DS, :].rearrange("p (a n) -> p a n", a=4), ACT.Copy)
                    A_.activation(KQT[:, j, 4, :], B[2 + j][0:DS, 256:384], ACT.Copy).then_inc(kqt_rdy, 1)
                for n in range(LEVELS - 1):
                    for j in range(2):
                        act.wait_ge(sq_ps, t * (2 * LEVELS - 2) + (2 * n + j + 1))
                        A_.activation(L[:, j, (n + 1) % 2, :, :], B[j][:, :].rearrange("p (a n) -> p a n", a=4),
                                      ACT.Copy).then_inc(sq_cp, 1)
                for j in range(2):
                    act.wait_ge(yt_ps, t * 2 + (j + 1))
                    A_.activation(YT[:, j, :, :], B[2 + j][0:DS, 0:256].rearrange("p (m n) -> p m n", m=2),
                                  ACT.Copy).then_inc(yt_rdy, 1)
            with act.Fori(0, NC // 2) as t:
                for j in range(2):
                    act.wait_ge(ot_ps, t * 2 + (j + 1))
                    A_.activation(oT[:, j, :], B[2 + j][0:DS, 0:128], ACT.Copy).then_inc(oT_rdy, 1)
                for j in range(2):
                    act.wait_ge(wo_ps, t * 2 + (j + 1))
                    A_.activation(WP[:, ds(t * 2 + j, 1), :].rearrange("p o d -> p (o d)"), B[4 + j][:, 0:D],
                                  ACT.Copy).then_inc(wo_out, 1)
            for n in (3, 4):
                act.wait_ge(sq_rdy, n)
                s_ = RO if n == 3 else T0
                A_.activation(small[:, s_, :], small[:, s_, :], ACT.Sqrt).then_inc(sq_done, 1)
            with act.Fori(0, NC // 2) as t:
                for j in range(2):
                    act.wait_ge(z1_rdy, t * 2 + (j + 1))
                    A_.activation(WP[:, ds(t * 2 + j, 1), :].rearrange("p o d -> p (o d)"), zt[:, j, :], ACT.Copy)
                    act.wait_ge(z1_ps, t * 2 + (j + 1))
                    A_.activation(z1T[:, j, :, :], B[j][:, 0:256].rearrange("p (k n) -> p k n", k=2),
                                  ACT.Copy).then_inc(z1T_rdy, 1)
            act.wait_ge(sq_rdy, 5)
            A_.activation(small[:, T2, :], small[:, T2, :], ACT.Exp)
            A_.activation(LG[:, :, :], LG[:, :, :], ACT.Exp).then_inc(sq_done, 1)

        @block.tensor
        def _(pe):
            T = nc.tensor
            I_ = ident[:, :]
            pe.sem_inc(zt_free, 2)
            pe.wait_ge(mk_rdy, 2)
            for m in range(2):
                T.transpose(B[0][:, m * 128:(m + 1) * 128], maskL[:, m, 1, :], I_)
                T.matmul(B[1][:, m:m + 1], pw_s[0:1, m, 1:129], one_m[0:1, 0:1], start=True, stop=True)
                last = T.matmul(B[1][:, 2 + m:3 + m], one_m[0:1, :], pw_s[0:1, m, 128:129], start=True, stop=True)
            last.then_inc(mk_ps, 1)
            pe.wait_ge(ld_w, 16 * 12)
            with pe.Fori(0, NB) as b:
                for j in range(CPB):
                    pe.wait_ge(z_rdy, b * CPB + (j + 1))
                    for k in range(KT):
                        last = T.transpose(B[k][:, j * CH:(j + 1) * CH], zt[:, j % 2, k * 128:(k + 1) * 128], I_)
                    last.then_inc(zt_free, 1)
                pe.wait_ge(zT_rdy, b * 2 + 2)
                pe.wait_ge(nu_out, b * 2 + 2)
                for w, o in ((wvT, 4), (ir1T, 5)):
                    for k in range(KT):
                        last = T.matmul(B[o][0:DS, :], w[:, k, :], zT[:, k, :], start=(k == 0), stop=(k == KT - 1))
                last.then_inc(ti_ps, 1)
                for h in range(2):
                    pe.wait_ge(pj_out, b * 2 + (h + 1))
                    for jj in range(2):
                        j = 2 * h + jj
                        for k in range(KT):
                            last = T.matmul(B[2 + h][:, jj * 200:jj * 200 + PJ], zT[:, k, j * CH:(j + 1) * CH],
                                            wcat[:, k, :], start=(k == 0), stop=(k == KT - 1))
                    last.then_inc(pj_ps, 1)
                pe.wait_ge(vT_rdy, b + 1)
                T.matmul(B[6][:, :], nm1T[:, :], vT[:, :], start=True, stop=True).then_inc(hd_ps, 1)
                pe.wait_ge(gT_rdy, b + 1)
                for j in range(CPB):
                    T.matmul(B[5][:, j:j + 1], gT[:, j * CH:(j + 1) * CH], ir2T[:, :], start=True, stop=True)
                pe.wait_ge(hd_rdy, b + 1)
                T.matmul(B[4][0:DS, :], nm2T[:, :], hT[:, :], start=True, stop=True).then_inc(nu_ps, 1)
            with pe.Fori(0, NC // 2) as t:
                for j in range(2):
                    pe.wait_ge(kq_rdy, t * 2 + (j + 1))
                    T.matmul(B[4 + j][0:DS, 0:128], KQ[:, j, 0, :], I_, start=True, stop=True)
                    for a in range(1, 4):
                        T.transpose(B[4 + j][0:DS, a * 128:(a + 1) * 128], KQ[:, j, a, :], I_)
                    T.transpose(B[2 + j][0:DS, 256:384], KQ[:, j, 4, :], I_).then_inc(kqt_ps, 1)
                for j in range(2):
                    pe.wait_ge(kqt_rdy, t * 2 + (j + 1))
                    for n, (a, b_) in enumerate(((0, 0), (1, 1), (0, 2))):
                        last = T.matmul(B[4 + j][:, n * 128:(n + 1) * 128], KQT[:, j, a, :], KQT[:, j, b_, :],
                                        start=True, stop=True)
                    last.then_inc(g_ps, 1)
                for n in range(LEVELS):
                    for j in range(2):
                        if n == 0:
                            pe.wait_ge(l_rdy, t * 2 + (j + 1))
                        else:
                            pe.wait_ge(sq_cp, t * (2 * LEVELS - 2) + (2 * (n - 1) + j + 1))
                        Ln = L[:, j, n % 2, :, :]
                        if n < LEVELS - 1:
                            for m in range(2):
                                a, b_ = Ln[:, 2 * m, :], Ln[:, 2 * m + 1, :]
                                T.matmul(B[j][:, 256 * m:256 * m + 128], b_, a, start=True, stop=True)
                                last = T.matmul(B[j][:, 256 * m + 128:256 * m + 256], a, b_, start=True, stop=True)
                            last.then_inc(sq_ps, 1)
                        if n > 0:
                            pe.wait_ge(ap_rdy, t * (2 * LEVELS) + (2 * (n - 1) + j + 1))
                        for m in range(2):
                            last = T.matmul(B[2 + j][:, m * 128:(m + 1) * 128], Ln[:, 2 * m + 1, :], X[:, j, m, :],
                                            start=True, stop=True)
                        last.then_inc(ap_ps, 1)
                for j in range(2):
                    pe.wait_ge(ap_rdy, t * (2 * LEVELS) + (2 * LEVELS - 1 + j))
                    for m in range(2):
                        last = T.matmul(B[2 + j][0:DS, m * 128:(m + 1) * 128], X[:, j, m, DS:2 * DS], I_,
                                        start=True, stop=True)
                    last.then_inc(yt_ps, 1)
                for j in range(2):
                    c = t * 2 + j
                    pe.wait_ge(yt_rdy, c + 1)
                    pe.wait_ge(f_rdy, c + 1)
                    for m in range(2):
                        last = T.matmul(B[6][:, m * DS:(m + 1) * DS], YT[:, j, m, :], state[:, m, :], start=True, stop=True)
                    last.then_inc(w_ps, 1)
                    for m in range(2):
                        T.matmul(B[7][:, m * DS:(m + 1) * DS], KQT[:, j, 3 + m, :], state[:, m, :],
                                 start=True, stop=False)
                        if m == 0:
                            pe.wait_ge(w_rdy, c + 1)
                        w = WP[:, ds(c, 1), m * DS:(m + 1) * DS].rearrange("p o d -> p (o d)")
                        T.matmul(B[7][:, m * DS:(m + 1) * DS], QM[:, j, m, :], w, start=False, stop=True)
                        last = T.matmul(B[6][0:DS, 256 + m * DS:256 + (m + 1) * DS], KR[:, j, m, :], w,
                                        start=True, stop=True)
                    last.then_inc(pp_ps, 1)
            with pe.Fori(0, NC // 2) as t:
                for j in range(2):
                    pe.wait_ge(ub_rdy, t * 2 + (j + 1))
                    T.matmul(B[j][0:DS, 0:128], ubc[:, j, :], I_, start=True, stop=True).then_inc(ub_ps, 1)
                for j in range(2):
                    pe.wait_ge(ns_rdy, t * 2 + (j + 1))
                    T.matmul(B[j][:, 128:128 + DS], nsT[:, j, :], ident[0:DS, 0:DS],
                             start=True, stop=True).then_inc(nst_ps, 1)
                for j in range(2):
                    pe.wait_ge(o_rdy, t * 2 + (j + 1))
                    T.matmul(B[2 + j][0:DS, 0:128], ot[:, j, :], I_, start=True, stop=True).then_inc(ot_ps, 1)
                for j in range(2):
                    pe.wait_ge(oT_rdy, t * 2 + (j + 1))
                    pe.wait_ge(wo_out, t * 2 + (j + 1))
                    T.matmul(B[4 + j][:, 0:D], oT[:, j, :], woN[:, :], start=True, stop=True).then_inc(wo_ps, 1)
            with pe.Fori(0, NC // 2) as t:
                for j in range(2):
                    pe.wait_ge(z1_rdy, t * 2 + (j + 1))
                    for k in range(KT):
                        last = T.transpose(B[j][:, k * 128:(k + 1) * 128], zt[:, j, k * 128:(k + 1) * 128], I_)
                    last.then_inc(z1_ps, 1)
                for j in range(2):
                    pe.wait_ge(z1T_rdy, t * 2 + (j + 1))
                    for k in range(KT):
                        last = T.matmul(B[2 + j][:, 0:NE], z1T[:, j, k, :], wroT[:, k, :], start=(k == 0), stop=(k == KT - 1))
                    last.then_inc(lg_ps, 1)
            pe.wait_ge(rk_rdy, 1)
            T.matmul(B[0][:, 0:NC * NE], tri[:, :], rt[:, 3, :, :].rearrange("p c e -> p (c e)"), start=True, stop=True)
            T.matmul(B[1][:, 0:NC * NE], one_m[:, :], rt[:, 3, :, :].rearrange("p c e -> p (c e)"),
                     start=True, stop=True).then_inc(rk_ps, 1)

        pblk.close()
        pa.close()
        pb = ctx.enter_context(ExitStack())
        KH = HID // 128
        w1_d = A["w1"].rearrange("e (k p) n -> e p k n", p=128)
        w2_d = A["w2"].rearrange("e (k p) n -> e p k n", p=128)
        st1 = sb("st1", [128, KT, HID], to=pb)
        st2 = sb("st2", [128, KH, D], to=pb)
        w1s = [[sb(f"w1_{q}{h}", [128, KT, HID], f32r, to=pb) for h in "hl"] for q in range(2)]
        w2s = [[sb(f"w2_{q}{h}", [128, KH, D], f32r, to=pb) for h in "hl"] for q in range(2)]
        b1s = sb("b1s", [128, NE * KH], to=pb)
        b2s = sb("b2s", [128, NE, D], to=pb)
        xg = sb("xg", [128, 2, D], to=pb)
        xT = [sb(f"xT{h}", [128, KT, TT], f32r, to=pb) for h in "hl"]
        h32 = sb("h32", [128, KH, TT], to=pb)
        hs = [sb(f"hs{h}", [128, KH, TT], f32r, to=pb) for h in "hl"]
        yt = sb("yt", [128, 2, D], to=pb)
        NG = 4
        g1 = sb("g1", [128, NG, D], to=pb)
        g2 = sb("g2", [128, NG, D], to=pb)

        ew_ld, ew_free, ew_rdy, ex_done = (sem("expert_weights_loaded"), sem("expert_stage_free"),
                                           sem("expert_weights_split"), sem("expert_done"))
        eb_ld, xg_ld, xg_free, xt_ps, xT_rdy = (sem("expert_biases_loaded"), sem("rows_loaded"), sem("rows_free"),
                                                sem("rows_T_in_psum"), sem("rows_T_split"))
        up_ps, h_act, h_rdy, dn_ps, y_rdy, y_out = (sem("up_in_psum"), sem("gelu_done"), sem("h_split"),
                                                    sem("down_in_psum"), sem("y_ready"), sem("y_stored"))
        moe_done, x2_rdy = sem("experts_done"), sem("x2_ready")
        g_ld = [sem(f"gathered_{i}") for i in range(NG)]
        g_free = sem("gather_free")
        p_st2, x_st, h_st, c_st = sem("weights_hi_done"), sem("rows_hi_done"), sem("h_hi_done"), sem("first_copy_added")

        def f32(ap):
            return ap.bitcast(fp32)

        def mm3(out, a, b, first, last):
            nc.tensor.matmul(out, a[0], b[0], start=first, stop=False)
            nc.tensor.matmul(out, a[0], b[1], start=False, stop=False)
            return nc.tensor.matmul(out, a[1], b[0], start=False, stop=last)

        def expert_tiles(eng, before, body, after):
            with eng.Fori(0, NE // 2) as p:
                for q in range(2):
                    e = p * 2 + q
                    t0 = eng.value_load(tiles0[0:1, ds(e, 1)], min_val=0, max_val=MT)
                    t1 = eng.value_load(tiles0[0:1, ds(e + 1, 1)], min_val=1, max_val=MT)
                    before(e, q)
                    with eng.Fori(t0, t1) as t:
                        body(e, q, t)
                    after(e, q)

        nop = lambda *a: None
        pblk = ctx.enter_context(ExitStack())
        block = pblk.enter_context(nc.Block())

        @block.sync
        def _(sp):
            sp.dma_start(b1s[:, :], A["b1T"]).then_inc(eb_ld, 16)
            for e in range(NE):
                sp.dma_start(b2s[:, e, :], A["b2"][e:e + 1, :].broadcast_to([128, D])).then_inc(eb_ld, 16)

            def weights(e):
                sp.wait_ge(ew_free, e + 1)
                sp.dma_start(st1[:, :, :], w1_d[ds(e, 1)].rearrange("o p k n -> p (o k) n")).then_inc(ew_ld, 16)
                sp.dma_start(st2[:, :, :], w2_d[ds(e, 1)].rearrange("o p k n -> p (o k) n")).then_inc(ew_ld, 16)

            def rows(e, q, t):
                sp.wait_ge(xg_free, t + 1)
                sp.dma_start(xg[:, :, :], z1_d[ds(t * TT, TT), :].rearrange("(j p) d -> p j d", p=128))\
                  .then_inc(xg_ld, 16)

            expert_tiles(sp, lambda e, q: weights(e), rows, nop)
            total = sp.value_load(tiles0[0:1, NE:NE + 1], min_val=NE, max_val=MT)
            sp.wait_ge(xg_free, total + 1)
            sp.dma_start(xg[:, :, :], z1_d[0:TT, :].rearrange("(j p) d -> p j d", p=128)).then_inc(xg_ld, 16)
        @block.gpsimd
        def _(pool):
            go = Steps(pool, p_st2)
            pool.sem_inc(ew_free, 1)

            def split(e, q):
                pool.wait_ge(ew_ld, e * 32 + 32)
                pool.wait_ge(ex_done, e + 1)
                for st_, w in ((st1, w1s[q]), (st2, w2s[q])):
                    nc.gpsimd.tensor_copy(w[0][:, :, :], st_[:, :, :]).then_inc(p_st2, 1)
                pool.wait_ge(p_st2, e * 2 + 2)
                nc.gpsimd.tensor_tensor(w1s[q][1][:, :, :], st1[:, :, :], f32(w1s[q][0][:, :, :]), ALU.subtract)
                nc.gpsimd.tensor_tensor(w2s[q][1][:, :, :], st2[:, :, :], f32(w2s[q][0][:, :, :]),
                                        ALU.subtract).then_inc(ew_rdy, 1)
                pool.wait_ge(ew_rdy, e + 1)
                pool.sem_inc(ew_free, 1)

            for e in range(NE):
                split(e, e % 2)
            pool.wait_ge(moe_done, 1)
            for c in range(NC):
                if c >= NG:
                    pool.wait_ge(g_free, c - NG + 1)
                for s_, g in ((slot1, g1), (slot2, g2)):
                    pool.indirect_dma_start(g[:, c % NG, :], None, ym_d,
                                            bass.IndirectOffsetOnAxis(s_[:, c:c + 1].bitcast(u32), 0)).then_inc(g_ld[c % NG], 16)

        @block.tensor
        def _(pe):
            T = nc.tensor
            pe.sem_inc(xg_free, 1)
            pe.sem_inc(ex_done, 2)

            def rows_T(n):
                pe.wait_ge(xg_ld, n * 16 + 16)
                for k in range(KT):
                    for j in range(2):
                        last = T.transpose(B[4][:, k * TT + j * 128:k * TT + (j + 1) * 128],
                                           xg[:, j, k * 128:(k + 1) * 128], ident[:, :])
                last.then_inc(xt_ps, 1)
                pe.wait_ge(xt_ps, n + 1)
                pe.sem_inc(xg_free, 1)

            def tile(e, q, t):
                pe.wait_ge(ew_rdy, e + 1)
                pe.wait_ge(xT_rdy, t + 1)
                for m in range(KH):
                    pe.wait_ge(h_act, t * KH + (m + 1))
                    for k in range(KT):
                        ms = slice(m * 128, (m + 1) * 128)
                        last = mm3(B[m % 4][:, 0:TT], [w[:, k, ms] for w in w1s[q]], [x[:, k, :] for x in xT],
                                   k == 0, k == KT - 1)
                    last.then_inc(up_ps, 1)
                rows_T(t + 1)
                pe.wait_ge(y_rdy, t * 2 + 2)
                for k in range(KH):
                    if k % 2 == 0:
                        pe.wait_ge(h_rdy, t * 4 + (k // 2 + 1 + 4))
                    for j in range(2):
                        js = slice(j * 128, (j + 1) * 128)
                        last = mm3(B[5 + j][:, 0:D], [h[:, k, js] for h in hs], [w[:, k, :] for w in w2s[q]],
                                   k == 0, k == KH - 1)
                        if k == KH - 1:
                            last.then_inc(dn_ps, 1)

            rows_T(0)
            expert_tiles(pe, nop, tile,
                         lambda e, q: pe.drain().then_inc(ex_done, 1))

        @block.scalar
        def _(act):
            act.sem_inc(h_act, 4)
            act.wait_ge(eb_ld, 16 * (NE + 1))

            def tile(e, q, t):
                for m in range(KH):
                    act.wait_ge(up_ps, t * KH + (m + 1))
                    if m % 2 == 0:
                        act.wait_ge(h_rdy, t * 4 + (m // 2 + 1))
                    nc.scalar.activation(h32[:, m, :], B[m % 4][:, 0:TT], ACT.Gelu_apprx_tanh,
                                         bias=b1s[:, ds(e * KH + m, 1)]).then_inc(h_act, 1)
                act.wait_ge(y_rdy, t * 2 + 4)
                act.dma_start(ym_d[ds(t * TT, TT), :].rearrange("(j p) d -> p j d", p=128),
                              yt[:, :, :]).then_inc(y_out, 16)

            expert_tiles(act, nop, tile, nop)
            total = act.value_load(tiles0[0:1, NE:NE + 1], min_val=NE, max_val=MT)
            act.wait_ge(y_out, total * 16 + 16)
            nc.scalar.activation(sc8[:, 0:1], ident[:, 0:1], ACT.Copy).then_inc(moe_done, 1)

        @block.vector
        def _(dve):
            V = nc.vector
            dve.sem_inc(h_rdy, 4)
            dve.sem_inc(y_rdy, 2)
            dve.sem_inc(y_out, 16)
            dve.wait_ge(eb_ld, 16 * (NE + 1))

            def rows_split(n):
                dve.wait_ge(xt_ps, n + 1)
                src = B[4][:, :].rearrange("p (k n) -> p k n", k=KT)
                V.tensor_copy(xT[0][:, :, :], src).then_inc(x_st, 1)
                dve.wait_ge(x_st, n + 1)
                V.tensor_tensor(xT[1][:, :, :], src, f32(xT[0][:, :, :]), ALU.subtract).then_inc(xT_rdy, 1)

            def tile(e, q, t):
                for m in range(0, KH, 2):
                    dve.wait_ge(h_act, t * KH + (m + 2 + 4))
                    V.tensor_copy(hs[0][:, m:m + 2, :], h32[:, m:m + 2, :]).then_inc(h_st, 1)
                    dve.wait_ge(h_st, t * 4 + (m // 2 + 1))
                    V.tensor_tensor(hs[1][:, m:m + 2, :], h32[:, m:m + 2, :], f32(hs[0][:, m:m + 2, :]),
                                    ALU.subtract).then_inc(h_rdy, 1)
                rows_split(t + 1)
                dve.wait_ge(y_out, t * 16 + 16)
                for j in range(2):
                    dve.wait_ge(dn_ps, t * 2 + (j + 1))
                    V.tensor_tensor(yt[:, j, :], B[5 + j][:, 0:D], b2s[:, ds(e, 1), :].rearrange("p o d -> p (o d)"),
                                    ALU.add).then_inc(y_rdy, 1)

            rows_split(0)
            expert_tiles(dve, nop, tile, nop)
            for c in range(NC):
                dve.wait_ge(g_ld[c % NG], 32 * (c // NG + 1))
                V.scalar_tensor_tensor(x_tok[:, c, :], g1[:, c % NG, :], gate1[:, c:c + 1], x_tok[:, c, :],
                                       ALU.mult, ALU.add).then_inc(c_st, 1)
                dve.wait_ge(c_st, c + 1)
                V.scalar_tensor_tensor(x_tok[:, c, :], g2[:, c % NG, :], gate2[:, c:c + 1], x_tok[:, c, :],
                                       ALU.mult, ALU.add).then_inc(x2_rdy, 1)
                dve.wait_ge(x2_rdy, c + 1)
                dve.sem_inc(g_free, 1)

        pblk.close()
        pb.close()
        pc = ctx.enter_context(ExitStack())
        xa_d = nc.dram_tensor("after_time_mix", (D, S), fp32, kind="Internal").ap()
        sx_d = nc.dram_tensor("residual_sum", (D, S), fp32, kind="Internal").ap()
        x3_d = nc.dram_tensor("x3_T", (D, S), fp32, kind="Internal").ap()
        byk = lambda a: a.rearrange("(k p) n -> p k n", p=128)
        st3 = sb("st3", [128, NC, 6], to=pc)
        mv3 = sb("mv3", [128, NC, 2], to=pc)
        wst = sb("wst", [128, KT, 3 * D], to=pc)
        wtm = [sb(f"wtm{h}", [128, KT, 3 * D], f32r, to=pc) for h in "hl"]
        tk = sb("tk", [128, 2, 3, D], to=pc)
        x2T = sb("x2T", [128, KT, BT], to=pc)
        Z2 = sb("Z2", [128, KT, BT + 1], to=pc)
        a3 = sb("a3", [128, KT, BT], to=pc)
        a3s = [sb(f"a3{h}", [128, KT, BT], f32r, to=pc) for h in "hl"]
        mixed = sb("mixed", [128, 3, KT, BT], to=pc)
        stt_ = sb("wkv_state", [128, 4, KT, BT + 1], to=pc)
        tmp = sb("wkv_tmp", [128, 4, KT, BT], to=pc)
        pq = sb("wkv_pq", [128, KT, BT], to=pc)

        v_ld, wt_ld, c_st1, tk_rdy, tk_free = (sem("vectors_loaded"), sem("w_tm_loaded"), sem("time_mix_steps"),
                                               sem("tokens_ready"), sem("token_buffers_free"))
        zt_rdy, a3_rdy, km_ps, ex_w, ex_d, xa_rdy, xa_out = (
            sem("block_T_ready"), sem("a3_split"), sem("kvr_in_psum"), sem("exponents_ready"), sem("exps_done"),
            sem("xa_ready"), sem("xa_stored"))
        z_cy, z_mv = sem("z_column_ready"), sem("z_column_moved")
        wts_rdy, ln_w, ln_d, z0_ps, km_out, zb_free = (sem("w_tm_split"), sem("ln_sqrt_wanted"), sem("ln_sqrt_done"),
                                                      sem("first_token_T"), sem("kvr_taken"), sem("block_T_free"))
        pblk = ctx.enter_context(ExitStack())
        block = pblk.enter_context(nc.Block())
        MX, SM, LS, AV = range(4)

        @block.sync
        def _(sp):
            for n, v in enumerate(("time_decay", "time_first", "tmk", "tmv", "tmr", "g1", "b1v", "g2", "b2v", "cmk", "cmr")):
                sp.dma_start(vec[:, n, :], A[v]).then_inc(v_ld, 16)
            sp.dma_start(wst[:, :, :], byk(A["W_tm"])).then_inc(wt_ld, 16)
            with sp.Fori(0, NB) as b:
                sp.wait_ge(xa_rdy, b + 1)
                sp.dma_start(byk(xa_d)[:, :, ds(b * BT, BT)], tmp[:, 2, :, :]).then_inc(xa_out, 16)
                sp.dma_start(byk(sx_d)[:, :, ds(b * BT, BT)], tmp[:, 3, :, :]).then_inc(xa_out, 16)
            sp.wait_ge(xa_out, 32 * NB)
        @block.vector
        def _(dve):
            V = nc.vector
            go = Steps(dve, c_st1)
            dve.wait_ge(v_ld, 16 * 11)
            for q_, s_ in ((QMK, TMK), (QMV, TMV), (QMR, TMR), (QCK, CMK), (QCR, CMR)):
                V.tensor_scalar(vec[:, q_, :], vec[:, s_, :], -1.0, 1.0, ALU.mult, ALU.add)
            V.memset(epsv[:, 0:1], 1e-8)
            V.memset(epsv[:, 1:2], 1e-5)
            for n, v in ((MX, -1e38), (SM, 1.0), (LS, -1e38), (AV, 0.0)):
                V.memset(stt_[:, n, :, BT:BT + 1], v)
            dve.wait_ge(wt_ld, 16)
            go(V.tensor_copy(wtm[0][:, :, :], wst[:, :, :]))
            V.tensor_tensor(wtm[1][:, :, :], wst[:, :, :], f32(wtm[0][:, :, :]), ALU.subtract).then_inc(wts_rdy, 1)
            for c in range(NC):
                last = V.bn_stats(st3[:, c, :], x_tok[:, c, :])
            go(last)
            for c in range(NC):
                last = V.bn_aggr(mv3[:, c, :], st3[:, c, :])
            go(last)
            V.tensor_scalar(small[:, 0, :], mv3[:, :, 1], 1e-5, None, ALU.add).then_inc(ln_w, 1)
            dve.wait_ge(ln_d, 1)
            go(V.reciprocal(small[:, 1, :], small[:, 0, :]))
            go(V.tensor_tensor(small[:, 2, :], small[:, 1, :], small[:, 1, :], ALU.mult))
            go(V.tensor_tensor(small[:, 2, :], small[:, 2, :], mv3[:, :, 1], ALU.mult))
            V.tensor_scalar(small[:, 2, :], small[:, 2, :], 1e-5, None, ALU.add).then_inc(ln_w, 1)
            dve.wait_ge(ln_d, 2)
            go(V.reciprocal(small[:, 3, :], small[:, 2, :]))
            go(V.tensor_tensor(small[:, 3, :], small[:, 3, :], small[:, 1, :], ALU.mult))
            V.tensor_scalar(tk[:, 0, 1, :], x_tok[:, 0, :], mv3[:, 0, 0:1], small[:, 1, 0:1],
                            ALU.subtract, ALU.mult).then_inc(tk_rdy, 1)
            with dve.Fori(0, NB) as b:
                go.turn(b, 15)
                for j in range(CPB):
                    c = b * CPB + j
                    x_, m_ = x_tok[:, ds(c, 1), :].rearrange("p o d -> p (o d)"), mv3[:, ds(c, 1), 0:1].rearrange("p o s -> p (o s)")
                    dve.wait_ge(tk_free, c + 1)
                    V.tensor_copy(tk[:, j % 2, 0, :], x_)
                    V.tensor_scalar(tk[:, j % 2, 1, :], x_, m_, small[:, 1, ds(c, 1)], ALU.subtract, ALU.mult)
                    V.tensor_scalar(tk[:, j % 2, 2, :], x_, m_, small[:, 3, ds(c, 1)], ALU.subtract,
                                    ALU.mult).then_inc(tk_rdy, 1)
                V.tensor_copy(stt_[:, :, :, 0:1], stt_[:, :, :, BT:BT + 1])
                dve.wait_ge(zt_rdy, b + 1)
                go(V.tensor_copy(a3s[0][:, :, :], a3[:, :, :]))
                V.tensor_tensor(a3s[1][:, :, :], a3[:, :, :], f32(a3s[0][:, :, :]), ALU.subtract).then_inc(a3_rdy, 1)
                for i, (q_, m_) in enumerate(((QMK, TMK), (QMV, TMV), (QMR, TMR))):
                    for k in range(KT):
                        last = V.tensor_scalar(mixed[:, i, k, :], Z2[:, k, 0:BT], vec[:, q_, k:k + 1], None, ALU.mult)
                go(last)
                for i, m_ in enumerate((TMK, TMV, TMR)):
                    dve.wait_ge(km_ps, b * 3 + (i + 1))
                    for k in range(KT):
                        last = V.scalar_tensor_tensor(mixed[:, i, k, :], B[2 * i + k][:, :], vec[:, m_, k:k + 1],
                                                      mixed[:, i, k, :], ALU.mult, ALU.add)
                    last.then_inc(km_out, 1)
                dve.wait_ge(km_out, b * 3 + 3)
                K_, V_ = mixed[:, 0, :, :], mixed[:, 1, :, :]
                prev, now = lambda n: stt_[:, n, :, 0:BT], lambda n: stt_[:, n, :, 1:BT + 1]
                for k in range(KT):
                    last = V.tensor_tensor_scan(stt_[:, MX, k, 1:BT + 1], vec[:, W_, k:k + 1].broadcast_to([128, BT]),
                                                mixed[:, 0, k, :], stt_[:, MX, k, 0:1], ALU.add, ALU.max)
                go(last)
                V.tensor_tensor(tmp[:, 0, :, :], prev(MX), now(MX), ALU.subtract)
                V.tensor_tensor(tmp[:, 1, :, :], K_, now(MX), ALU.subtract).then_inc(ex_w, 1)
                dve.wait_ge(ex_d, b * 3 + 1)
                for k in range(KT):
                    last = V.tensor_tensor_scan(stt_[:, SM, k, 1:BT + 1], tmp[:, 0, k, :], tmp[:, 1, k, :],
                                                stt_[:, SM, k, 0:1], ALU.mult, ALU.add)
                last.then_inc(ex_w, 1)
                dve.wait_ge(ex_d, b * 3 + 2)
                go(V.tensor_tensor(now(LS), now(MX), pq[:, :, :], ALU.add))
                for k in range(KT):
                    V.scalar_tensor_tensor(tmp[:, 0, k, :], stt_[:, LS, k, 0:BT], vec[:, W_, k:k + 1],
                                           mixed[:, 0, k, :], ALU.add, ALU.subtract)
                    last = V.scalar_tensor_tensor(tmp[:, 2, k, :], stt_[:, LS, k, 0:BT], vec[:, U_, k:k + 1],
                                                  mixed[:, 0, k, :], ALU.subtract, ALU.subtract)
                go(last)
                V.tensor_scalar(tmp[:, 1, :, :], tmp[:, 0, :, :], 0.0, None, ALU.max)
                V.tensor_scalar(tmp[:, 3, :, :], tmp[:, 2, :, :], 0.0, None, ALU.max)
                go(V.tensor_scalar(tmp[:, 0, :, :], tmp[:, 0, :, :], 0.0, None, ALU.min))
                V.tensor_scalar(tmp[:, 2, :, :], tmp[:, 2, :, :], 0.0, None, ALU.min).then_inc(ex_w, 1)
                dve.wait_ge(ex_d, b * 3 + 3)
                go(V.tensor_tensor(pq[:, :, :], tmp[:, 1, :, :], V_, ALU.mult))
                for k in range(KT):
                    last = V.tensor_tensor_scan(stt_[:, AV, k, 1:BT + 1], tmp[:, 0, k, :], pq[:, k, :],
                                                stt_[:, AV, k, 0:1], ALU.mult, ALU.add)
                go(last)
                V.tensor_tensor(tmp[:, 0, :, :], tmp[:, 2, :, :], prev(AV), ALU.mult)
                go(V.tensor_tensor(tmp[:, 1, :, :], tmp[:, 3, :, :], V_, ALU.mult))
                for k in range(KT):
                    last = V.scalar_tensor_tensor(tmp[:, 2, k, :], tmp[:, 2, k, :], 1e-8, tmp[:, 3, k, :], ALU.add, ALU.add)
                go(last)
                go(V.reciprocal(tmp[:, 2, :, :], tmp[:, 2, :, :]))
                go(V.tensor_tensor(tmp[:, 0, :, :], tmp[:, 0, :, :], tmp[:, 1, :, :], ALU.add))
                go(V.tensor_tensor(tmp[:, 0, :, :], tmp[:, 0, :, :], tmp[:, 2, :, :], ALU.mult))
                go(V.tensor_tensor(tmp[:, 0, :, :], tmp[:, 0, :, :], mixed[:, 2, :, :], ALU.mult))
                go(V.tensor_tensor(tmp[:, 2, :, :], tmp[:, 0, :, :], Z2[:, :, 1:BT + 1], ALU.add))
                V.tensor_tensor(tmp[:, 3, :, :], tmp[:, 2, :, :], x2T[:, :, :], ALU.add).then_inc(xa_rdy, 1)
                dve.wait_ge(xa_out, b * 32 + 32)
                dve.sem_inc(zb_free, 1)
                go.end(NB)

        @block.scalar
        def _(act):
            A_ = nc.scalar
            act.sem_inc(zb_free, 1)
            for n in range(2):
                act.wait_ge(ln_w, n + 1)
                A_.activation(small[:, 2 * n, :], small[:, 2 * n, :], ACT.Sqrt).then_inc(ln_d, 1)
            act.wait_ge(z0_ps, 1)
            A_.activation(Z2[:, :, BT:BT + 1], B[6][:, 0:256].rearrange("p (k n) -> p k n", k=KT)[:, :, 0:1],
                          ACT.Copy).then_inc(z_cy, 1)
            with act.Fori(0, NB) as b:
                act.wait_ge(z_cy, b + 1)
                act.wait_ge(zb_free, b + 1)
                A_.activation(Z2[:, :, 0:1], Z2[:, :, BT:BT + 1], ACT.Copy).then_inc(z_mv, 1)
                act.wait_ge(tk_free, b * CPB + (CPB + 2))
                act.wait_ge(z_mv, b + 1)
                for k in range(KT):
                    A_.activation(a3[:, k, :], B[4 + k][:, :], ACT.Identity, bias=vec[:, B1, k:k + 1], scale=vec[:, G1, k:k + 1])
                for k in range(KT):
                    A_.activation(x2T[:, k, :], B[k][:, :], ACT.Copy)
                A_.activation(Z2[:, 0, 1:BT + 1], B[2][:, :], ACT.Copy)
                A_.activation(Z2[:, 1, 1:BT + 1], B[3][:, :], ACT.Copy).then_inc(zt_rdy, 1)
                act.wait_ge(zt_rdy, b + 1)
                act.sem_inc(z_cy, 1)
                act.wait_ge(km_out, b * 3 + 3)
                A_.activation(mixed[:, 2, :, :], mixed[:, 2, :, :], ACT.Sigmoid)
                act.wait_ge(ex_w, b * 3 + 1)
                for k in range(KT):
                    A_.activation(tmp[:, 0, k, :], tmp[:, 0, k, :], ACT.Exp, bias=vec[:, W_, k:k + 1])
                A_.activation(tmp[:, 1, :, :], tmp[:, 1, :, :], ACT.Exp).then_inc(ex_d, 1)
                act.wait_ge(ex_w, b * 3 + 2)
                A_.activation(pq[:, :, :], stt_[:, SM, :, 1:BT + 1], ACT.Ln, bias=epsv[:, 0:1]).then_inc(ex_d, 1)
                act.wait_ge(ex_w, b * 3 + 3)
                A_.activation(tmp[:, 0, :, :], tmp[:, 0, :, :], ACT.Exp)
                A_.activation(tmp[:, 2, :, :], tmp[:, 2, :, :], ACT.Exp)
                A_.activation(tmp[:, 1, :, :], tmp[:, 1, :, :], ACT.Exp, scale=-1.0)
                A_.activation(tmp[:, 3, :, :], tmp[:, 3, :, :], ACT.Exp, scale=-1.0).then_inc(ex_d, 1)

        @block.tensor
        def _(pe):
            T = nc.tensor
            pe.wait_ge(tk_rdy, 1)
            for k in range(KT):
                last = T.transpose(B[6][:, k * 128:(k + 1) * 128], tk[:, 0, 1, k * 128:(k + 1) * 128], ident[:, :])
            last.then_inc(z0_ps, 1)
            pe.wait_ge(z0_ps, 1)
            pe.sem_inc(tk_free, 2)
            pe.wait_ge(wts_rdy, 1)
            with pe.Fori(0, NB) as b:
                for j in range(CPB):
                    pe.wait_ge(tk_rdy, b * CPB + (j + 2))
                    for a in range(3):
                        for k in range(KT):
                            last = T.transpose(B[2 * a + k][:, j * CH:(j + 1) * CH], tk[:, j % 2, a, k * 128:(k + 1) * 128],
                                               ident[:, :])
                    last.then_inc(tk_free, 1)
                pe.wait_ge(a3_rdy, b + 1)
                for i in range(3):
                    for mk in range(KT):
                        m = i * KT + mk
                        for k in range(KT):
                            last = mm3(B[m][:, :], [w[:, k, m * 128:(m + 1) * 128] for w in wtm],
                                       [x[:, k, :] for x in a3s], k == 0, k == KT - 1)
                    last.then_inc(km_ps, 1)
                pe.wait_ge(km_out, b * 3 + 3)

        pblk.close()
        pc.close()
        px.close()
        KH = HID // 128
        pd = ctx.enter_context(ExitStack())
        cst = sb("cst", [128, KT, HID], to=pd)
        cst2 = sb("cst2", [128, KH, D], to=pd)
        wcm = [sb(f"wcm{h}", [128, KT, HID], f32r, to=pd) for h in "hl"]
        wcp = [sb(f"wcp{h}", [128, KH, D], f32r, to=pd) for h in "hl"]
        IN = sb("IN", [128, 2, 3, KT, BT], to=pd)
        sq = sb("sq", [128, KT, BT], to=pd)
        rs = sb("rs", [128, BT], to=pd)
        XN = sb("XN", [128, KT, BT], to=pd)
        XNs = [sb(f"XN{h}", [128, KT, BT], f32r, to=pd) for h in "hl"]
        kx = sb("kx", [128, KT, BT], to=pd)
        rr = sb("rr", [128, KT, BT], to=pd)
        kq = sb("kq", [128, KT, BT], to=pd)
        kh = [sb(f"kh{h}", [128, KH, BT], f32r, to=pd) for h in "hl"]
        x3b = sb("x3b", [128, 2, KT, BT], to=pd)
        cw_ld, cw_rdy, cin_ld, c_free, d_st1 = (sem("channel_weights_loaded"), sem("channel_weights_split"),
                                                [sem(f"channel_block_loaded_{q}") for q in range(2)],
                                                sem("channel_block_free"), sem("channel_mix_steps"))
        mean_ps, xc_rdy, sqr_rdy, var_ps, rs_rdy, xn_rdy, rr_rdy, rr_d = (
            sem("mean_in_psum"), sem("centred"), sem("squares_ready"), sem("variance_in_psum"), sem("deviation_ready"),
            sem("xn_split"), sem("r_ready"), sem("r_sigmoid_done"))
        cm_ps, kk_tk, kk_rdy, cp_ps, x3_rdy, x3_out = (sem("key_in_psum"), sem("key_taken"), sem("key_split"),
                                                       sem("value_in_psum"), sem("x3_ready"),
                                                       [sem(f"x3_stored_{q}") for q in range(2)])
        pblk = ctx.enter_context(ExitStack())
        block = pblk.enter_context(nc.Block())

        @block.sync
        def _(sp):
            sp.dma_start(cst[:, :, :], byk(A["W_cm"])).then_inc(cw_ld, 16)
            sp.dma_start(cst2[:, :, :], A["W_cp"].rearrange("(k p) n -> p k n", p=128)).then_inc(cw_ld, 16)
            xa, sx, x3 = byk(xa_d), byk(sx_d), byk(x3_d)

            def load(b, q, first=False):
                sp.dma_start(IN[:, q, 0, :, :], xa[:, :, ds(b * BT, BT)]).then_inc(cin_ld[q], 16)
                if first:
                    sp.dma_start(IN[:, q, 1, :, 1:BT], xa[:, :, 0:BT - 1]).then_inc(cin_ld[q], 16)
                    with nc.allow_non_contiguous_dma(reason="one column of 256 channels"):
                        sp.dma_start(IN[:, q, 1, :, 0:1], xa[:, :, S - 1:S]).then_inc(cin_ld[q], 16)
                else:
                    sp.dma_start(IN[:, q, 1, :, :], xa[:, :, ds(b * BT - 1, BT)]).then_inc(cin_ld[q], 16)
                sp.dma_start(IN[:, q, 2, :, :], sx[:, :, ds(b * BT, BT)]).then_inc(cin_ld[q], 16)

            load(0, 0, True)
            load(1, 1)

            def store(t, q):
                b = t * 2 + q
                sp.wait_ge(x3_rdy, b + 1)
                sp.dma_start(x3[:, :, ds(b * BT, BT)], x3b[:, q, :, :]).then_inc(x3_out[q], 16)

            with sp.Fori(0, NB // 2 - 1) as t:
                for q in range(2):
                    store(t, q)
                    load(t * 2 + (q + 2), q)
            for q in range(2):
                store(NB // 2 - 1, q)
                sp.wait_ge(x3_out[q], 16 * (NB // 2) + 16)
        def norm_dve(dve, go, xin, out_step):
            V = nc.vector
            one = lambda a: a.rearrange("p (o n) -> p o n", o=1).broadcast_to([128, KT, BT])
            dve.wait_ge(mean_ps, out_step)
            V.tensor_tensor(xin, xin, one(B[0][:, :]), ALU.subtract).then_inc(xc_rdy, 1)
            dve.wait_ge(rs_rdy, out_step)
            go(V.reciprocal(rs[:, :], rs[:, :]))
            go(V.tensor_tensor(xin, xin, one(rs[:, :]), ALU.mult))

        def norm_act(act, xin, n):
            act.wait_ge(xc_rdy, n)
            nc.scalar.activation(sq[:, :, :], xin, ACT.Square).then_inc(sqr_rdy, 1)
            act.wait_ge(var_ps, n)
            nc.scalar.activation(rs[:, :], B[1][:, :], ACT.Sqrt, bias=epsv[:, 1:2]).then_inc(rs_rdy, 1)

        def norm_pe(pe, xin, n):
            for src, rdy, bk, out in ((xin, None, 0, mean_ps), (sq, sqr_rdy, 1, var_ps)):
                if rdy is not None:
                    pe.wait_ge(rdy, n)
                for k in range(KT):
                    last = nc.tensor.matmul(B[bk][:, :], avg[:, :], src[:, k, :], start=(k == 0), stop=(k == KT - 1))
                last.then_inc(out, 1)

        @block.vector
        def _(dve):
            V = nc.vector
            go = Steps(dve, d_st1)
            go(V.memset(avg[:, :], 1.0 / D))
            dve.wait_ge(cw_ld, 32)
            for st_, w in ((cst, wcm), (cst2, wcp)):
                go(V.tensor_copy(w[0][:, :, :], st_[:, :, :]))
                V.tensor_tensor(w[1][:, :, :], st_[:, :, :], f32(w[0][:, :, :]), ALU.subtract).then_inc(cw_rdy, 1)
            dve.wait_ge(cw_rdy, 2)
            with dve.Fori(0, NB // 2) as t:
                go.turn(t, 2 * (2 + 2 + 1 + 4 * 3 + 1))
                for q in range(2):
                    b = t * 2 + q
                    xa_, xp_, sx_ = (IN[:, q, n, :, :] for n in range(3))
                    norm_dve(dve, go, xa_, b + 1)
                    for k in range(KT):
                        last = V.tensor_scalar(XN[:, k, :], xa_[:, k, :], vec[:, G2, k:k + 1], vec[:, B2, k:k + 1],
                                               ALU.mult, ALU.add)
                    go(last)
                    go(V.tensor_copy(XNs[0][:, :, :], XN[:, :, :]))
                    V.tensor_tensor(XNs[1][:, :, :], XN[:, :, :], f32(XNs[0][:, :, :]), ALU.subtract).then_inc(xn_rdy, 1)
                    for k in range(KT):
                        V.tensor_scalar(kx[:, k, :], xp_[:, k, :], vec[:, QCK, k:k + 1], None, ALU.mult)
                        last = V.tensor_scalar(rr[:, k, :], xp_[:, k, :], vec[:, QCR, k:k + 1], None, ALU.mult)
                    go(last)
                    for k in range(KT):
                        last = V.scalar_tensor_tensor(rr[:, k, :], XN[:, k, :], vec[:, CMR, k:k + 1], rr[:, k, :],
                                                      ALU.mult, ALU.add)
                    last.then_inc(rr_rdy, 1)
                    for m in range(0, KH, 2):
                        for k in range(2):
                            dve.wait_ge(cm_ps, b * KH + (m + k + 1))
                            last = V.scalar_tensor_tensor(kq[:, k, :], B[2 + (m + k) % 4][:, :], vec[:, CMK, k:k + 1],
                                                          kx[:, k, :], ALU.mult, ALU.add)
                            last.then_inc(kk_tk, 1)
                        dve.wait_ge(kk_tk, b * KH + (m + 2 + 4))
                        go(V.scalar_tensor_tensor(kq[:, :, :].rearrange("p k n -> p (k n)"), kq[:, :, :].rearrange("p k n -> p (k n)"), 0.0,
                                                  kq[:, :, :].rearrange("p k n -> p (k n)"), ALU.max, ALU.mult))
                        go(V.tensor_copy(kh[0][:, m:m + 2, :], kq[:, :, :]))
                        go(V.tensor_tensor(kh[1][:, m:m + 2, :], kq[:, :, :], f32(kh[0][:, m:m + 2, :]), ALU.subtract))
                        dve.sem_inc(kk_rdy, 1)
                    dve.wait_ge(rr_d, b + 1)
                    dve.wait_ge(cp_ps, b + 1)
                    dve.wait_ge(x3_out[q], t * 16 + 16)
                    for k in range(KT):
                        last = V.tensor_tensor(rr[:, k, :], B[6 + k][:, :], rr[:, k, :], ALU.mult)
                    go(last)
                    V.tensor_tensor(x3b[:, q, :, :], rr[:, :, :], sx_, ALU.add).then_inc(x3_rdy, 1)
                go.end(NB // 2)

        @block.scalar
        def _(act):
            for q in range(2):
                act.sem_inc(x3_out[q], 16)
            act.sem_inc(kk_tk, 4)
            with act.Fori(0, NB // 2) as t:
                for q in range(2):
                    b = t * 2 + q
                    norm_act(act, IN[:, q, 0, :, :], b + 1)
                    act.wait_ge(rr_rdy, b + 1)
                    nc.scalar.activation(rr[:, :, :], rr[:, :, :], ACT.Sigmoid).then_inc(rr_d, 1)

        @block.tensor
        def _(pe):
            pe.wait_ge(cw_rdy, 2)
            with pe.Fori(0, NB // 2) as t:
                for q in range(2):
                    b = t * 2 + q
                    pe.wait_ge(cin_ld[q], t * 48 + (64 - 16 * q))
                    norm_pe(pe, IN[:, q, 0, :, :], b + 1)
                    pe.wait_ge(xn_rdy, b + 1)
                    for m in range(KH):
                        pe.wait_ge(kk_tk, b * KH + (m + 1))
                        for k in range(KT):
                            last = mm3(B[2 + m % 4][:, :], [w[:, k, m * 128:(m + 1) * 128] for w in wcm],
                                       [x[:, k, :] for x in XNs], k == 0, k == KT - 1)
                        last.then_inc(cm_ps, 1)
                    for k in range(KH):
                        if k % 2 == 0:
                            pe.wait_ge(kk_rdy, b * (KH // 2) + (k // 2 + 1))
                        for m in range(KT):
                            last = mm3(B[6 + m][:, :], [w[:, k, m * 128:(m + 1) * 128] for w in wcp],
                                       [h[:, k, :] for h in kh], k == 0, k == KH - 1)
                    last.then_inc(cp_ps, 1)
                    pe.wait_ge(x3_rdy, b + 1)

        pblk.close()
        pd.close()
        pe_ = ctx.enter_context(ExitStack())
        names = (("w1", KT, HID), ("w2", KT, HID), ("h1", KH, HID), ("h2", KH, HID), ("w3", KH, D))
        FW = {n: sb("ffn_" + n, [128, k, c], f32r, to=pe_) for n, k, c in names}
        scl = sb("scl", [128, 4 * KH + KT], to=pe_)
        x3i = sb("x3i", [128, 2, KT, BT], to=pe_)
        sq2 = sb("sq2", [128, KT, BT], to=pe_)
        rs2 = sb("rs2", [128, BT], to=pe_)
        xc = sb("xc", [128, KT, BT], to=pe_)
        fT = [sb(f"fT{h}", [128, KT, BT], f32r, to=pe_) for h in "hl"]
        hA = [sb(f"hA{h}", [128, KH, BT], f32r, to=pe_) for h in "hl"]
        hB = [sb(f"hB{h}", [128, KH, BT], f32r, to=pe_) for h in "hl"]
        gq = sb("gq", [128, 4, BT], to=pe_)
        outb = sb("outb", [128, KT, BT], to=pe_)
        flg = sb("flg", [128, 16], to=pe_)
        flr = sb("flr", [1, 2], i32, to=pe_)
        fw_ld, sc_ld, x3_ld, e_st = (sem("ffn_weights_loaded"), sem("ffn_scales_loaded"),
                                     [sem(f"x3_loaded_{q}") for q in range(2)], sem("ffn_steps"))
        fl_rdy, fl_ps, fl_rg = sem("low_bits_counted"), sem("low_bits_summed"), sem("low_bits_flag")
        m2_ps, c2_rdy, s2_rdy, v2_ps, r2_rdy, f_rdy2 = (sem("ffn_mean_in_psum"), sem("ffn_centred"), sem("ffn_squares"),
                                                       sem("ffn_variance_in_psum"), sem("ffn_deviation"), sem("f_split"))
        bk_ps, g_act, h_spl, bk_free, o_ps, o_rdy2, o_out = (
            sem("bank_filled"), sem("activation_done"), sem("hidden_split"), sem("bank_free"), sem("out_in_psum"),
            sem("out_ready"), sem("out_stored"))
        a_rdy = sem("gate_ready")
        pblk = ctx.enter_context(ExitStack())
        block = pblk.enter_context(nc.Block())
        off = dict(w1=0, w2=KH, h1=2 * KH, h2=3 * KH, w3=4 * KH)

        @block.sync
        def _(sp):
            sp.wait_ge(cp_w, 16 * len(names))
            for n, k, c in names:
                sp.dma_start(f32(FW[n][:, :, :]), raw[n].rearrange("(k p) n -> p k n", p=128)).then_inc(fw_ld, 16)
            sp.dma_start(scl[:, :], A["scales"]).then_inc(sc_ld, 16)
            x3 = byk(x3_d)
            for q in range(2):
                sp.dma_start(x3i[:, q, :, :], x3[:, :, q * BT:(q + 1) * BT]).then_inc(x3_ld[q], 16)

            def store(b):
                sp.wait_ge(o_rdy2, b + 1)
                sp.dma_start(byk(A["out"])[:, :, ds(b * BT, BT)], outb[:, :, :]).then_inc(o_out, 16)

            with sp.Fori(0, NB // 2 - 1) as t:
                for q in range(2):
                    b = t * 2 + q
                    store(b)
                    sp.dma_start(x3i[:, q, :, :], x3[:, :, ds((b + 2) * BT, BT)]).then_inc(x3_ld[q], 16)
            for q in range(2):
                store(NB - 2 + q)
            sp.wait_ge(o_out, 16 * NB + 16)

        @block.vector
        def _(dve):
            V = nc.vector
            go = Steps(dve, e_st)
            dve.sem_inc(o_out, 16)
            dve.wait_ge(sc_ld, 16)
            dve.wait_ge(fw_ld, 16 * len(names))
            go(V.memset(flg[:, :], 0.0))
            rnd = hA[0][:, :, :].rearrange("p k n -> p (k n)")
            n = 0
            for nm, k, c in names:
                w = FW[nm][:, :, :].rearrange("p k n -> p (k n)")
                for o in range(0, k * c, 4096):
                    m = min(4096, k * c - o)
                    go(V.tensor_copy(rnd[:, 0:m], f32(w[:, o:o + m])))
                    go(V.scalar_tensor_tensor(hB[0][:, :, :].rearrange("p k n -> p (k n)")[:, 0:m], f32(w[:, o:o + m]), 0.0,
                                              f32(rnd[:, 0:m]), ALU.add, ALU.not_equal, accum_out=flg[:, n:n + 1]))
                    n += 1
            go(V.tensor_reduce(flg[:, 15:16], flg[:, 0:15], AX.X, ALU.add))
            V.tensor_copy(flg[:, 14:15], flg[:, 15:16]).then_inc(fl_rdy, 1)
            dve.wait_ge(fl_ps, 1)
            V.tensor_scalar(flr[0:1, 0:1], B[7][0:1, 0:1], 0.0, None, ALU.is_gt).then_inc(fl_rg, 1)
            one = lambda a: a.rearrange("p (o n) -> p o n", o=1).broadcast_to([128, KT, BT])

            def split(dst, m, b, layer):
                src = gq[:, m % 4:m % 4 + 2, :]
                go(V.tensor_copy(dst[0][:, m:m + 2, :], src))
                V.tensor_tensor(dst[1][:, m:m + 2, :], src, f32(dst[0][:, m:m + 2, :]), ALU.subtract).then_inc(h_spl, 1)

            with dve.Fori(0, NB // 2) as t:
                go.turn(t, 2 * (3 + 4 * 2 + 4 + 4))
                for q in range(2):
                    b = t * 2 + q
                    x_ = x3i[:, q, :, :]
                    dve.wait_ge(m2_ps, b + 1)
                    V.tensor_tensor(xc[:, :, :], x_, one(B[0][:, :]), ALU.subtract).then_inc(c2_rdy, 1)
                    dve.wait_ge(r2_rdy, b + 1)
                    go(V.reciprocal(rs2[:, :], rs2[:, :]))
                    go(V.tensor_tensor(xc[:, :, :], xc[:, :, :], one(rs2[:, :]), ALU.mult))
                    go(V.tensor_copy(fT[0][:, :, :], xc[:, :, :]))
                    V.tensor_tensor(fT[1][:, :, :], xc[:, :, :], f32(fT[0][:, :, :]), ALU.subtract).then_inc(f_rdy2, 1)
                    for m in range(0, KH, 2):
                        for k in range(2):
                            dve.wait_ge(a_rdy, b * KH + (m + k + 1))
                            last = V.scalar_tensor_tensor(gq[:, (m + k) % 4, :], B[3 + 2 * ((m + k) % 2)][:, :],
                                                          scl[:, off["w2"] + m + k:off["w2"] + m + k + 1],
                                                          gq[:, (m + k) % 4, :], ALU.mult, ALU.mult)
                            last.then_inc(bk_free, 1)
                        dve.wait_ge(bk_free, b * (3 * KH) + (m + 2 + 4))
                        go(V.tensor_copy(hA[0][:, m:m + 2, :], gq[:, m % 4:m % 4 + 2, :]))
                        go(V.tensor_tensor(hA[1][:, m:m + 2, :], gq[:, m % 4:m % 4 + 2, :], f32(hA[0][:, m:m + 2, :]), ALU.subtract))
                        dve.sem_inc(h_spl, 1)
                    for layer, dst in ((1, hB), (2, hA)):
                        for m in range(0, KH, 2):
                            dve.wait_ge(g_act, b * (2 * KH) + ((layer - 1) * KH + m + 2))
                            split(dst, m, b, layer)
                    dve.wait_ge(o_ps, b + 1)
                    dve.wait_ge(o_out, b * 16 + 16)
                    for k in range(KT):
                        last = V.scalar_tensor_tensor(outb[:, k, :], B[6 + k][:, :],
                                                      scl[:, off["w3"] + k:off["w3"] + k + 1], x_[:, k, :],
                                                      ALU.mult, ALU.add)
                    last.then_inc(o_rdy2, 1)
                    dve.wait_ge(o_rdy2, b + 1)
                go.end(NB // 2)

        @block.scalar
        def _(act):
            A_ = nc.scalar
            act.sem_inc(bk_free, 4)
            act.wait_ge(sc_ld, 16)
            with act.Fori(0, NB // 2) as t:
                for q in range(2):
                    b = t * 2 + q
                    act.wait_ge(c2_rdy, b + 1)
                    A_.activation(sq2[:, :, :], xc[:, :, :], ACT.Square).then_inc(s2_rdy, 1)
                    act.wait_ge(v2_ps, b + 1)
                    A_.activation(rs2[:, :], B[1][:, :], ACT.Sqrt, bias=epsv[:, 1:2]).then_inc(r2_rdy, 1)
                    HS = 12
                    for m in range(KH):
                        act.wait_ge(bk_ps, b * (3 * KH) + (m + 1))
                        if m >= 4:
                            act.wait_ge(h_spl, b * HS + ((m - 4) // 2 + 1))
                        A_.activation(gq[:, m % 4, :], B[2 + 2 * (m % 2)][:, :], ACT.Silu,
                                      scale=scl[:, off["w1"] + m:off["w1"] + m + 1]).then_inc(a_rdy, 1)
                    for layer, nm in ((1, "h1"), (2, "h2")):
                        for m in range(KH):
                            act.wait_ge(bk_ps, b * (3 * KH) + (layer * KH + m + 1))
                            act.wait_ge(h_spl, b * HS + (layer * 4 + (m - 4) // 2 + 1))
                            A_.activation(gq[:, m % 4, :], B[2 + m % 4][:, :], ACT.Gelu,
                                          scale=scl[:, off[nm] + m:off[nm] + m + 1]).then_inc(g_act, 1)
                            act.wait_ge(g_act, b * (2 * KH) + ((layer - 1) * KH + m + 1))
                            act.sem_inc(bk_free, 1)

        @block.tensor
        def _(pe):
            T = nc.tensor
            pe.wait_ge(fl_rdy, 1)
            T.matmul(B[7][:, 0:1], one_m[:, :], flg[:, 15:16], start=True, stop=True).then_inc(fl_ps, 1)
            pe.wait_ge(fl_rg, 1)
            flag = pe.alloc_register("low_bits")
            pe.reg_load(flag, flr[0:1, 0:1])

            def block_of(b, q, exact):
                def mm(out, w, x, first, last):
                    if exact:
                        T.matmul(out, w, x[0], start=first, stop=False)
                        return T.matmul(out, w, x[1], start=False, stop=last)
                    T.matmul(out, f32(w), f32(x[0]), start=first, stop=False)
                    return T.matmul(out, f32(w), f32(x[1]), start=False, stop=last)

                pe.wait_ge(f_rdy2, b + 1)
                HS = 12
                for m in range(KH):
                    pe.wait_ge(bk_free, b * (3 * KH) + (m + 3))
                    for n, nm in enumerate(("w1", "w2")):
                        for k in range(KT):
                            last = mm(B[2 + 2 * (m % 2) + n][:, :], FW[nm][:, k, m * 128:(m + 1) * 128],
                                      [f[:, k, :] for f in fT], k == 0, k == KT - 1)
                    last.then_inc(bk_ps, 1)
                for layer, nm, src in ((1, "h1", hA), (2, "h2", hB)):
                    for m in range(KH):
                        pe.wait_ge(bk_free, b * (3 * KH) + (KH + 3 + m // 2 if layer == 1 and m < 4 else layer * KH + m + 1))
                        for k in range(KH):
                            if m == 0 and k % 2 == 0:
                                pe.wait_ge(h_spl, b * HS + ((layer - 1) * 4 + k // 2 + 1))
                            last = mm(B[2 + m % 4][:, :], FW[nm][:, k, m * 128:(m + 1) * 128],
                                      [h[:, k, :] for h in src], k == 0, k == KH - 1)
                        last.then_inc(bk_ps, 1)
                for k in range(KH):
                    if k % 2 == 0:
                        pe.wait_ge(h_spl, b * HS + (8 + k // 2 + 1))
                    for m in range(KT):
                        last = mm(B[6 + m][:, :], FW["w3"][:, k, m * 128:(m + 1) * 128],
                                  [h[:, k, :] for h in hA], k == 0, k == KH - 1)
                last.then_inc(o_ps, 1)

            def turn(t, exact):
                for q in range(2):
                    b = t * 2 + q
                    pe.wait_ge(x3_ld[q], t * 16 + 16)
                    for src, rdy, bk, out in ((x3i[:, q, :, :], None, 0, m2_ps), (sq2, s2_rdy, 1, v2_ps)):
                        if rdy is not None:
                            pe.wait_ge(rdy, b + 1)
                        for k in range(KT):
                            last = T.matmul(B[bk][:, :], avg[:, :], src[:, k, :], start=(k == 0), stop=(k == KT - 1))
                        last.then_inc(out, 1)
                    block_of(b, q, exact)

            with pe.If_eq(flag, 0):
                with pe.Fori(0, NB // 2) as t:
                    turn(t, True)
            with pe.Else():
                with pe.Fori(0, NB // 2) as t:
                    turn(t, False)

        pblk.close()
        pe_.close()


def layout(I):
    import numpy as np
    g = lambda n: np.asarray(I[n])
    t = lambda n: np.ascontiguousarray(g(n).T)
    out = {
        "x": g("L0_attn_x"),
        "wcatT": np.ascontiguousarray(np.concatenate([g("L0_attn_Wk"), g("L0_attn_Wv"), g("L0_attn_Wq"), g("L0_attn_pw")], 0).T),
        "wvT": t("L0_attn_Wv"), "ir1T": t("L0_attn_ir_w1"), "ir2T": t("L0_attn_ir_w2"),
        "nm1T": t("L0_attn_nm_w1"), "nm2T": t("L0_attn_nm_w2"), "woT": t("L0_attn_Wo"), "wroT": g("L0_ffn_w_router"),
        "ir_b1": g("L0_attn_ir_b1"), "ir_b2": g("L0_attn_ir_b2"), "nm_b1": g("L0_attn_nm_b1"), "nm_b2": g("L0_attn_nm_b2"),
        "norm_w": g("L0_attn_norm_w"),
        "fast_alpha": g("L0_attn_fast_alpha").reshape(1), "slow_alpha": g("L0_attn_slow_alpha").reshape(1),
    }
    out.update({"w1": g("L0_ffn_w1"), "w2": g("L0_ffn_w2"), "b1T": np.ascontiguousarray(g("L0_ffn_b1").reshape(NE * HID // 128, 128).T), "b2": g("L0_ffn_b2")})
    vk = lambda n: np.ascontiguousarray(g("L1_attn_" + n).reshape(KT, 128).T)
    for n in ("time_decay", "time_first", "tmk", "tmv", "tmr", "g1", "g2", "cmk", "cmr"):
        out[n] = vk(n)
    out["b1v"], out["b2v"] = vk("b1"), vk("b2")
    for n in ("W_tm", "W_cm", "W_cp"):
        out[n] = g("L1_attn_" + n)
    col = lambda n: g("L1_ffn_" + n).reshape(-1, 128).T
    out["scales"] = np.ascontiguousarray(np.concatenate([col(n) for n in ("w1_s", "w2_s", "h1_s", "h2_s", "w3_s")], 1))
    for n in ("w1", "w2", "h1", "h2", "w3"):
        out["ffn_" + n] = t("L1_ffn_" + n + "_w")
    return out


def kernel(**inputs):
    import numpy as np
    import concourse.bacc as _bacc
    from concourse import mybir as _mybir
    from concourse.bass_utils import run_bass_kernel_spmd as _run

    nc = _bacc.Bacc("TRN2", target_bir_lowering=False, num_devices=1)
    arrays, A = {}, {}
    for name, a in layout(inputs).items():
        arrays[f"in_{name}_dram"] = a
        A[name] = nc.dram_tensor(f"in_{name}_dram", a.shape, _mybir.dt.from_np(a.dtype), kind="ExternalInput").ap()
    A["out"] = nc.dram_tensor("out_0_dram", (D, S), _mybir.dt.float32, kind="ExternalOutput").ap()
    build(nc, A)
    r = _run(nc, [arrays], core_ids=[0])
    return np.ascontiguousarray(np.asarray(r.results[0]["out_0_dram"]).T).reshape(1, S, D)
```

```python
import concourse.bass as bass
from concourse import mybir
from contextlib import ExitStack

S, D, DS, HID, NE = 4096, 256, 64, 1024, 8
CH = 128
NC = S // CH
KT = D // 128
BT = 512
NB = S // BT
CPB = BT // CH
PJ = 3 * DS + 3
LOGIT = 0.8472978603872034
LEVELS = 7
TT = 256
MT = 2 * S // TT + NE


class Steps:

    def __init__(self, eng, sem):
        self.eng, self.sem, self.done, self.here, self.at = eng, sem, 0, 0, None

    def on(self, eng):
        self.eng = eng
        return self

    def turn(self, i, per):
        self.at, self.per, self.here = i, per, 0

    def end(self, turns):
        assert self.here == self.per, (self.here, self.per)
        self.done += turns * self.per
        self.at, self.here = None, 0

    def __call__(self, ins):
        ins.then_inc(self.sem, 1)
        if self.at is None:
            self.done += 1
            self.eng.wait_ge(self.sem, self.done)
        else:
            self.here += 1
            self.eng.wait_ge(self.sem, self.at * self.per + (self.done + self.here))


def build(nc, A):
    fp32, f32r, i32, u32 = mybir.dt.float32, mybir.dt.float32r, mybir.dt.int32, mybir.dt.uint32
    ALU, ACT, AX = mybir.AluOpType, mybir.ActivationFunctionType, mybir.AxisListType
    ds = bass.ds

    ctx = ExitStack()
    with ctx:
        def sem(name):
            return ctx.enter_context(nc.semaphore(name))

        def bank(name):
            return ctx.enter_context(nc.psum_tensor(name, [128, 512], fp32))

        shapes = (("w1", D, HID), ("w2", D, HID), ("h1", HID, HID), ("h2", HID, HID), ("w3", HID, D))
        WORDS = sum(r * c for _, r, c in shapes)
        raw_d = nc.dram_tensor("ffn_copy", (WORDS,), fp32, kind="Internal").ap()
        raw, o = {}, 0
        for n, rows, cols in shapes:
            raw[n] = raw_d[o:o + rows * cols].rearrange("(r c) -> r c", c=cols)
            o += rows * cols
        x_tok_d = A["x"].rearrange("o (c p) d -> p (o c) d", p=CH)
        z1_d = nc.dram_tensor("z1_sorted", (MT * TT, D), fp32, kind="Internal").ap()
        ym_d = nc.dram_tensor("moe_sorted", (MT * TT, D), fp32, kind="Internal").ap()

        def sb(name, shape, dt=fp32, to=None):
            return (to or ctx).enter_context(nc.sbuf_tensor(name, shape, dt))

        def f32(ap):
            return ap.bitcast(fp32)

        ident = sb("ident", [128, 128])
        one_m = sb("one_m", [128, 128])
        slot1 = sb("slot1", [128, NC], i32)
        slot2 = sb("slot2", [128, NC], i32)
        gate1 = sb("gate1", [128, NC])
        gate2 = sb("gate2", [128, NC])
        tiles0 = sb("tiles0", [1, NE + 1], i32)
        small = sb("small", [128, 16, NC])
        sc8 = sb("sc8", [128, 8])

        NV = 15
        (W_, U_, TMK, TMV, TMR, G1, B1, G2, B2, CMK, CMR, QMK, QMV, QMR, QCK) = range(NV)
        QCR = NV
        vec = sb("vec", [128, NV + 1, KT])
        epsv = sb("epsv", [128, 2])
        avg = sb("avg", [128, 128])
        CK = 256
        lowb = sb("lowb", [128, CK])
        px = ctx.enter_context(ExitStack())
        x_tok = sb("x_tok", [128, NC, D], to=px)

        pz = ctx.enter_context(ExitStack())
        WP = sb("WP", [128, NC, 256], to=pz)
        pa = ctx.enter_context(ExitStack())
        PR = sb("PR", [128, NC, 200], to=pa)
        NU = sb("NU", [DS, S], to=pa)
        wcat = sb("wcat", [128, KT, PJ], to=pa)
        wvT = sb("wvT", [128, KT, DS], to=pa)
        ir1T = sb("ir1T", [128, KT, DS], to=pa)
        ir2T = sb("ir2T", [DS, 1], to=pa)
        nm1T = sb("nm1T", [DS, 2 * DS], to=pa)
        nm2T = sb("nm2T", [2 * DS, DS], to=pa)
        wroT = sb("wroT", [128, KT, NE], to=pa)
        woT = sb("woT", [DS, D], to=pa)
        woN = sb("woN", [DS, D], to=pa)
        b_ir1 = sb("b_ir1", [DS, 1], to=pa)
        b_nm1 = sb("b_nm1", [2 * DS, 1], to=pa)
        b_nm2 = sb("b_nm2", [DS, 1], to=pa)
        normw = sb("normw", [DS, 1], to=pa)
        scal = sb("scal", [128, 4], to=pa)
        st = sb("st", [128, NC, 6], to=pa)
        mv = sb("mv", [128, NC, 2], to=pa)
        zt = sb("zt", [128, 2, D], to=pa)
        zT = sb("zT", [128, KT, BT], to=pa)
        vT = sb("vT", [DS, BT], to=pa)
        gT = sb("gT", [DS, BT], to=pa)
        hT = sb("hT", [128, BT], to=pa)
        maskL = sb("maskL", [128, 2, 2, 128], to=pa)
        maskQ = sb("maskQ", [128, 2, 128], to=pa)
        pw_s = sb("pw_s", [128, 2, 132], to=pa)
        lam = sb("lam", [128, 2], to=pa)
        rev = sb("rev", [128, 2], to=pa)
        beta = sb("beta", [128, 2], to=pa)
        blam = sb("blam", [128, 2], to=pa)
        alC = sb("alC", [128, 2], to=pa)
        state = sb("state", [DS, 2, DS], to=pa)
        KQ = sb("KQ", [128, 2, 2, 3, DS], to=pa)
        KR = sb("KR", [128, 2, 2, 2, DS], to=pa)
        KQT = sb("KQT", [DS, 2, 2, 5, 128], to=pa)
        X = sb("X", [128, 2, 2, 2, 128], to=pa)
        L = sb("L", [128, 2, 2, 2, 4, 128], to=pa)
        QM = sb("QM", [128, 2, 2, 2, 128], to=pa)
        YT = sb("YT", [DS, 2, 2, 128], to=pa)
        lamr = sb("lamr", [DS, 2, 128], to=pa)
        Lv = L[:, :, :, :, :, :].rearrange("p a b c d e -> p (a b c d e)")
        ubc, ot, ts = Lv[:, 0:CPB * DS], Lv[:, 256:256 + CPB * DS], Lv[:, 512:512 + CPB * DS]
        aN, bN, nsT, oT = (Lv[0:DS, 1024 + n * BT:1024 + (n + 1) * BT] for n in range(4))
        nsC = Lv[0:DS, 3072:3073]
        z1T = sb("z1T", [128, 2, KT, 128], to=pa)
        LG = sb("LG", [128, NC, NE], to=pa)
        big = sb("big", [128, NC, DS], to=pa)
        rt = sb("rt", [128, 6, NC, NE], to=pa)
        top8 = sb("top8", [128, NC, 8], to=pa)
        idx8 = sb("idx8", [128, NC, 8], u32, to=pa)
        iota8 = sb("iota8", [128, NC, NE], to=pa)
        base8 = sb("base8", [128, NE], to=pa)
        tri = sb("tri", [128, 128], to=pa)
        cnt8 = sb("cnt8", [128, 4, NE], to=pa)
        ckS = sb("ckS", [128, 1], to=pa)
        ckr = sb("ckr", [128, CK], f32r, to=pa)
        zero = sb("zero", [128, 4 * D], to=pa)

        B = [bank(f"bank{i}") for i in range(8)]

        ld_x, ld_w, ld_s = sem("x_loaded"), sem("weights_loaded"), sem("scalars_loaded")
        consts = sem("constants_ready")
        d_st, p_st = sem("vector_steps"), sem("pool_steps")
        steps = Steps(None, d_st)
        z_rdy, zT_rdy = sem("z_ready"), sem("zT_ready")
        pj_ps, pj_out = sem("projection_in_psum"), sem("projection_taken")
        ti_ps, gT_rdy, vT_rdy = sem("vT_irT_in_psum"), sem("gT_ready"), sem("vT_ready")
        hd_ps, hd_rdy, nu_ps, nu_out = sem("nm_hidden_in_psum"), sem("nm_hidden_ready"), sem("nu_imp_in_psum"), sem("nu_imp_taken")
        sq_rdy, sq_done = sem("sqrt_wanted"), sem("sqrt_done")
        kq_rdy, kqt_ps, kqt_rdy = sem("kq_ready"), sem("kqT_in_psum"), sem("kqT_ready")
        g_ps, l_rdy = sem("gram_in_psum"), sem("L_ready")
        sq_ps, sq_cp = sem("square_in_psum"), sem("square_taken")
        ap_ps, ap_rdy = sem("LX_in_psum"), sem("X_ready")
        yt_ps, yt_rdy = sem("YT_in_psum"), sem("YT_ready")
        w_ps, w_rdy, f_rdy, pp_ps, pp_rdy = (sem("Yf_in_psum"), sem("w_ready"), sem("state_ready"), sem("pred_in_psum"), sem("pred_taken"))
        ub_rdy, ub_ps, ns_rdy, nst_ps, o_rdy, ot_ps, oT_rdy, wo_ps, wo_out = (
            sem("u_copied"), sem("u_rows_in_psum"), sem("ns_ready"), sem("nsT_back_in_psum"), sem("o_ready"),
            sem("oT_in_psum"), sem("oT_ready"), sem("attn_out_in_psum"), sem("x1_ready"))
        z1_rdy, z1_ps, z1T_rdy, lg_ps = (sem("z1_ready"), sem("z1T_in_psum"), sem("z1T_ready"),
                                        sem("logits_in_psum"))
        rk_rdy, rk_ps, scat = sem("mask_ready"), sem("ranks_in_psum"), sem("rows_scattered")
        cp_w = sem("ffn_weights_copied")
        ck_ld, ck_st = [sem(f"check_loaded_{q}") for q in range(2)], sem("check_steps")
        NCK = WORDS // (128 * CK)
        assert NCK % 2 == 0 and WORDS == NCK * 128 * CK
        zf = sem("zeros_stored")
        ZF = MT * TT // (128 * 4)
        x_rdy, lq_rdy, mk_cp = sem("right_side_ready"), sem("decayed_q_ready"), sem("decay_rows_ready")
        zt_free, mk_rdy, mk_ps = sem("z_buffer_free"), sem("masks_ready"), sem("mask_transposes_in_psum")

        def pj(o, n=1):
            return slice(o, o + n * DS)

        pblk = ctx.enter_context(ExitStack())
        block = pblk.enter_context(nc.Block())

        @block.sync
        def _(sp):
            sp.dma_start(x_tok[:, :, :], x_tok_d).then_inc(ld_x, 16)
            col = lambda a: a.rearrange("(p o) -> p o", o=1)
            for dst, src in ((wcat, A["wcatT"]), (wvT, A["wvT"]), (ir1T, A["ir1T"]), (wroT, A["wroT"])):
                sp.dma_start(dst[:, :, :], src.rearrange("(k p) n -> p k n", p=128)).then_inc(ld_w, 16)
            for dst, src in ((ir2T, A["ir2T"]), (nm1T, A["nm1T"]), (nm2T, A["nm2T"]), (woT, A["woT"]),
                             (b_ir1, col(A["ir_b1"])), (b_nm1, col(A["nm_b1"])), (b_nm2, col(A["nm_b2"])),
                             (normw, col(A["norm_w"]))):
                sp.dma_start(dst[:, :], src).then_inc(ld_w, 16)
            for n, a in enumerate((A["fast_alpha"], A["slow_alpha"], A["ir_b2"])):
                sp.dma_start(scal[:, n:n + 1], a.rearrange("(o n) -> o n", o=1).broadcast_to([128, 1])).then_inc(ld_s, 16)
            for n in raw:
                sp.dma_start(raw[n], A["ffn_" + n]).then_inc(cp_w, 16)
            sp.wait_ge(consts, 2)
            for d_ in (z1_d, ym_d):
                v = d_.rearrange("(a p r) d -> a p (r d)", p=128, r=4)
                for a in range(ZF):
                    sp.dma_start(v[a], zero[:, :]).then_inc(zf, 16)
        RSTD, RK, RQ, US, P0, P1, P2, UN, QKD, RO, IMP, T0, T1, T2, T3, RST1 = range(16)

        @block.gpsimd
        def _(pool):
            go = Steps(pool, p_st)
            go(nc.gpsimd.memset(ident[:, :], 0.0))
            nc.gpsimd.memset(one_m[:, :], 1.0)
            go(nc.gpsimd.memset(tri[:, :], 1.0))
            go(nc.gpsimd.affine_select(out=ident[:, :], in_=ident[:, :], compare_op=ALU.not_equal, fill=1.0,
                                       base=0, pattern=[[-1, 128]], channel_multiplier=1))
            go(nc.gpsimd.affine_select(out=tri[:, :], in_=tri[:, :], compare_op=ALU.is_gt, fill=0.0,
                                       base=0, pattern=[[1, 128]], channel_multiplier=-1))
            go(nc.gpsimd.iota(idx8[:, :, :].bitcast(i32), pattern=[[0, NC], [1, NE]], base=0, channel_multiplier=0))
            go(nc.gpsimd.tensor_copy(iota8[:, :, :], idx8[:, :, :].bitcast(i32)))
            nc.gpsimd.memset(sc8[:, :], 0.0).then_inc(consts, 1)
            nc.gpsimd.memset(zero[:, :], 0.0).then_inc(consts, 1)
            P = nc.gpsimd
            ckb = lambda q: zero[:, q * CK:(q + 1) * CK]
            pool.wait_ge(zf, 16 * 2 * ZF)
            pool.wait_ge(cp_w, 16 * len(shapes))
            words = raw_d.rearrange("(c p n) -> c p n", p=128, n=CK)
            P.memset(lowb[:, :], 0.0).then_inc(ck_st, 1)
            P.memset(ckS[:, :], 2.0 ** 60).then_inc(ck_st, 1)
            pool.wait_ge(ck_st, 2)
            for q in range(2):
                pool.dma_start(ckb(q), words[q]).then_inc(ck_ld[q], 16)

            def check(i, q):
                c = i * 2 + q
                k_ = ckb(q)
                pool.wait_ge(ck_ld[q], i * 16 + 16)
                for n, (dst, a, b_, op) in enumerate((
                        (ckr[:, :], k_, one_m[:, 0:1].broadcast_to([128, CK]), ALU.mult),
                        (k_, k_, f32(ckr[:, :]), ALU.subtract),
                        (k_, k_, ckS[:, 0:1].broadcast_to([128, CK]), ALU.mult),
                        (k_, k_, k_, ALU.mult),
                        (lowb[:, :], lowb[:, :], k_, ALU.add))):
                    P.tensor_tensor(dst, a, b_, op).then_inc(ck_st, 1)
                    pool.wait_ge(ck_st, c * 5 + (n + 3))

            def checks(i):
                for q in range(2):
                    check(i, q)
                    pool.dma_start(ckb(q), words[ds(i * 2 + (2 + q), 1)].rearrange("o p n -> (o p) n")).then_inc(ck_ld[q], 16)

            EARLY = 8
            with pool.Fori(0, EARLY) as i:
                checks(i)
            pool.wait_ge(mk_cp, 2)
            with pool.Fori(0, NC // 4) as h:
                for p in range(2):
                    for j in range(2):
                        c = h * 4 + (2 * p + j)
                        pool.wait_ge(kqt_rdy, c + 1)
                        nc.gpsimd.tensor_tensor(KQT[:, p, j, 3:5, :], KQT[:, p, j, 2:3, :].broadcast_to([DS, 2, 128]),
                                                lamr[:, :, :], ALU.mult).then_inc(lq_rdy, 1)
                    checks(h * 2 + (EARLY + p))
            with pool.Fori(NC // 2 + EARLY, NCK // 2 - 1) as i:
                checks(i)
            for q in range(2):
                check(NCK // 2 - 1, q)
        @block.vector
        def _(dve):
            V = nc.vector
            go = steps.on(dve)
            def row(t, c):
                return t[:, ds(c, 1), :].rearrange("p o d -> p (o d)")

            def ln_stats():
                for c in range(NC):
                    last = V.bn_stats(st[:, c, :], x_tok[:, c, :])
                go(last)
                for c in range(NC):
                    last = V.bn_aggr(mv[:, c, :], st[:, c, :])
                go(last)
                V.tensor_scalar(small[:, T0, :], mv[:, :, 1], 1e-5, None, ALU.add).then_inc(sq_rdy, 1)

            dve.sem_inc(nu_out, 2)
            dve.sem_inc(pj_out, 2)
            dve.wait_ge(ld_x, 16)
            ln_stats()
            dve.wait_ge(ld_s, 48)
            dve.wait_ge(consts, 2)
            for m in range(2):
                al = scal[:, m:m + 1]
                go(V.tensor_scalar(beta[:, m:m + 1], al, -1.0, 1.0, ALU.mult, ALU.add))
                V.memset(pw_s[:, m, 0:1], 0.0)
                go(V.tensor_tensor_scan(pw_s[:, m, 1:129], al.broadcast_to([128, 128]), ident[:, :], 0.0,
                                        ALU.mult, ALU.add))
                V.tensor_copy(maskQ[:, m, :], pw_s[:, m, 0:128])
                V.tensor_copy(rev[:, m:m + 1], pw_s[:, m, 128:129])
                V.tensor_scalar(maskL[:, m, 1, :], pw_s[:, m, 0:128], beta[:, m:m + 1], None,
                                ALU.mult).then_inc(mk_rdy, 1)
            dve.wait_ge(mk_ps, 1)
            for m in range(2):
                V.tensor_copy(maskL[:, m, 0, :], B[0][:, m * 128:(m + 1) * 128])
                V.tensor_copy(lamr[:, m, :], B[1][0:DS, 128 * (m + 1):128 * (m + 2)]).then_inc(mk_cp, 1)
                go(V.tensor_copy(lam[:, m:m + 1], B[1][:, m:m + 1]))
                V.tensor_scalar(alC[:, m:m + 1], B[1][:, 2 + m:3 + m], scal[:, m:m + 1], None, ALU.mult)
                go(V.tensor_tensor(blam[:, m:m + 1], beta[:, m:m + 1], lam[:, m:m + 1], ALU.mult))
            dve.wait_ge(ld_w, 16 * 12)
            go(V.tensor_scalar(woN[:, :], woT[:, :], normw[:, :], None, ALU.mult))
            dve.wait_ge(sq_done, 1)
            go(V.reciprocal(small[:, RSTD, :], small[:, T0, :]))
            with dve.Fori(0, NB) as b:
                for j in range(CPB):
                    c = b * CPB + j
                    dve.wait_ge(zt_free, c + 1)
                    V.tensor_scalar(zt[:, j % 2, :], row(x_tok, c), row(mv, c)[:, 0:1],
                                    small[:, RSTD, ds(c, 1)], ALU.subtract, ALU.mult).then_inc(z_rdy, 1)
                dve.wait_ge(ti_ps, b + 1)
                V.tensor_copy(vT[:, :], B[4][0:DS, :]).then_inc(vT_rdy, 1)
                for h in range(2):
                    dve.wait_ge(pj_ps, 2 * b + (h + 1))
                    V.tensor_copy(PR[:, ds(b * CPB + 2 * h, 2), 0:PJ],
                                  B[2 + h][:, 0:400].rearrange("p (j n) -> p j n", j=2)[:, :, 0:PJ]).then_inc(pj_out, 1)
                dve.wait_ge(nu_ps, b + 1)
                V.tensor_scalar(NU[:, ds(b * BT, BT)], B[4][0:DS, :], b_nm2[:, :], None, ALU.add).then_inc(nu_out, 1)
                V.tensor_copy(small[:, IMP, ds(b * CPB, CPB)], B[5][:, 0:CPB]).then_inc(nu_out, 1)
            dve.wait_ge(pj_out, 2 * NB + 2)
            dve.wait_ge(nu_out, 2 * NB + 2)
            go(V.tensor_scalar(small[:, US, :], small[:, IMP, :], scal[:, 2:3], 0.0, ALU.add, ALU.is_gt))
            for dst, o in ((RK, 0), (RQ, 2 * DS)):
                go(V.tensor_tensor(big[:, :, :], PR[:, :, pj(o)], PR[:, :, pj(o)], ALU.mult))
                go(V.tensor_reduce(small[:, dst, :], big[:, :, :], AX.X, ALU.add))
            go(V.tensor_tensor(small[:, T2, :], PR[:, :, PJ - 3], PR[:, :, PJ - 2], ALU.max))
            go(V.tensor_tensor(small[:, T2, :], small[:, T2, :], PR[:, :, PJ - 1], ALU.max))
            for n in range(3):
                last = V.tensor_tensor(small[:, P0 + n, :], PR[:, :, PJ - 3 + n], small[:, T2, :], ALU.subtract)
            last.then_inc(sq_rdy, 1)
            dve.wait_ge(sq_done, 2)
            go(V.tensor_tensor(small[:, T2, :], small[:, P0, :], small[:, P1, :], ALU.add))
            go(V.tensor_tensor(small[:, T2, :], small[:, T2, :], small[:, P2, :], ALU.add))
            go(V.reciprocal(small[:, T3, :], small[:, T2, :]))
            for n in range(3):
                V.tensor_tensor(small[:, P0 + n, :], small[:, P0 + n, :], small[:, T3, :], ALU.mult)
            for dst, o in ((RK, 0), (RQ, 2 * DS)):
                go(V.tensor_scalar(small[:, dst, :], small[:, dst, :], 1e-12, None, ALU.max))
                go(V.reciprocal(small[:, dst, :], small[:, dst, :]))
                go(V.tensor_tensor(PR[:, :, pj(o)], PR[:, :, pj(o)],
                                   small[:, dst, :].rearrange("p (c o) -> p c o", o=1).broadcast_to([128, NC, DS]), ALU.mult))
            go(V.tensor_tensor(big[:, :, :], PR[:, :, pj(0)], PR[:, :, pj(2 * DS)], ALU.mult))
            go(V.tensor_reduce(small[:, QKD, :], big[:, :, :], AX.X, ALU.add))
            go(V.memset(state[:, :, :], 0.0))
            dve.sem_inc(oT_rdy, 1)
            dve.sem_inc(f_rdy, 1)
            dve.sem_inc(pp_rdy, 1)

            def prepare(t, p, j):
                c = t * 2 + j
                pr, u = row(PR, c), small[:, US, ds(c, 1)]
                V.tensor_copy(KQ[:, p, j, 0, :], pr[:, pj(0)])
                V.tensor_copy(KQ[:, p, j, 2, :], pr[:, pj(2 * DS)])
                V.tensor_scalar(KQ[:, p, j, 1, :], pr[:, pj(0)], u, None, ALU.mult).then_inc(kq_rdy, 1)

            def right_side(t, p, j):
                c = t * 2 + j
                pr, u = row(PR, c), small[:, US, ds(c, 1)]
                dve.wait_ge(kq_rdy, c + 1)
                for m in range(2):
                    V.tensor_scalar(KR[:, p, j, m, :], KQ[:, p, j, m, :], rev[:, m:m + 1], None, ALU.mult)
                    V.tensor_scalar(X[:, p, j, m, DS:2 * DS], KQ[:, p, j, m, :], blam[:, m:m + 1], None, ALU.mult)
                V.tensor_scalar(X[:, p, j, 0, 0:DS], pr[:, pj(DS)], beta[:, 0:1], None, ALU.mult)
                V.tensor_scalar(X[:, p, j, 1, 0:DS], pr[:, pj(DS)], beta[:, 1:2], u, ALU.mult, ALU.mult).then_inc(x_rdy, 1)

            def masks(t, p, j):
                c = t * 2 + j
                dve.wait_ge(g_ps, c + 1)
                for m in range(2):
                    gm = B[4 + j][:, m * 128:(m + 1) * 128].rearrange("p (o n) -> p o n", o=1)
                    V.tensor_tensor(L[:, p, j, 0, 2 * m:2 * m + 2, :], gm.broadcast_to([128, 2, 128]),
                                    maskL[:, m, :, :], ALU.mult)
                qk = B[4 + j][:, 256:384].rearrange("p (o n) -> p o n", o=1)
                V.tensor_tensor(QM[:, p, j, :, :], qk.broadcast_to([128, 2, 128]), maskQ[:, :, :],
                                ALU.mult).then_inc(l_rdy, 1)

            def apply(t, p, n):
                for j in range(2):
                    dve.wait_ge(ap_ps, t * (2 * LEVELS) + (2 * n + j + 1))
                    if n == 0:
                        dve.wait_ge(x_rdy, t * 2 + (j + 1))
                    V.tensor_tensor(X[:, p, j, :, :], X[:, p, j, :, :],
                                    B[2 + j][:, 0:256].rearrange("p (m n) -> p m n", m=2),
                                    ALU.subtract if n == 0 else ALU.add).then_inc(ap_rdy, 1)

            def rows_w(t, p, j):
                c = t * 2 + j
                dve.wait_ge(w_ps, c + 1)
                V.tensor_tensor(row(WP, c)[:, 0:128].rearrange("p (m n) -> p m n", m=2), X[:, p, j, :, 0:DS],
                                B[6][:, 0:128].rearrange("p (m n) -> p m n", m=2), ALU.subtract).then_inc(w_rdy, 1)

            def new_state(t, j):
                c = t * 2 + j
                dve.wait_ge(pp_ps, c + 1)
                for m in range(2):
                    last = V.scalar_tensor_tensor(state[:, m, :], state[:, m, :], alC[0:DS, m:m + 1],
                                                  B[6][0:DS, 256 + m * DS:256 + (m + 1) * DS], ALU.mult, ALU.add)
                last.then_inc(f_rdy, 1)
                V.tensor_copy(row(WP, c)[:, 128:256], B[7][:, 0:128]).then_inc(pp_rdy, 1)
                dve.wait_ge(f_rdy, c + 2)

            def turn(t, p, head=True, tail=True):
                apply(t, p, 0)
                if head:
                    prepare(t + 1, 1 - p, 0)
                apply(t, p, 1)
                if tail:
                    rows_w(t - 1, 1 - p, 0)
                if head:
                    prepare(t + 1, 1 - p, 1)
                apply(t, p, 2)
                if tail:
                    new_state(t - 1, 0)
                if head:
                    right_side(t + 1, 1 - p, 0)
                apply(t, p, 3)
                if tail:
                    rows_w(t - 1, 1 - p, 1)
                apply(t, p, 4)
                if tail:
                    new_state(t - 1, 1)
                if head:
                    right_side(t + 1, 1 - p, 1)
                apply(t, p, 5)
                if head:
                    masks(t + 1, 1 - p, 0)
                    masks(t + 1, 1 - p, 1)
                apply(t, p, 6)
                dve.wait_ge(ap_rdy, (t + 1) * (2 * LEVELS))

            for j in range(2):
                prepare(0, 0, j)
            for j in range(2):
                right_side(0, 0, j)
            for j in range(2):
                masks(0, 0, j)
            turn(0, 0, tail=False)
            with dve.Fori(0, NC // 4 - 1) as h:
                turn(h * 2 + 1, 1)
                turn(h * 2 + 2, 0)
            turn(NC // 2 - 1, 1, head=False)
            for j in range(2):
                rows_w(NC // 2 - 1, 1, j)
                new_state(NC // 2 - 1, j)

            dve.wait_ge(w_rdy, NC)
            dve.wait_ge(pp_rdy, NC + 1)
            go(V.tensor_tensor(big[:, :, :], WP[:, :, 128:128 + DS], WP[:, :, 128 + DS:256], ALU.add))
            go(V.scalar_tensor_tensor(big[:, :, :], big[:, :, :], -0.5, PR[:, :, pj(DS)], ALU.mult, ALU.add))
            go(V.tensor_tensor(big[:, :, :], big[:, :, :], big[:, :, :], ALU.mult))
            go(V.tensor_reduce(small[:, UN, :], big[:, :, :], AX.X, ALU.add))
            go(V.tensor_scalar(small[:, UN, :], small[:, UN, :], 1.0 / (1.0 + 1e-6), LOGIT, ALU.mult, ALU.is_gt))
            go(V.tensor_scalar(small[:, UN, :], small[:, UN, :], 0.1, None, ALU.mult))
            for m in range(2):
                V.tensor_scalar(small[:, T0 + 2 * m, :], small[:, P0 + m, :], scal[:, m:m + 1], None, ALU.mult)
                last = V.tensor_tensor(small[:, T1 + 2 * m, :], small[:, P0 + m, :], small[:, QKD, :], ALU.mult)
            go(last)
            go(V.memset(nsC, 0.0))
            cv = lambda a: a.rearrange("p (c d) -> p c d", d=DS)

            def gate_rows(b):
                V.tensor_copy(cv(ubc), small[:, UN, ds(b * CPB, CPB)].rearrange("p (c o) -> p c o", o=1)
                              .broadcast_to([128, CPB, DS])).then_inc(ub_rdy, 1)

            def neuron(b):
                dve.wait_ge(ub_ps, b + 1)
                V.tensor_scalar(aN, B[0][0:DS, :], -1.0, 1.0, ALU.mult, ALU.add)
                go(V.tensor_tensor(bN, B[0][0:DS, :], NU[:, ds(b * BT, BT)], ALU.mult))
                V.tensor_tensor_scan(nsT, aN, bN, nsC, ALU.mult, ALU.add).then_inc(ns_rdy, 1)
                dve.wait_ge(ns_rdy, b + 1)
                go(V.tensor_copy(nsC, nsT[:, BT - 1:BT]))

            def per_token(s_, b):
                return small[:, s_, ds(b * CPB, CPB)].rearrange("p (c o) -> p c o", o=1).broadcast_to([128, CPB, DS])

            def output(b, neurons, gates):
                dve.wait_ge(nst_ps, b + 1)
                dve.wait_ge(oT_rdy, b + 1)
                go(V.tensor_tensor(cv(ot), cv(B[1][:, 0:CPB * DS]), per_token(P2, b), ALU.mult))
                if neurons:
                    neuron(b + 1)
                if gates:
                    gate_rows(b + 2)
                for s_, o in ((T0, 128), (T1, 0), (T2, 128 + DS), (T3, DS)):
                    go(V.tensor_tensor(cv(ts), WP[:, ds(b * CPB, CPB), o:o + DS], per_token(s_, b), ALU.mult))
                    go(V.tensor_tensor(ot, ot, ts, ALU.add))
                go(V.tensor_tensor(ts, ot, ot, ALU.mult))
                V.tensor_reduce(small[:, RO, ds(b * CPB, CPB)], cv(ts), AX.X, ALU.add).then_inc(o_rdy, 1)

            gate_rows(0)
            neuron(0)
            gate_rows(1)
            with dve.Fori(0, NB - 2) as b:
                go.turn(b, 12)
                output(b, True, True)
                go.end(NB - 2)
            output(NB - 2, True, False)
            output(NB - 1, False, False)
            dve.wait_ge(wo_out, NB + 1)
            dve.wait_ge(o_rdy, NB)
            V.tensor_scalar(small[:, RO, :], small[:, RO, :], 1.0 / DS, 1e-6, ALU.mult, ALU.add).then_inc(sq_rdy, 1)
            dve.wait_ge(sq_done, 3)
            go(V.reciprocal(small[:, RO, :], small[:, RO, :]))
            for c in range(NC):
                last = V.scalar_tensor_tensor(x_tok[:, c, :], WP[:, c, :], small[:, RO, c:c + 1], x_tok[:, c, :],
                                              ALU.mult, ALU.add)
            go(last)
            ln_stats()
            dve.wait_ge(sq_done, 4)
            go(V.reciprocal(small[:, RST1, :], small[:, T0, :]))
            with dve.Fori(0, NC // 4) as t:
                for j in range(4):
                    c = t * 4 + j
                    z_ = (row(x_tok, c), row(mv, c)[:, 0:1], small[:, RST1, ds(c, 1)], ALU.subtract, ALU.mult)
                    dve.wait_ge(z1_ps, c + 1)
                    V.tensor_scalar(zt[:, j % 2, :], *z_).then_inc(z1_rdy, 1)
                    V.tensor_scalar(row(WP, c), *z_)
            dve.wait_ge(lg_ps, NC)
            go(V.tensor_copy(LG[:, :, :], B[2][:, 0:NC * NE].rearrange("p (c e) -> p c e", e=NE)))
            bc = lambda a: a.rearrange("p (c o) -> p c o", o=1).broadcast_to([128, NC, NE])
            for n, (src, m_, oh) in enumerate(((LG[:, :, :], T1, 0), (rt[:, 2, :, :], T2, 1))):
                go(V.tensor_reduce(small[:, m_, :], src, AX.X, ALU.max))
                go(V.tensor_tensor(rt[:, 3, :, :], src, bc(small[:, m_, :]), ALU.is_equal))
                go(V.scalar_tensor_tensor(rt[:, 3, :, :], rt[:, 3, :, :], -64.0, iota8[:, :, :], ALU.mult, ALU.add))
                go(V.tensor_reduce(small[:, T3, :], rt[:, 3, :, :], AX.X, ALU.min))
                go(V.tensor_tensor(rt[:, oh, :, :], rt[:, 3, :, :], bc(small[:, T3, :]), ALU.is_equal))
                if n == 0:
                    go(V.scalar_tensor_tensor(rt[:, 2, :, :], rt[:, 0, :, :], -3e38, LG[:, :, :], ALU.mult, ALU.add))
            V.tensor_tensor(rt[:, 3, :, :], rt[:, 0, :, :], rt[:, 1, :, :], ALU.add).then_inc(rk_rdy, 1)
            go(V.tensor_tensor(small[:, T2, :], small[:, T2, :], small[:, T1, :], ALU.subtract))
            V.tensor_tensor(LG[:, :, :], LG[:, :, :], bc(small[:, T1, :]), ALU.subtract).then_inc(sq_rdy, 1)
            dve.wait_ge(sq_done, 5)
            go(V.tensor_reduce(small[:, T3, :], LG[:, :, :], AX.X, ALU.add))
            go(V.reciprocal(gate1[:, :], small[:, T3, :]))
            go(V.tensor_tensor(gate2[:, :], gate1[:, :], small[:, T2, :], ALU.mult))
            dve.wait_ge(rk_ps, 1)
            go(V.tensor_copy(rt[:, 4, :, :], B[1][:, 0:NC * NE].rearrange("p (c e) -> p c e", e=NE)))
            for e in range(NE):
                last = V.tensor_tensor_scan(rt[:, 2, :, e], one_m[:, 0:NC], rt[:, 4, :, e], 0.0, ALU.mult, ALU.add)
            go(last)
            go(V.tensor_copy(cnt8[:, 0, :], rt[:, 2, NC - 1, :]))
            go(V.tensor_scalar(cnt8[:, 3, :], cnt8[:, 0, :], 0.0, None, ALU.is_gt))
            for j in range(1, S // TT):
                go(V.scalar_tensor_tensor(cnt8[:, 3, :], cnt8[:, 0, :], float(TT * j), cnt8[:, 3, :], ALU.is_gt, ALU.add))
            go(V.tensor_scalar(cnt8[:, 3, :], cnt8[:, 3, :], 1.0, None, ALU.max))
            go(V.tensor_tensor_scan(cnt8[:, 2, :], one_m[:, 0:NE], cnt8[:, 3, :], 0.0, ALU.mult, ALU.add))
            go(V.tensor_tensor(base8[:, :], cnt8[:, 2, :], cnt8[:, 3, :], ALU.subtract))
            go(V.tensor_scalar(base8[:, :], base8[:, :], float(TT), None, ALU.mult))
            go(V.tensor_tensor(rt[:, 4, :, :], rt[:, 2, :, :], rt[:, 4, :, :], ALU.subtract))
            go(V.tensor_tensor(rt[:, 4, :, :], rt[:, 4, :, :], B[0][:, 0:NC * NE].rearrange("p (c e) -> p c e", e=NE), ALU.add))
            go(V.tensor_tensor(rt[:, 4, :, :], rt[:, 4, :, :],
                               base8[:, :].rearrange("p (o e) -> p o e", o=1).broadcast_to([128, NC, NE]), ALU.add))
            for oh, dst in ((0, slot1), (1, slot2)):
                go(V.tensor_tensor(rt[:, 5, :, :], rt[:, 4, :, :], rt[:, oh, :, :], ALU.mult))
                go(V.tensor_reduce(small[:, T3, :], rt[:, 5, :, :], AX.X, ALU.add))
                go(V.tensor_copy(dst[:, :], small[:, T3, :]))
            V.memset(tiles0[:, 0:1], 0)
            V.tensor_copy(tiles0[0:1, 1:NE + 1], cnt8[0:1, 2, :])

        @block.scalar
        def _(act):
            A_ = nc.scalar
            act.sem_inc(wo_out, 1)
            act.wait_ge(sq_rdy, 1)
            A_.activation(small[:, T0, :], small[:, T0, :], ACT.Sqrt).then_inc(sq_done, 1)
            act.wait_ge(ld_w, 16 * 12)
            with act.Fori(0, NB) as b:
                act.wait_ge(zt_free, b * CPB + (CPB + 2))
                for k in range(KT):
                    A_.activation(zT[:, k, :], B[k][:, :], ACT.Copy).then_inc(zT_rdy, 1)
                act.wait_ge(ti_ps, b + 1)
                A_.activation(gT[:, :], B[5][0:DS, :], ACT.Gelu, bias=b_ir1[:, :]).then_inc(gT_rdy, 1)
                act.wait_ge(hd_ps, b + 1)
                A_.activation(hT[:, :], B[6][:, :], ACT.Gelu, bias=b_nm1[:, :]).then_inc(hd_rdy, 1)
            act.wait_ge(sq_rdy, 2)
            A_.activation(small[:, RK, :], small[:, RK, :], ACT.Sqrt)
            A_.activation(small[:, RQ, :], small[:, RQ, :], ACT.Sqrt)
            A_.activation(small[:, P0:P0 + 3, :], small[:, P0:P0 + 3, :], ACT.Exp).then_inc(sq_done, 1)
            def transposed(t, p, j):
                act.wait_ge(kqt_ps, t * 2 + (j + 1))
                A_.activation(KQT[:, p, j, 0:3, :], B[4 + j][0:DS, 0:384].rearrange("p (a n) -> p a n", a=3),
                              ACT.Copy).then_inc(kqt_rdy, 1)

            def square(t, p, n):
                for j in range(2):
                    act.wait_ge(sq_ps, t * (2 * LEVELS - 2) + (2 * n + j + 1))
                    src = B[j][:, :].rearrange("p (a n) -> p a n", a=4)
                    if n < LEVELS - 2:
                        A_.activation(L[:, p, j, (n + 1) % 2, :, :], src, ACT.Copy).then_inc(sq_cp, 1)
                    else:
                        A_.activation(L[:, p, j, (n + 1) % 2, 1::2, :], src[:, 1::2, :], ACT.Copy).then_inc(sq_cp, 1)

            def yt(t):
                act.wait_ge(yt_ps, t + 1)
                A_.activation(YT[:, :, :, :], B[7][0:DS, :].rearrange("p (j m n) -> p j m n", j=2, m=2),
                              ACT.Copy).then_inc(yt_rdy, 1)

            def turn(t, p, head=True, tail=True):
                square(t, p, 0)
                if tail:
                    yt(t - 1)
                for n in range(1, LEVELS - 1):
                    square(t, p, n)
                    if n in (2, 4) and head:
                        transposed(t + 1, 1 - p, n // 2 - 1)

            for j in range(2):
                transposed(0, 0, j)
            turn(0, 0, tail=False)
            with act.Fori(0, NC // 4 - 1) as h:
                turn(h * 2 + 1, 1)
                turn(h * 2 + 2, 0)
            turn(NC // 2 - 1, 1, head=False)
            yt(NC // 2 - 1)
            with act.Fori(0, NB) as b:
                act.wait_ge(ot_ps, b + 1)
                A_.activation(oT, B[2][0:DS, :], ACT.Copy).then_inc(oT_rdy, 1)
                act.wait_ge(wo_ps, b + 1)
                for h in range(2):
                    last = A_.activation(WP[:, ds(b * CPB + 2 * h, 2), :], B[3 + h][:, :].rearrange("p (c d) -> p c d", c=2),
                                         ACT.Copy)
                last.then_inc(wo_out, 1)
            for n in (3, 4):
                act.wait_ge(sq_rdy, n)
                s_ = RO if n == 3 else T0
                A_.activation(small[:, s_, :], small[:, s_, :], ACT.Sqrt).then_inc(sq_done, 1)
            with act.Fori(0, NC // 4) as t:
                for j in range(4):
                    act.wait_ge(z1_ps, t * 4 + (j + 3))
                    A_.activation(z1T[:, j % 2, :, :], B[j % 2][:, 0:256].rearrange("p (k n) -> p k n", k=2),
                                  ACT.Copy).then_inc(z1T_rdy, 1)
            act.wait_ge(sq_rdy, 5)
            A_.activation(small[:, T2, :], small[:, T2, :], ACT.Exp)
            A_.activation(LG[:, :, :], LG[:, :, :], ACT.Exp).then_inc(sq_done, 1)

        @block.tensor
        def _(pe):
            T = nc.tensor
            I_ = ident[:, :]
            pe.sem_inc(zt_free, 2)
            pe.wait_ge(mk_rdy, 2)
            for m in range(2):
                T.transpose(B[0][:, m * 128:(m + 1) * 128], maskL[:, m, 1, :], I_)
                T.matmul(B[1][:, m:m + 1], pw_s[0:1, m, 1:129], one_m[0:1, 0:1], start=True, stop=True)
                T.matmul(B[1][0:DS, 128 * (m + 1):128 * (m + 2)], one_m[0:1, 0:DS], pw_s[0:1, m, 1:129], start=True, stop=True)
                last = T.matmul(B[1][:, 2 + m:3 + m], one_m[0:1, :], pw_s[0:1, m, 128:129], start=True, stop=True)
            last.then_inc(mk_ps, 1)
            pe.wait_ge(ld_w, 16 * 12)
            with pe.Fori(0, NB) as b:
                for j in range(CPB):
                    pe.wait_ge(z_rdy, b * CPB + (j + 1))
                    for k in range(KT):
                        last = T.transpose(B[k][:, j * CH:(j + 1) * CH], zt[:, j % 2, k * 128:(k + 1) * 128], I_)
                    last.then_inc(zt_free, 1)
                pe.wait_ge(zT_rdy, b * 2 + 2)
                pe.wait_ge(nu_out, b * 2 + 2)
                for w, o in ((wvT, 4), (ir1T, 5)):
                    for k in range(KT):
                        last = T.matmul(B[o][0:DS, :], w[:, k, :], zT[:, k, :], start=(k == 0), stop=(k == KT - 1))
                last.then_inc(ti_ps, 1)
                for h in range(2):
                    pe.wait_ge(pj_out, b * 2 + (h + 1))
                    for jj in range(2):
                        j = 2 * h + jj
                        for k in range(KT):
                            last = T.matmul(B[2 + h][:, jj * 200:jj * 200 + PJ], zT[:, k, j * CH:(j + 1) * CH],
                                            wcat[:, k, :], start=(k == 0), stop=(k == KT - 1))
                    last.then_inc(pj_ps, 1)
                pe.wait_ge(vT_rdy, b + 1)
                T.matmul(B[6][:, :], nm1T[:, :], vT[:, :], start=True, stop=True).then_inc(hd_ps, 1)
                pe.wait_ge(gT_rdy, b + 1)
                for j in range(CPB):
                    T.matmul(B[5][:, j:j + 1], gT[:, j * CH:(j + 1) * CH], ir2T[:, :], start=True, stop=True)
                pe.wait_ge(hd_rdy, b + 1)
                T.matmul(B[4][0:DS, :], nm2T[:, :], hT[:, :], start=True, stop=True).then_inc(nu_ps, 1)
            def transposes(t, p, j):
                pe.wait_ge(kq_rdy, t * 2 + (j + 1))
                pe.wait_ge(l_rdy, t * 2 + (j + 1))
                for a in range(3):
                    last = T.matmul(B[4 + j][0:DS, a * 128:(a + 1) * 128], KQ[:, p, j, a, :], I_, start=True, stop=True)
                last.then_inc(kqt_ps, 1)

            def grams(t, p, j):
                pe.wait_ge(kqt_rdy, t * 2 + (j + 1))
                for n, (a, b_) in enumerate(((0, 0), (1, 1), (0, 2))):
                    last = T.matmul(B[4 + j][:, n * 128:(n + 1) * 128], KQT[:, p, j, a, :], KQT[:, p, j, b_, :],
                                    start=True, stop=True)
                last.then_inc(g_ps, 1)

            def level(t, p, n, first):
                for j in range(2):
                    if n == 0:
                        pe.wait_ge(l_rdy, t * 2 + (j + 3))
                        pe.wait_ge(x_rdy, t * 2 + (j + 1))
                    else:
                        pe.wait_ge(sq_cp, t * (2 * LEVELS - 2) + (2 * (n - 1) + j + 1))
                    Ln = L[:, p, j, n % 2, :, :]
                    if n < LEVELS - 1:
                        for m in range(2):
                            a, b_ = Ln[:, 2 * m, :], Ln[:, 2 * m + 1, :]
                            if n < LEVELS - 2:
                                T.matmul(B[j][:, 256 * m:256 * m + 128], b_, a, start=True, stop=True)
                            last = T.matmul(B[j][:, 256 * m + 128:256 * m + 256], a, b_, start=True, stop=True)
                        last.then_inc(sq_ps, 1)
                    if n > 0:
                        pe.wait_ge(ap_rdy, t * (2 * LEVELS) + (2 * (n - 1) + j + 1))
                    elif not first:
                        pe.wait_ge(ap_rdy, t * (2 * LEVELS))
                    for m in range(2):
                        last = T.matmul(B[2 + j][:, m * 128:(m + 1) * 128], Ln[:, 2 * m + 1, :], X[:, p, j, m, :],
                                        start=True, stop=True)
                    last.then_inc(ap_ps, 1)

            def y_transposes(t, p):
                pe.wait_ge(ap_rdy, (t + 1) * (2 * LEVELS))
                pe.wait_ge(pp_rdy, t * 2 + 1)
                for j in range(2):
                    for m in range(2):
                        last = T.matmul(B[7][0:DS, (2 * j + m) * 128:(2 * j + m + 1) * 128], X[:, p, j, m, DS:2 * DS], I_,
                                        start=True, stop=True)
                last.then_inc(yt_ps, 1)

            def y_state(t, j):
                c = t * 2 + j
                pe.wait_ge(yt_rdy, t + 1)
                pe.wait_ge(f_rdy, c + 1)
                for m in range(2):
                    last = T.matmul(B[6][:, m * DS:(m + 1) * DS], YT[:, j, m, :], state[:, m, :], start=True, stop=True)
                last.then_inc(w_ps, 1)

            def predict(t, p, j):
                c = t * 2 + j
                pe.wait_ge(pp_rdy, c + 1)
                pe.wait_ge(lq_rdy, c + 1)
                for m in range(2):
                    T.matmul(B[7][:, m * DS:(m + 1) * DS], KQT[:, p, j, 3 + m, :], state[:, m, :],
                             start=True, stop=False)
                    if m == 0:
                        pe.wait_ge(w_rdy, c + 1)
                    w = WP[:, ds(c, 1), m * DS:(m + 1) * DS].rearrange("p o d -> p (o d)")
                    T.matmul(B[7][:, m * DS:(m + 1) * DS], QM[:, p, j, m, :], w, start=False, stop=True)
                    last = T.matmul(B[6][0:DS, 256 + m * DS:256 + (m + 1) * DS], KR[:, p, j, m, :], w,
                                    start=True, stop=True)
                last.then_inc(pp_ps, 1)

            def turn(t, p, head=True, tail=True):
                for n in range(LEVELS):
                    level(t, p, n, not tail)
                    if tail:
                        if n == 0:
                            y_transposes(t - 1, 1 - p)
                        elif n == 1:
                            y_state(t - 1, 0)
                        elif n == 2:
                            predict(t - 1, 1 - p, 0)
                        elif n == 3:
                            y_state(t - 1, 1)
                        elif n == 4:
                            predict(t - 1, 1 - p, 1)
                    if head:
                        if n in (2, 4):
                            transposes(t + 1, 1 - p, n // 2 - 1)
                        if n in (4, 5):
                            grams(t + 1, 1 - p, n - 4)

            pe.sem_inc(l_rdy, 2)
            for j in range(2):
                transposes(0, 0, j)
            for j in range(2):
                grams(0, 0, j)
            turn(0, 0, tail=False)
            with pe.Fori(0, NC // 4 - 1) as h:
                turn(h * 2 + 1, 1)
                turn(h * 2 + 2, 0)
            turn(NC // 2 - 1, 1, head=False)
            y_transposes(NC // 2 - 1, 1)
            for j in range(2):
                y_state(NC // 2 - 1, j)
                predict(NC // 2 - 1, 1, j)

            def gate_columns(b):
                pe.wait_ge(ub_rdy, b + 1)
                for j in range(CPB):
                    last = T.matmul(B[0][0:DS, j * CH:(j + 1) * CH], ubc[:, j * DS:(j + 1) * DS], I_, start=True, stop=True)
                last.then_inc(ub_ps, 1)

            def neuron_back(b):
                pe.wait_ge(ns_rdy, b + 1)
                for j in range(CPB):
                    last = T.matmul(B[1][:, j * DS:(j + 1) * DS], nsT[:, j * CH:(j + 1) * CH], ident[0:DS, 0:DS],
                                    start=True, stop=True)
                last.then_inc(nst_ps, 1)

            def output(b):
                pe.wait_ge(o_rdy, b + 1)
                for j in range(CPB):
                    last = T.matmul(B[2][0:DS, j * CH:(j + 1) * CH], ot[:, j * DS:(j + 1) * DS], I_, start=True, stop=True)
                last.then_inc(ot_ps, 1)
                pe.wait_ge(oT_rdy, b + 2)
                pe.wait_ge(wo_out, b + 1)
                for j in range(CPB):
                    last = T.matmul(B[3 + j // 2][:, (j % 2) * D:(j % 2 + 1) * D], oT[:, j * CH:(j + 1) * CH], woN[:, :],
                                    start=True, stop=True)
                last.then_inc(wo_ps, 1)

            gate_columns(0)
            neuron_back(0)
            gate_columns(1)
            with pe.Fori(0, NB - 2) as b:
                neuron_back(b + 1)
                gate_columns(b + 2)
                output(b)
            neuron_back(NB - 1)
            output(NB - 2)
            output(NB - 1)
            def z1_columns(c, j):
                pe.wait_ge(z1_rdy, c + 1)
                for k in range(KT):
                    last = T.transpose(B[j % 2][:, k * 128:(k + 1) * 128], zt[:, j % 2, k * 128:(k + 1) * 128], I_)
                last.then_inc(z1_ps, 1)

            def logits(c, j):
                pe.wait_ge(z1T_rdy, c + 1)
                for k in range(KT):
                    last = T.matmul(B[2][:, ds(c * NE, NE)], z1T[:, j % 2, k, :], wroT[:, k, :], start=(k == 0), stop=(k == KT - 1))
                last.then_inc(lg_ps, 1)

            pe.sem_inc(z1_ps, 2)
            z1_columns(0, 0)
            with pe.Fori(0, NC // 4 - 1) as t:
                for j in range(4):
                    z1_columns(t * 4 + (j + 1), j + 1)
                    logits(t * 4 + j, j)
            for j in range(4):
                if j < 3:
                    z1_columns(NC - 3 + j, j + 1)
                logits(NC - 4 + j, j)
            pe.wait_ge(rk_rdy, 1)
            T.matmul(B[0][:, 0:NC * NE], tri[:, :], rt[:, 3, :, :].rearrange("p c e -> p (c e)"), start=True, stop=True)
            T.matmul(B[1][:, 0:NC * NE], one_m[:, :], rt[:, 3, :, :].rearrange("p c e -> p (c e)"),
                     start=True, stop=True).then_inc(rk_ps, 1)

        pblk.close()
        pa.close()
        pb = ctx.enter_context(ExitStack())
        KH = HID // 128
        w1_d = A["w1"].rearrange("e (k p) n -> e p k n", p=128)
        w2_d = A["w2"].rearrange("e (k p) n -> e p k n", p=128)
        st1 = sb("st1", [128, KT, HID], to=pb)
        st2 = sb("st2", [128, KH, D], to=pb)
        w1s = [[sb(f"w1_{q}{h}", [128, KT, HID], f32r, to=pb) for h in "hl"] for q in range(2)]
        w2s = [[sb(f"w2_{q}{h}", [128, KH, D], f32r, to=pb) for h in "hl"] for q in range(2)]
        b1s = sb("b1s", [128, NE * KH], to=pb)
        b2s = sb("b2s", [128, NE, D], to=pb)
        xg = sb("xg", [128, 2, D], to=pb)
        xT = [sb(f"xT{h}", [128, KT, TT], f32r, to=pb) for h in "hl"]
        h32 = sb("h32", [128, KH, TT], to=pb)
        hs = [sb(f"hs{h}", [128, KH, TT], f32r, to=pb) for h in "hl"]
        yt = sb("yt", [128, 2, D], to=pb)

        ew_ld, ew_free, ew_rdy, ex_done = (sem("expert_weights_loaded"), sem("expert_stage_free"),
                                           sem("expert_weights_split"), sem("expert_done"))
        eb_ld, xg_ld, xg_free, xt_ps, xT_rdy = (sem("expert_biases_loaded"), sem("rows_loaded"), sem("rows_free"),
                                                sem("rows_T_in_psum"), sem("rows_T_split"))
        up_ps, h_act, h_rdy, dn_ps, y_rdy, y_out = (sem("up_in_psum"), sem("gelu_done"), sem("h_split"),
                                                    sem("down_in_psum"), sem("y_ready"), sem("y_stored"))
        p_st2, x_st, h_st = sem("weights_hi_done"), sem("rows_hi_done"), sem("h_hi_done")

        def mm3(out, a, b, first, last):
            nc.tensor.matmul(out, a[0], b[0], start=first, stop=False)
            nc.tensor.matmul(out, a[0], b[1], start=False, stop=False)
            return nc.tensor.matmul(out, a[1], b[0], start=False, stop=last)

        def expert_tiles(eng, before, body, after):
            with eng.Fori(0, NE // 2) as p:
                for q in range(2):
                    e = p * 2 + q
                    t0 = eng.value_load(tiles0[0:1, ds(e, 1)], min_val=0, max_val=MT)
                    t1 = eng.value_load(tiles0[0:1, ds(e + 1, 1)], min_val=1, max_val=MT)
                    before(e, q)
                    with eng.Fori(t0, t1) as t:
                        body(e, q, t)
                    after(e, q)

        nop = lambda *a: None
        pblk = ctx.enter_context(ExitStack())
        block = pblk.enter_context(nc.Block())

        @block.sync
        def _(sp):
            sp.dma_start(b1s[:, :], A["b1T"]).then_inc(eb_ld, 16)
            for e in range(NE):
                sp.dma_start(b2s[:, e, :], A["b2"][e:e + 1, :].broadcast_to([128, D])).then_inc(eb_ld, 16)

            def weights(e):
                sp.wait_ge(ew_free, e + 1)
                sp.dma_start(st1[:, :, :], w1_d[ds(e, 1)].rearrange("o p k n -> p (o k) n")).then_inc(ew_ld, 16)
                sp.dma_start(st2[:, :, :], w2_d[ds(e, 1)].rearrange("o p k n -> p (o k) n")).then_inc(ew_ld, 16)

            def rows(e, q, t):
                sp.wait_ge(xg_free, t + 1)
                sp.wait_ge(scat, 16 * 2 * NC)
                sp.dma_start(xg[:, :, :], z1_d[ds(t * TT, TT), :].rearrange("(j p) d -> p j d", p=128))\
                  .then_inc(xg_ld, 16)

            expert_tiles(sp, lambda e, q: weights(e), rows, nop)
            total = sp.value_load(tiles0[0:1, NE:NE + 1], min_val=NE, max_val=MT)
            sp.wait_ge(xg_free, total + 1)
            sp.dma_start(xg[:, :, :], z1_d[0:TT, :].rearrange("(j p) d -> p j d", p=128)).then_inc(xg_ld, 16)
        @block.gpsimd
        def _(pool):
            go = Steps(pool, p_st2)
            pool.wait_ge(zf, 16 * 2 * ZF)
            for c in range(NC):
                for s_ in (slot1, slot2):
                    pool.indirect_dma_start(z1_d, bass.IndirectOffsetOnAxis(s_[:, c:c + 1].bitcast(u32), 0),
                                            WP[:, c, :], None).then_inc(scat, 16)

            def split(e, q):
                pool.wait_ge(ew_ld, e * 32 + 32)
                pool.wait_ge(ex_done, e + 1)
                for st_, w in ((st1, w1s[q]), (st2, w2s[q])):
                    nc.gpsimd.tensor_copy(w[0][:, :, :], st_[:, :, :]).then_inc(p_st2, 1)
                pool.wait_ge(p_st2, (e - 1) * 2 + 2)
                nc.gpsimd.tensor_tensor(w1s[q][1][:, :, :], st1[:, :, :], f32(w1s[q][0][:, :, :]), ALU.subtract)
                nc.gpsimd.tensor_tensor(w2s[q][1][:, :, :], st2[:, :, :], f32(w2s[q][0][:, :, :]),
                                        ALU.subtract).then_inc(ew_rdy, 1)
                pool.wait_ge(ew_rdy, e + 1)
                pool.sem_inc(ew_free, 1)

            for e in range(1, NE):
                split(e, e % 2)

        @block.tensor
        def _(pe):
            T = nc.tensor
            pe.sem_inc(xg_free, 1)
            pe.sem_inc(ex_done, 2)

            def rows_T(n):
                pe.wait_ge(xg_ld, n * 16 + 16)
                for k in range(KT):
                    for j in range(2):
                        last = T.transpose(B[4][:, k * TT + j * 128:k * TT + (j + 1) * 128],
                                           xg[:, j, k * 128:(k + 1) * 128], ident[:, :])
                last.then_inc(xt_ps, 1)
                pe.wait_ge(xt_ps, n + 1)
                pe.sem_inc(xg_free, 1)

            def tile(e, q, t):
                pe.wait_ge(ew_rdy, e + 1)
                pe.wait_ge(xT_rdy, t + 1)
                for m in range(KH):
                    pe.wait_ge(h_act, t * KH + (m + 1))
                    for k in range(KT):
                        ms = slice(m * 128, (m + 1) * 128)
                        last = mm3(B[m % 4][:, 0:TT], [w[:, k, ms] for w in w1s[q]], [x[:, k, :] for x in xT],
                                   k == 0, k == KT - 1)
                    last.then_inc(up_ps, 1)
                rows_T(t + 1)
                pe.wait_ge(y_rdy, t * 2 + 2)
                for k in range(KH):
                    if k % 2 == 0:
                        pe.wait_ge(h_rdy, t * 4 + (k // 2 + 1 + 4))
                    for j in range(2):
                        js = slice(j * 128, (j + 1) * 128)
                        last = mm3(B[5 + j][:, 0:D], [h[:, k, js] for h in hs], [w[:, k, :] for w in w2s[q]],
                                   k == 0, k == KH - 1)
                        if k == KH - 1:
                            last.then_inc(dn_ps, 1)

            rows_T(0)
            expert_tiles(pe, nop, tile,
                         lambda e, q: pe.drain().then_inc(ex_done, 1))

        @block.scalar
        def _(act):
            act.sem_inc(h_act, 4)
            act.wait_ge(eb_ld, 16 * (NE + 1))

            def tile(e, q, t):
                for m in range(KH):
                    act.wait_ge(up_ps, t * KH + (m + 1))
                    if m % 2 == 0:
                        act.wait_ge(h_rdy, t * 4 + (m // 2 + 1))
                    nc.scalar.activation(h32[:, m, :], B[m % 4][:, 0:TT], ACT.Gelu_apprx_tanh,
                                         bias=b1s[:, ds(e * KH + m, 1)]).then_inc(h_act, 1)
                act.wait_ge(y_rdy, t * 2 + 4)
                act.dma_start(ym_d[ds(t * TT, TT), :].rearrange("(j p) d -> p j d", p=128),
                              yt[:, :, :]).then_inc(y_out, 16)

            expert_tiles(act, nop, tile, nop)
            total = act.value_load(tiles0[0:1, NE:NE + 1], min_val=NE, max_val=MT)
            act.wait_ge(y_out, total * 16 + 16)
            nc.scalar.activation(sc8[:, 0:1], ident[:, 0:1], ACT.Copy)

        @block.vector
        def _(dve):
            V = nc.vector
            dve.sem_inc(h_rdy, 4)
            dve.sem_inc(y_rdy, 2)
            dve.sem_inc(y_out, 16)
            dve.sem_inc(ew_free, 1)
            go = steps.on(dve)
            for e in range(1):
                dve.wait_ge(ew_ld, e * 32 + 32)
                for st_, w in ((st1, w1s[e]), (st2, w2s[e])):
                    go(V.tensor_copy(w[0][:, :, :], st_[:, :, :]))
                V.tensor_tensor(w1s[e][1][:, :, :], st1[:, :, :], f32(w1s[e][0][:, :, :]), ALU.subtract)
                V.tensor_tensor(w2s[e][1][:, :, :], st2[:, :, :], f32(w2s[e][0][:, :, :]), ALU.subtract).then_inc(ew_rdy, 1)
                dve.wait_ge(ew_rdy, e + 1)
                dve.sem_inc(ew_free, 1)
            dve.wait_ge(eb_ld, 16 * (NE + 1))

            def rows_split(n):
                dve.wait_ge(xt_ps, n + 1)
                src = B[4][:, :].rearrange("p (k n) -> p k n", k=KT)
                V.tensor_copy(xT[0][:, :, :], src).then_inc(x_st, 1)
                dve.wait_ge(x_st, n + 1)
                V.tensor_tensor(xT[1][:, :, :], src, f32(xT[0][:, :, :]), ALU.subtract).then_inc(xT_rdy, 1)

            def tile(e, q, t):
                for m in range(0, KH, 2):
                    dve.wait_ge(h_act, t * KH + (m + 2 + 4))
                    V.tensor_copy(hs[0][:, m:m + 2, :], h32[:, m:m + 2, :]).then_inc(h_st, 1)
                    dve.wait_ge(h_st, t * 4 + (m // 2 + 1))
                    V.tensor_tensor(hs[1][:, m:m + 2, :], h32[:, m:m + 2, :], f32(hs[0][:, m:m + 2, :]),
                                    ALU.subtract).then_inc(h_rdy, 1)
                rows_split(t + 1)
                dve.wait_ge(y_out, t * 16 + 16)
                for j in range(2):
                    dve.wait_ge(dn_ps, t * 2 + (j + 1))
                    V.tensor_tensor(yt[:, j, :], B[5 + j][:, 0:D], b2s[:, ds(e, 1), :].rearrange("p o d -> p (o d)"),
                                    ALU.add).then_inc(y_rdy, 1)

            rows_split(0)
            expert_tiles(dve, nop, tile, nop)

        pblk.close()
        pb.close()
        pz.close()
        KH = HID // 128
        pw_ = ctx.enter_context(ExitStack())
        wcm = [sb(f"wcm{h}", [128, KT, HID], f32r, to=pw_) for h in "hl"]
        wcp = [sb(f"wcp{h}", [128, KH, D], f32r, to=pw_) for h in "hl"]
        pc = ctx.enter_context(ExitStack())
        cst = sb("cst", [128, KT * HID], to=pc)
        NG = 4
        g1 = sb("g1", [128, NG, D], to=pc)
        g2 = sb("g2", [128, NG, D], to=pc)
        x2_rdy, c_st = sem("x2_ready"), sem("first_copy_added")
        g_ld = [sem(f"gathered_{i}") for i in range(NG)]
        cw_ld, cw_hi, cw_rdy = (sem("channel_weights_loaded"), sem("channel_weights_high"), sem("channel_weights_split"))
        xa_d = nc.dram_tensor("after_time_mix", (D, S), fp32, kind="Internal").ap()
        sx_d = nc.dram_tensor("residual_sum", (D, S), fp32, kind="Internal").ap()
        x3_d = nc.dram_tensor("x3_T", (D, S), fp32, kind="Internal").ap()
        byk = lambda a: a.rearrange("(k p) n -> p k n", p=128)
        st3 = sb("st3", [128, NC, 6], to=pc)
        mv3 = sb("mv3", [128, NC, 2], to=pc)
        wst = sb("wst", [128, KT, 3 * D], to=pc)
        wtm = [sb(f"wtm{h}", [128, KT, 3 * D], f32r, to=pc) for h in "hl"]
        tk = sb("tk", [128, 2, 3, D], to=pc)
        x2T = sb("x2T", [128, 2, KT, BT], to=pc)
        Z2 = sb("Z2", [128, 2, KT, BT + 1], to=pc)
        a3 = sb("a3", [128, KT, BT], to=pc)
        a3s = [sb(f"a3{h}", [128, KT, BT], f32r, to=pc) for h in "hl"]
        mixed = sb("mixed", [128, 2, 3, KT, BT], to=pc)
        stt_ = sb("wkv_state", [128, 4, KT, BT + 1], to=pc)
        tmp = sb("wkv_tmp", [128, 4, KT, BT], to=pc)
        pq = sb("wkv_pq", [128, KT, BT], to=pc)
        den = sb("wkv_den", [128, KT, BT], to=pc)

        v_ld, wt_ld, tk_rdy, tk_free = (sem("vectors_loaded"), sem("w_tm_loaded"),
                                               sem("tokens_ready"), sem("token_buffers_free"))
        zt_rdy, a3_rdy, km_ps, ex_w, ex_d, xa_rdy, xa_out = (
            sem("block_T_ready"), sem("a3_split"), sem("kvr_in_psum"), sem("exponents_ready"), sem("exps_done"),
            sem("xa_ready"), sem("xa_stored"))
        sg_d, tx_rdy, pv2_rdy, dn_w, dn_d = (sem("r_gate_done"), sem("tokens_x_ready"), sem("previous_parts_ready"),
                                             sem("denominators_ready"), sem("reciprocals_done"))
        dn_l = sem("denominator_logs")
        wts_rdy, z0_ps, km_out = sem("w_tm_split"), sem("first_token_T"), sem("kvr_taken")
        SQ = 5
        pblk = ctx.enter_context(ExitStack())
        block = pblk.enter_context(nc.Block())
        MX, SM, LS, AV = range(4)

        @block.sync
        def _(sp):
            for n, v in enumerate(("time_decay", "time_first", "tmk", "tmv", "tmr", "g1", "b1v", "g2", "b2v", "cmk", "cmr")):
                sp.dma_start(vec[:, n, :], A[v]).then_inc(v_ld, 16)
            sp.dma_start(wst[:, :, :], byk(A["W_tm"])).then_inc(wt_ld, 16)
            with sp.Fori(0, NB) as b:
                sp.wait_ge(xa_rdy, b + 1)
                sp.dma_start(byk(xa_d)[:, :, ds(b * BT, BT)], tmp[:, 2, :, :]).then_inc(xa_out, 16)
                sp.dma_start(byk(sx_d)[:, :, ds(b * BT, BT)], tmp[:, 3, :, :]).then_inc(xa_out, 16)
            sp.wait_ge(xa_out, 32 * NB + 32)
        @block.gpsimd
        def _(pool):
            P = nc.gpsimd

            def gather(c):
                for s_, g in ((slot1, g1), (slot2, g2)):
                    pool.indirect_dma_start(g[:, c % NG, :], None, ym_d,
                                            bass.IndirectOffsetOnAxis(s_[:, c:c + 1].bitcast(u32), 0)).then_inc(g_ld[c % NG], 16)

            def scaled(g, gate, c):
                P.tensor_tensor(g[:, c % NG, :], g[:, c % NG, :], gate[:, c:c + 1].broadcast_to([128, D]),
                                ALU.mult).then_inc(c_st, 1)

            for c in range(NG):
                gather(c)
            pool.dma_start(cst[:, :].rearrange("p (k n) -> p k n", k=KT), byk(A["W_cm"])).then_inc(cw_ld, 16)
            for c in range(NC):
                pool.wait_ge(g_ld[c % NG], 32 * (c // NG + 1))
                scaled(g1, gate1, c)
                scaled(g2, gate2, c)
                pool.wait_ge(c_st, 3 * c + 2)
                P.tensor_tensor(g1[:, c % NG, :], g1[:, c % NG, :], g2[:, c % NG, :], ALU.add).then_inc(c_st, 1)
                pool.wait_ge(c_st, 3 * c + 3)
                P.tensor_tensor(x_tok[:, c, :], x_tok[:, c, :], g1[:, c % NG, :], ALU.add).then_inc(x2_rdy, 1)
                pool.wait_ge(x2_rdy, c + 1)
                if c + NG < NC:
                    gather(c + NG)
            for n, w in enumerate((wcm, wcp)):
                pool.wait_ge(cw_ld, 16 * (n + 1))
                flat = [a[:, :, :].rearrange("p k n -> p (k n)") for a in w]
                P.tensor_copy(flat[0], cst[:, :]).then_inc(cw_hi, 1)
                pool.wait_ge(cw_hi, n + 1)
                P.tensor_tensor(flat[1], cst[:, :], f32(flat[0]), ALU.subtract).then_inc(cw_rdy, 1)
                pool.wait_ge(cw_rdy, n + 1)
                if n == 0:
                    pool.dma_start(cst[:, :].rearrange("p (k n) -> p k n", k=KH),
                                   A["W_cp"].rearrange("(k p) n -> p k n", p=128)).then_inc(cw_ld, 16)

        @block.vector
        def _(dve):
            V = nc.vector
            go = steps.on(dve)
            dve.wait_ge(v_ld, 16 * 11)
            for q_, s_ in ((QMK, TMK), (QMV, TMV), (QMR, TMR), (QCK, CMK), (QCR, CMR)):
                V.tensor_scalar(vec[:, q_, :], vec[:, s_, :], -1.0, 1.0, ALU.mult, ALU.add)
            V.memset(epsv[:, 0:1], 1e-8)
            V.memset(epsv[:, 1:2], 1e-5)
            for n, v in ((MX, -1e38), (SM, 1.0), (LS, -1e38), (AV, 0.0)):
                V.memset(stt_[:, n, :, BT:BT + 1], v)
            dve.wait_ge(wt_ld, 16)
            go(V.tensor_copy(wtm[0][:, :, :], wst[:, :, :]))
            V.tensor_tensor(wtm[1][:, :, :], wst[:, :, :], f32(wtm[0][:, :, :]), ALU.subtract).then_inc(wts_rdy, 1)
            batches = (0, CPB, 2 * CPB, NC // 2, NC)

            def statistics(n):
                c0, c1 = batches[n], batches[n + 1]
                cs = slice(c0, c1)
                for c in range(c0, c1):
                    dve.wait_ge(x2_rdy, c + 1)
                    last = V.bn_stats(st3[:, c, :], x_tok[:, c, :])
                go(last)
                for c in range(c0, c1):
                    last = V.bn_aggr(mv3[:, c, :], st3[:, c, :])
                go(last)
                V.tensor_scalar(small[:, 0, cs], mv3[:, cs, 1], 1e-5, None, ALU.add).then_inc(sq_rdy, 1)
                dve.wait_ge(sq_done, SQ + 2 * n + 1)
                go(V.reciprocal(small[:, 1, cs], small[:, 0, cs]))
                go(V.tensor_tensor(small[:, 2, cs], small[:, 1, cs], small[:, 1, cs], ALU.mult))
                go(V.tensor_tensor(small[:, 2, cs], small[:, 2, cs], mv3[:, cs, 1], ALU.mult))
                V.tensor_scalar(small[:, 2, cs], small[:, 2, cs], 1e-5, None, ALU.add).then_inc(sq_rdy, 1)
                dve.wait_ge(sq_done, SQ + 2 * n + 2)
                go(V.reciprocal(small[:, 3, cs], small[:, 2, cs]))
                go(V.tensor_tensor(small[:, 3, cs], small[:, 3, cs], small[:, 1, cs], ALU.mult))

            statistics(0)
            V.tensor_scalar(tk[:, 0, 1, :], x_tok[:, 0, :], mv3[:, 0, 0:1], small[:, 1, 0:1],
                            ALU.subtract, ALU.mult).then_inc(tk_rdy, 1)
            prev, now = lambda n: stt_[:, n, :, 0:BT], lambda n: stt_[:, n, :, 1:BT + 1]
            T_ = [tmp[:, n, :, :] for n in range(4)]
            DN = den[:, :, :]

            def tokens(b):
                for j in range(CPB):
                    c = b * CPB + j
                    x_, m_ = x_tok[:, ds(c, 1), :].rearrange("p o d -> p (o d)"), mv3[:, ds(c, 1), 0:1].rearrange("p o s -> p (o s)")
                    dve.wait_ge(tk_free, c + 1)
                    V.tensor_scalar(tk[:, j % 2, 1, :], x_, m_, small[:, 1, ds(c, 1)], ALU.subtract, ALU.mult)
                    V.tensor_scalar(tk[:, j % 2, 2, :], x_, m_, small[:, 3, ds(c, 1)], ALU.subtract,
                                    ALU.mult).then_inc(tk_rdy, 1)

            def split(b, p):
                dve.wait_ge(zt_rdy, b + 1)
                go(V.tensor_copy(a3s[0][:, :, :], a3[:, :, :]))
                V.tensor_tensor(a3s[1][:, :, :], a3[:, :, :], f32(a3s[0][:, :, :]), ALU.subtract).then_inc(a3_rdy, 1)

            def products(b, p):
                dve.wait_ge(pv2_rdy, b + 1)
                for i, m_ in enumerate((TMK, TMV, TMR)):
                    dve.wait_ge(km_ps, b * 3 + (i + 1))
                    for k in range(KT):
                        last = V.scalar_tensor_tensor(mixed[:, p, i, k, :], B[2 * i + k][:, :], vec[:, m_, k:k + 1],
                                                      mixed[:, p, i, k, :], ALU.mult, ALU.add)
                    last.then_inc(km_out, 1)

            def wkv(b, p, more=True):
                K_, V_, R_ = (mixed[:, p, i, :, :] for i in range(3))
                dve.wait_ge(km_out, b * 3 + 3)
                go(V.tensor_copy(stt_[:, :, :, 0:1], stt_[:, :, :, BT:BT + 1]))
                for k in range(KT):
                    last = V.tensor_tensor_scan(stt_[:, MX, k, 1:BT + 1], vec[:, W_, k:k + 1].broadcast_to([128, BT]),
                                                K_[:, k, :], stt_[:, MX, k, 0:1], ALU.add, ALU.max)
                go(last)
                V.tensor_tensor(T_[0], prev(MX), now(MX), ALU.subtract).then_inc(ex_w, 1)
                V.tensor_tensor(T_[1], K_, now(MX), ALU.subtract).then_inc(ex_w, 1)
                if more:
                    tokens(b + 1)
                dve.wait_ge(ex_d, b * 4 + 1)
                for k in range(KT):
                    last = V.tensor_tensor_scan(stt_[:, SM, k, 1:BT + 1], tmp[:, 0, k, :], tmp[:, 1, k, :],
                                                stt_[:, SM, k, 0:1], ALU.mult, ALU.add)
                last.then_inc(ex_w, 1)
                dve.wait_ge(ex_d, b * 4 + 2)
                go(V.tensor_tensor(now(LS), now(MX), pq[:, :, :], ALU.add))
                dve.wait_ge(xa_out, b * 32 + 32)
                for k in range(KT):
                    V.scalar_tensor_tensor(tmp[:, 0, k, :], stt_[:, LS, k, 0:BT], vec[:, W_, k:k + 1],
                                           K_[:, k, :], ALU.add, ALU.subtract)
                    last = V.scalar_tensor_tensor(tmp[:, 2, k, :], stt_[:, LS, k, 0:BT], vec[:, U_, k:k + 1],
                                                  K_[:, k, :], ALU.subtract, ALU.subtract)
                go(last)
                V.tensor_scalar(T_[1], T_[0], 0.0, None, ALU.max)
                V.tensor_scalar(T_[3], T_[2], 0.0, None, ALU.max)
                go(V.tensor_scalar(T_[0], T_[0], 0.0, None, ALU.min))
                V.tensor_scalar(T_[2], T_[2], 0.0, None, ALU.min).then_inc(ex_w, 1)
                if more:
                    split(b + 1, 1 - p)
                dve.wait_ge(ex_d, b * 4 + 3)
                V.tensor_tensor(DN, T_[2], T_[3], ALU.add).then_inc(dn_w, 1)
                dve.wait_ge(ex_d, b * 4 + 4)
                go(V.tensor_tensor(pq[:, :, :], T_[1], V_, ALU.mult))
                for k in range(KT):
                    last = V.tensor_tensor_scan(stt_[:, AV, k, 1:BT + 1], tmp[:, 0, k, :], pq[:, k, :],
                                                stt_[:, AV, k, 0:1], ALU.mult, ALU.add)
                go(last)
                V.tensor_tensor(T_[0], T_[2], prev(AV), ALU.mult)
                go(V.tensor_tensor(T_[1], T_[3], V_, ALU.mult))
                if more:
                    products(b + 1, 1 - p)
                go(V.tensor_tensor(T_[0], T_[0], T_[1], ALU.add))
                dve.wait_ge(dn_d, b + 1)
                go(V.tensor_tensor(T_[0], T_[0], DN, ALU.mult))
                dve.wait_ge(sg_d, b + 1)
                go(V.tensor_tensor(T_[0], T_[0], R_, ALU.mult))
                go(V.tensor_tensor(T_[2], T_[0], Z2[:, p, :, 1:BT + 1], ALU.add))
                V.tensor_tensor(T_[3], T_[2], x2T[:, p, :, :], ALU.add).then_inc(xa_rdy, 1)

            tokens(0)
            statistics(1)
            split(0, 0)
            products(0, 0)
            wkv(0, 0)
            statistics(2)
            wkv(1, 1)
            wkv(2, 0)
            statistics(3)
            with dve.Fori(0, NB // 2 - 2) as t:
                go.turn(t, 2 * 13)
                wkv(t * 2 + 3, 1)
                wkv(t * 2 + 4, 0)
                go.end(NB // 2 - 2)
            wkv(NB - 1, 1, more=False)

        @block.scalar
        def _(act):
            A_ = nc.scalar
            act.sem_inc(xa_out, 32)
            batches = (0, CPB, 2 * CPB, NC // 2, NC)

            def statistics(n):
                cs = slice(batches[n], batches[n + 1])
                for i in range(2):
                    act.wait_ge(sq_rdy, SQ + 2 * n + i + 1)
                    A_.activation(small[:, 2 * i, cs], small[:, 2 * i, cs], ACT.Sqrt).then_inc(sq_done, 1)

            def blocks_T(b, p, first=False):
                if first:
                    act.wait_ge(z0_ps, 1)
                    A_.activation(Z2[:, 0, :, 0:1], B[6][:, 0:256].rearrange("p (k n) -> p k n", k=KT)[:, :, 0:1], ACT.Copy)
                else:
                    act.wait_ge(zt_rdy, b)
                    A_.activation(Z2[:, p, :, 0:1], Z2[:, 1 - p, :, BT:BT + 1], ACT.Copy)
                act.wait_ge(tk_free, b * CPB + (CPB + 2))
                for k in range(KT):
                    A_.activation(a3[:, k, :], B[4 + k][:, :], ACT.Identity, bias=vec[:, B1, k:k + 1], scale=vec[:, G1, k:k + 1])
                for k in range(KT):
                    A_.activation(x2T[:, p, k, :], B[k][:, :], ACT.Copy)
                A_.activation(Z2[:, p, 0, 1:BT + 1], B[2][:, :], ACT.Copy)
                A_.activation(Z2[:, p, 1, 1:BT + 1], B[3][:, :], ACT.Copy).then_inc(zt_rdy, 1)
                act.wait_ge(zt_rdy, b + 1)
                for i, q_ in enumerate((QMK, QMV, QMR)):
                    for k in range(KT):
                        last = A_.activation(mixed[:, p, i, k, :], Z2[:, p, k, 0:BT], ACT.Copy, scale=vec[:, q_, k:k + 1])
                last.then_inc(pv2_rdy, 1)

            def copies(b):
                for j in range(CPB):
                    c = b * CPB + j
                    act.wait_ge(tk_free, c + 1)
                    A_.activation(tk[:, j % 2, 0, :], x_tok[:, ds(c, 1), :].rearrange("p o d -> p (o d)"),
                                  ACT.Copy).then_inc(tx_rdy, 1)

            def r_gate(b, p):
                act.wait_ge(km_out, b * 3 + 3)
                A_.activation(mixed[:, p, 2, :, :], mixed[:, p, 2, :, :], ACT.Sigmoid).then_inc(sg_d, 1)

            def wkv(b, p, more=True):
                act.wait_ge(ex_w, b * 4 + 1)
                for k in range(KT):
                    A_.activation(tmp[:, 0, k, :], tmp[:, 0, k, :], ACT.Exp, bias=vec[:, W_, k:k + 1])
                act.wait_ge(ex_w, b * 4 + 2)
                A_.activation(tmp[:, 1, :, :], tmp[:, 1, :, :], ACT.Exp).then_inc(ex_d, 1)
                if more:
                    copies(b + 1)
                act.wait_ge(ex_w, b * 4 + 3)
                A_.activation(pq[:, :, :], stt_[:, SM, :, 1:BT + 1], ACT.Ln, bias=epsv[:, 0:1]).then_inc(ex_d, 1)
                if more:
                    blocks_T(b + 1, 1 - p)
                act.wait_ge(ex_w, b * 4 + 4)
                A_.activation(tmp[:, 2, :, :], tmp[:, 2, :, :], ACT.Exp)
                A_.activation(tmp[:, 3, :, :], tmp[:, 3, :, :], ACT.Exp, scale=-1.0).then_inc(ex_d, 1)
                A_.activation(tmp[:, 1, :, :], tmp[:, 1, :, :], ACT.Exp, scale=-1.0)
                A_.activation(tmp[:, 0, :, :], tmp[:, 0, :, :], ACT.Exp).then_inc(ex_d, 1)
                act.wait_ge(dn_w, b + 1)
                A_.activation(den[:, :, :], den[:, :, :], ACT.Ln, bias=epsv[:, 0:1]).then_inc(dn_l, 1)
                act.wait_ge(dn_l, b + 1)
                A_.activation(den[:, :, :], den[:, :, :], ACT.Exp, scale=-1.0).then_inc(dn_d, 1)
                if more:
                    r_gate(b + 1, 1 - p)

            statistics(0)
            copies(0)
            blocks_T(0, 0, True)
            statistics(1)
            r_gate(0, 0)
            wkv(0, 0)
            statistics(2)
            wkv(1, 1)
            wkv(2, 0)
            statistics(3)
            with act.Fori(0, NB // 2 - 2) as t:
                wkv(t * 2 + 3, 1)
                wkv(t * 2 + 4, 0)
            wkv(NB - 1, 1, more=False)

        @block.tensor
        def _(pe):
            T = nc.tensor
            pe.wait_ge(tk_rdy, 1)
            for k in range(KT):
                last = T.transpose(B[6][:, k * 128:(k + 1) * 128], tk[:, 0, 1, k * 128:(k + 1) * 128], ident[:, :])
            last.then_inc(z0_ps, 1)
            pe.wait_ge(z0_ps, 1)
            pe.sem_inc(tk_free, 2)
            pe.wait_ge(wts_rdy, 1)
            with pe.Fori(0, NB) as b:
                for j in range(CPB):
                    pe.wait_ge(tx_rdy, b * CPB + (j + 1))
                    pe.wait_ge(tk_rdy, b * CPB + (j + 2))
                    for a in range(3):
                        for k in range(KT):
                            last = T.transpose(B[2 * a + k][:, j * CH:(j + 1) * CH], tk[:, j % 2, a, k * 128:(k + 1) * 128],
                                               ident[:, :])
                    last.then_inc(tk_free, 1)
                pe.wait_ge(a3_rdy, b + 1)
                for i in range(3):
                    for mk in range(KT):
                        m = i * KT + mk
                        for k in range(KT):
                            last = mm3(B[m][:, :], [w[:, k, m * 128:(m + 1) * 128] for w in wtm],
                                       [x[:, k, :] for x in a3s], k == 0, k == KT - 1)
                    last.then_inc(km_ps, 1)
                pe.wait_ge(km_out, b * 3 + 3)

        pblk.close()
        pc.close()
        KH = HID // 128
        pd = ctx.enter_context(ExitStack())
        IN = sb("IN", [128, 2, 3, KT, BT], to=pd)
        sq = sb("sq", [128, KT, BT], to=pd)
        rs = sb("rs", [128, BT], to=pd)
        XN = sb("XN", [128, KT, BT], to=pd)
        XNs = [sb(f"XN{h}", [128, KT, BT], f32r, to=pd) for h in "hl"]
        kx = sb("kx", [128, KT, BT], to=pd)
        rr = sb("rr", [128, 2, KT, BT], to=pd)
        kq = sb("kq", [128, 2, KT, BT], to=pd)
        kh = [sb(f"kh{h}", [128, KH, BT], f32r, to=pd) for h in "hl"]
        x3b = sb("x3b", [128, 2, KT, BT], to=pd)
        csx_ld = [sem(f"residual_block_loaded_{q}") for q in range(2)]
        cin_ld, avg_rdy = [sem(f"channel_block_loaded_{q}") for q in range(2)], sem("means_weight_ready")
        mean_ps, xc_rdy, sqr_rdy, var_ps, rs_rdy, xn_rdy, rr_rdy, rr_d = (
            sem("mean_in_psum"), sem("centred"), sem("squares_ready"), sem("variance_in_psum"), sem("deviation_ready"),
            sem("xn_split"), sem("r_ready"), sem("r_sigmoid_done"))
        xn_f, xn_hi, pv_rdy, kq_sq, kk_hi = (sem("xn_ready"), sem("xn_high_part"), sem("previous_token_parts"),
                                             sem("key_squared"), sem("key_high_part"))
        cm_ps, kk_tk, kk_rdy, cp_ps, x3_rdy, x3_out = (sem("key_in_psum"), sem("key_taken"), sem("key_split"),
                                                       sem("value_in_psum"), sem("x3_ready"),
                                                       [sem(f"x3_stored_{q}") for q in range(2)])
        pblk = ctx.enter_context(ExitStack())
        block = pblk.enter_context(nc.Block())

        @block.sync
        def _(sp):
            xa, sx, x3 = byk(xa_d), byk(sx_d), byk(x3_d)

            def load(b, q, first=False):
                sp.dma_start(IN[:, q, 0, :, :], xa[:, :, ds(b * BT, BT)]).then_inc(cin_ld[q], 16)
                if first:
                    sp.dma_start(IN[:, q, 1, :, 1:BT], xa[:, :, 0:BT - 1]).then_inc(cin_ld[q], 16)
                    with nc.allow_non_contiguous_dma(reason="one column of 256 channels"):
                        sp.dma_start(IN[:, q, 1, :, 0:1], xa[:, :, S - 1:S]).then_inc(cin_ld[q], 16)
                else:
                    sp.dma_start(IN[:, q, 1, :, :], xa[:, :, ds(b * BT - 1, BT)]).then_inc(cin_ld[q], 16)

            def load_sum(b, q):
                sp.dma_start(IN[:, q, 2, :, :], sx[:, :, ds(b * BT, BT)]).then_inc(csx_ld[q], 16)

            load(0, 0, True)
            load(1, 1)
            for q in range(2):
                load_sum(q, q)

            def store(t, q):
                b = t * 2 + q
                sp.wait_ge(x3_rdy, b + 1)
                sp.dma_start(x3[:, :, ds(b * BT, BT)], x3b[:, q, :, :]).then_inc(x3_out[q], 16)

            with sp.Fori(0, NB // 2 - 1) as t:
                for q in range(2):
                    sp.wait_ge(xn_f, t * 2 + (q + 1))
                    sp.wait_ge(pv_rdy, t * 2 + (q + 1))
                    load(t * 2 + (q + 2), q)
                    store(t, q)
                    load_sum(t * 2 + (q + 2), q)
            for q in range(2):
                store(NB // 2 - 1, q)
                sp.wait_ge(x3_out[q], 16 * (NB // 2) + 16)
        @block.vector
        def _(dve):
            V = nc.vector
            go = steps.on(dve)
            one = lambda a: a.rearrange("p (o n) -> p o n", o=1).broadcast_to([128, KT, BT])
            flat = lambda a: a.rearrange("p k n -> p (k n)")
            go(V.memset(avg[:, :], 1.0 / D))
            dve.sem_inc(avg_rdy, 1)

            def centre(b, q):
                dve.wait_ge(mean_ps, b + 1)
                V.tensor_tensor(IN[:, q, 0, :, :], IN[:, q, 0, :, :], one(B[0][:, :]), ALU.subtract).then_inc(xc_rdy, 1)

            def scale(b, q):
                xin = IN[:, q, 0, :, :]
                dve.wait_ge(rs_rdy, b + 1)
                go(V.reciprocal(rs[:, :], rs[:, :]))
                go(V.tensor_tensor(xin, xin, one(rs[:, :]), ALU.mult))
                for k in range(KT):
                    last = V.tensor_scalar(XN[:, k, :], xin[:, k, :], vec[:, G2, k:k + 1], vec[:, B2, k:k + 1],
                                           ALU.mult, ALU.add)
                last.then_inc(xn_f, 1)
                dve.wait_ge(xn_f, b + 1)
                dve.wait_ge(pv_rdy, b + 1)
                for k in range(KT):
                    last = V.scalar_tensor_tensor(rr[:, q, k, :], XN[:, k, :], vec[:, CMR, k:k + 1], rr[:, q, k, :],
                                                  ALU.mult, ALU.add)
                last.then_inc(rr_rdy, 1)
                dve.wait_ge(xn_hi, b + 1)
                V.tensor_tensor(XNs[1][:, :, :], XN[:, :, :], f32(XNs[0][:, :, :]), ALU.subtract).then_inc(xn_rdy, 1)

            def low(b, m):
                i = m // 2
                dve.wait_ge(kk_hi, b * (KH // 2) + (i + 1))
                V.tensor_tensor(kh[1][:, m:m + 2, :], kq[:, i % 2, :, :], f32(kh[0][:, m:m + 2, :]),
                                ALU.subtract).then_inc(kk_rdy, 1)

            def turn(t, q, b, more=True):
                for m in range(0, KH, 2):
                    i = m // 2
                    if i > 1:
                        dve.wait_ge(kk_rdy, b * (KH // 2) + (i - 1))
                    for k in range(2):
                        dve.wait_ge(cm_ps, b * KH + (m + k + 1))
                        V.scalar_tensor_tensor(kq[:, i % 2, k, :], B[2 + (m + k) % 4][:, :], vec[:, CMK, k:k + 1],
                                               kx[:, k, :], ALU.mult, ALU.add).then_inc(kk_tk, 1)
                    dve.wait_ge(kk_tk, b * KH + (m + 2 + 4))
                    k_ = flat(kq[:, i % 2, :, :])
                    V.scalar_tensor_tensor(k_, k_, 0.0, k_, ALU.max, ALU.mult).then_inc(kq_sq, 1)
                    if m > 0:
                        low(b, m - 2)
                    if m == 2 and more:
                        centre(b + 1, 1 - q)
                low(b, KH - 2)
                if more:
                    scale(b + 1, 1 - q)
                dve.wait_ge(rr_d, b + 1)
                dve.wait_ge(cp_ps, b + 1)
                dve.wait_ge(x3_out[q], t * 16 + 16)
                for k in range(KT):
                    last = V.tensor_tensor(rr[:, q, k, :], B[6 + k][:, :], rr[:, q, k, :], ALU.mult)
                go(last)
                dve.wait_ge(csx_ld[q], t * 16 + 16)
                V.tensor_tensor(x3b[:, q, :, :], rr[:, q, :, :], IN[:, q, 2, :, :], ALU.add).then_inc(x3_rdy, 1)

            centre(0, 0)
            scale(0, 0)
            with dve.Fori(0, NB // 2 - 1) as t:
                go.turn(t, 2 * 3)
                for q in range(2):
                    turn(t, q, t * 2 + q)
                go.end(NB // 2 - 1)
            for q in range(2):
                turn(NB // 2 - 1, q, NB - 2 + q, more=q == 0)

        @block.gpsimd
        def _(pool):
            def parts(b, q, loaded):
                pool.wait_ge(cin_ld[q], loaded)
                pool.wait_ge(kk_tk, b * KH + 4)
                wide = lambda n: vec[:, n, :].rearrange("p (k o) -> p k o", o=1).broadcast_to([128, KT, BT])
                nc.gpsimd.tensor_tensor(kx[:, :, :], IN[:, q, 1, :, :], wide(QCK), ALU.mult)
                nc.gpsimd.tensor_tensor(rr[:, q, :, :], IN[:, q, 1, :, :], wide(QCR), ALU.mult).then_inc(pv_rdy, 1)

            with pool.Fori(0, NB // 2) as t:
                for q in range(2):
                    parts(t * 2 + q, q, t * 32 + (48 - 16 * q))

        @block.scalar
        def _(act):
            A_ = nc.scalar
            for q in range(2):
                act.sem_inc(x3_out[q], 16)
            act.sem_inc(kk_tk, 4)

            def gate(b, q, first=False):
                act.wait_ge(var_ps, b + 1)
                A_.activation(rs[:, :], B[1][:, :], ACT.Sqrt, bias=epsv[:, 1:2]).then_inc(rs_rdy, 1)
                act.wait_ge(xn_f, b + 1)
                if not first:
                    act.wait_ge(cm_ps, b * KH)
                A_.activation(XNs[0][:, :, :], XN[:, :, :], ACT.Copy).then_inc(xn_hi, 1)
                act.wait_ge(rr_rdy, b + 1)
                A_.activation(rr[:, q, :, :], rr[:, q, :, :], ACT.Sigmoid).then_inc(rr_d, 1)

            def square(b, q):
                act.wait_ge(xc_rdy, b + 1)
                A_.activation(sq[:, :, :], IN[:, q, 0, :, :], ACT.Square).then_inc(sqr_rdy, 1)

            def turn(b, q, more=True):
                for m in range(0, KH, 2):
                    act.wait_ge(kq_sq, b * (KH // 2) + (m // 2 + 1))
                    A_.activation(kh[0][:, m:m + 2, :], kq[:, (m // 2) % 2, :, :], ACT.Copy).then_inc(kk_hi, 1)
                    if m == 2 and more:
                        square(b + 1, 1 - q)
                if more:
                    gate(b + 1, 1 - q)

            square(0, 0)
            gate(0, 0, first=True)
            with act.Fori(0, NB // 2 - 1) as t:
                for q in range(2):
                    turn(t * 2 + q, q)
            for q in range(2):
                turn(NB - 2 + q, q, more=q == 0)

        @block.tensor
        def _(pe):
            def mean(b, q, loaded):
                pe.wait_ge(cin_ld[q], loaded)
                for k in range(KT):
                    last = nc.tensor.matmul(B[0][:, :], avg[:, :], IN[:, q, 0, k, :], start=(k == 0), stop=(k == KT - 1))
                last.then_inc(mean_ps, 1)

            def variance(b, q):
                pe.wait_ge(sqr_rdy, b + 1)
                for k in range(KT):
                    last = nc.tensor.matmul(B[1][:, :], avg[:, :], sq[:, k, :], start=(k == 0), stop=(k == KT - 1))
                last.then_inc(var_ps, 1)

            def turn(t, q, b, more=True):
                pe.wait_ge(xn_rdy, b + 1)
                for m in range(KH):
                    pe.wait_ge(kk_tk, b * KH + (m + 1))
                    for k in range(KT):
                        last = mm3(B[2 + m % 4][:, :], [w[:, k, m * 128:(m + 1) * 128] for w in wcm],
                                   [x[:, k, :] for x in XNs], k == 0, k == KT - 1)
                    last.then_inc(cm_ps, 1)
                    if m == 5 and more:
                        variance(b + 1, 1 - q)
                    if m == 2 and more:
                        mean(b + 1, 1 - q, t * 32 + (32 if q == 0 else 80))
                for k in range(KH):
                    if k % 2 == 0:
                        pe.wait_ge(kk_rdy, b * (KH // 2) + (k // 2 + 1))
                    for m in range(KT):
                        last = mm3(B[6 + m][:, :], [w[:, k, m * 128:(m + 1) * 128] for w in wcp],
                                   [h[:, k, :] for h in kh], k == 0, k == KH - 1)
                last.then_inc(cp_ps, 1)

            pe.wait_ge(avg_rdy, 1)
            mean(0, 0, 48)
            variance(0, 0)
            with pe.Fori(0, NB // 2 - 1) as t:
                for q in range(2):
                    turn(t, q, t * 2 + q)
            for q in range(2):
                turn(NB // 2 - 1, q, NB - 2 + q, more=q == 0)

        pblk.close()
        pd.close()
        pw_.close()
        px.close()
        pe_ = ctx.enter_context(ExitStack())
        names = (("w1", KT, HID), ("w2", KT, HID), ("h1", KH, HID), ("h2", KH, HID), ("w3", KH, D))
        FW = {n: sb("ffn_" + n, [128, k, c], f32r, to=pe_) for n, k, c in names}
        scl = sb("scl", [128, 4 * KH + KT], to=pe_)
        x3i = sb("x3i", [128, 2, KT, BT], to=pe_)
        sq2 = sb("sq2", [128, KT, BT], to=pe_)
        rs2 = sb("rs2", [128, BT], to=pe_)
        xc = sb("xc", [128, KT, BT], to=pe_)
        fT = [sb(f"fT{h}", [128, KT, BT], f32r, to=pe_) for h in "hl"]
        hA = [sb(f"hA{h}", [128, KH, BT], f32r, to=pe_) for h in "hl"]
        hB = [sb(f"hB{h}", [128, KH, BT], f32r, to=pe_) for h in "hl"]
        gq = sb("gq", [128, 4, BT], to=pe_)
        outb = sb("outb", [128, KT, BT], to=pe_)
        flg = sb("flg", [128, 1], to=pe_)
        flr = sb("flr", [1, 2], i32, to=pe_)
        fw_ld = {n: sem("ffn_loaded_" + n) for n in ("w1", "h1", "h2", "w3")}
        fw_ld["w2"] = fw_ld["w1"]
        sc_ld, x3_ld = sem("ffn_scales_loaded"), [sem(f"x3_loaded_{q}") for q in range(2)]
        low_bits = sem("low_bits_steps")
        m2_ps, c2_rdy, s2_rdy, v2_ps, r2_rdy, f_rdy2 = (sem("ffn_mean_in_psum"), sem("ffn_centred"), sem("ffn_squares"),
                                                       sem("ffn_variance_in_psum"), sem("ffn_deviation"), sem("f_split"))
        bk_ps, g_act, h_spl, bk_free, o_ps, o_rdy2, o_out = (
            sem("bank_filled"), sem("activation_done"), sem("hidden_split"), sem("bank_free"), sem("out_in_psum"),
            sem("out_ready"), sem("out_stored"))
        a_rdy = sem("gate_ready")
        pblk = ctx.enter_context(ExitStack())
        block = pblk.enter_context(nc.Block())
        off = dict(w1=0, w2=KH, h1=2 * KH, h2=3 * KH, w3=4 * KH)

        @block.sync
        def _(sp):
            sp.wait_ge(cp_w, 16 * len(names))
            sp.dma_start(scl[:, :], A["scales"]).then_inc(sc_ld, 16)
            x3 = byk(x3_d)
            for q in range(2):
                sp.dma_start(x3i[:, q, :, :], x3[:, :, q * BT:(q + 1) * BT]).then_inc(x3_ld[q], 16)
            for n, k, c in names:
                sp.dma_start(f32(FW[n][:, :, :]), raw[n].rearrange("(k p) n -> p k n", p=128)).then_inc(fw_ld[n], 16)

            def store(b):
                sp.wait_ge(o_rdy2, b + 1)
                sp.dma_start(byk(A["out"])[:, :, ds(b * BT, BT)], outb[:, :, :]).then_inc(o_out, 16)

            with sp.Fori(0, NB // 2 - 1) as t:
                for q in range(2):
                    b = t * 2 + q
                    store(b)
                    sp.dma_start(x3i[:, q, :, :], x3[:, :, ds((b + 2) * BT, BT)]).then_inc(x3_ld[q], 16)
            for q in range(2):
                store(NB - 2 + q)
            sp.wait_ge(o_out, 16 * NB + 16)

        @block.vector
        def _(dve):
            V = nc.vector
            go = steps.on(dve)
            dve.sem_inc(o_out, 16)
            dve.wait_ge(sc_ld, 16)
            V.tensor_reduce(flg[:, :], lowb[:, :], AX.X, ALU.add).then_inc(low_bits, 1)
            dve.wait_ge(low_bits, 2)
            V.tensor_scalar(flr[0:1, 0:1], B[7][0:1, 0:1], 0.0, None, ALU.is_gt).then_inc(low_bits, 1)
            one = lambda a: a.rearrange("p (o n) -> p o n", o=1).broadcast_to([128, KT, BT])

            def split(dst, m, b, layer):
                src = gq[:, m % 4:m % 4 + 2, :]
                go(V.tensor_copy(dst[0][:, m:m + 2, :], src))
                V.tensor_tensor(dst[1][:, m:m + 2, :], src, f32(dst[0][:, m:m + 2, :]), ALU.subtract).then_inc(h_spl, 1)

            def centre(b, q):
                dve.wait_ge(m2_ps, b + 1)
                V.tensor_tensor(xc[:, :, :], x3i[:, q, :, :], one(B[0][:, :]), ALU.subtract).then_inc(c2_rdy, 1)

            def scale(b):
                dve.wait_ge(r2_rdy, b + 1)
                go(V.reciprocal(rs2[:, :], rs2[:, :]))
                go(V.tensor_tensor(xc[:, :, :], xc[:, :, :], one(rs2[:, :]), ALU.mult))
                go(V.tensor_copy(fT[0][:, :, :], xc[:, :, :]))
                V.tensor_tensor(fT[1][:, :, :], xc[:, :, :], f32(fT[0][:, :, :]), ALU.subtract).then_inc(f_rdy2, 1)

            def turn(t, following):
                for q in range(2):
                    b = t * 2 + q
                    x_ = x3i[:, q, :, :]
                    more = q == 0 or following
                    for m in range(0, KH, 2):
                        for k in range(2):
                            dve.wait_ge(a_rdy, b * KH + (m + k + 1))
                            last = V.scalar_tensor_tensor(gq[:, (m + k) % 4, :], B[3 + 2 * ((m + k) % 2)][:, :],
                                                          scl[:, off["w2"] + m + k:off["w2"] + m + k + 1],
                                                          gq[:, (m + k) % 4, :], ALU.mult, ALU.mult)
                            last.then_inc(bk_free, 1)
                        dve.wait_ge(bk_free, b * (3 * KH) + (m + 2 + 4))
                        go(V.tensor_copy(hA[0][:, m:m + 2, :], gq[:, m % 4:m % 4 + 2, :]))
                        go(V.tensor_tensor(hA[1][:, m:m + 2, :], gq[:, m % 4:m % 4 + 2, :], f32(hA[0][:, m:m + 2, :]), ALU.subtract))
                        dve.sem_inc(h_spl, 1)
                    if more:
                        centre(b + 1, 1 - q)
                    for layer, dst in ((1, hB), (2, hA)):
                        for m in range(0, KH, 2):
                            dve.wait_ge(g_act, b * (2 * KH) + ((layer - 1) * KH + m + 2))
                            split(dst, m, b, layer)
                            if more and layer == 1 and m == 4:
                                scale(b + 1)
                    dve.wait_ge(o_ps, b + 1)
                    dve.wait_ge(o_out, b * 16 + 16)
                    for k in range(KT):
                        last = V.scalar_tensor_tensor(outb[:, k, :], B[6 + k][:, :],
                                                      scl[:, off["w3"] + k:off["w3"] + k + 1], x_[:, k, :],
                                                      ALU.mult, ALU.add)
                    last.then_inc(o_rdy2, 1)
                    dve.wait_ge(o_rdy2, b + 1)

            centre(0, 0)
            scale(0)
            with dve.Fori(0, NB // 2 - 1) as t:
                go.turn(t, 2 * (3 + 4 * 2 + 4 + 4))
                turn(t, True)
                go.end(NB // 2 - 1)
            turn(NB // 2 - 1, False)

        @block.scalar
        def _(act):
            A_ = nc.scalar
            act.sem_inc(bk_free, 4)
            act.wait_ge(sc_ld, 16)
            HS = 12

            def square(b):
                act.wait_ge(c2_rdy, b + 1)
                A_.activation(sq2[:, :, :], xc[:, :, :], ACT.Square).then_inc(s2_rdy, 1)

            def deviation(b):
                act.wait_ge(v2_ps, b + 1)
                A_.activation(rs2[:, :], B[1][:, :], ACT.Sqrt, bias=epsv[:, 1:2]).then_inc(r2_rdy, 1)

            def turn(t, following):
                for q in range(2):
                    b = t * 2 + q
                    more = q == 0 or following
                    for m in range(KH):
                        act.wait_ge(bk_ps, b * (3 * KH) + (m + 1))
                        if m >= 4:
                            act.wait_ge(h_spl, b * HS + ((m - 4) // 2 + 1))
                        A_.activation(gq[:, m % 4, :], B[2 + 2 * (m % 2)][:, :], ACT.Silu,
                                      scale=scl[:, off["w1"] + m:off["w1"] + m + 1]).then_inc(a_rdy, 1)
                    if more:
                        square(b + 1)
                    for layer, nm in ((1, "h1"), (2, "h2")):
                        for m in range(KH):
                            act.wait_ge(bk_ps, b * (3 * KH) + (layer * KH + m + 1))
                            act.wait_ge(h_spl, b * HS + (layer * 4 + (m - 4) // 2 + 1))
                            A_.activation(gq[:, m % 4, :], B[2 + m % 4][:, :], ACT.Gelu,
                                          scale=scl[:, off[nm] + m:off[nm] + m + 1]).then_inc(g_act, 1)
                            act.wait_ge(g_act, b * (2 * KH) + ((layer - 1) * KH + m + 1))
                            act.sem_inc(bk_free, 1)
                            if more and layer == 1 and m == 4:
                                deviation(b + 1)

            square(0)
            deviation(0)
            with act.Fori(0, NB // 2 - 1) as t:
                turn(t, True)
            turn(NB // 2 - 1, False)

        @block.tensor
        def _(pe):
            T = nc.tensor
            pe.wait_ge(low_bits, 1)
            T.matmul(B[7][:, 0:1], one_m[:, :], flg[:, :], start=True, stop=True).then_inc(low_bits, 1)
            pe.wait_ge(low_bits, 3)
            flag = pe.alloc_register("low_bits")
            pe.reg_load(flag, flr[0:1, 0:1])

            def norm(b, q, src, rdy, bk, out):
                if rdy is not None:
                    pe.wait_ge(rdy, b + 1)
                for k in range(KT):
                    last = T.matmul(B[bk][:, :], avg[:, :], src[:, k, :], start=(k == 0), stop=(k == KT - 1))
                last.then_inc(out, 1)

            def mean(b, q):
                pe.wait_ge(x3_ld[q], (b - q) * 8 + 16)
                norm(b, q, x3i[:, q, :, :], None, 0, m2_ps)

            def variance(b, q):
                norm(b, q, sq2, s2_rdy, 1, v2_ps)

            def block_of(b, q, exact, more):
                def mm(out, w, x, first, last):
                    if exact:
                        T.matmul(out, w, x[0], start=first, stop=False)
                        return T.matmul(out, w, x[1], start=False, stop=last)
                    T.matmul(out, f32(w), f32(x[0]), start=first, stop=False)
                    return T.matmul(out, f32(w), f32(x[1]), start=False, stop=last)

                pe.wait_ge(f_rdy2, b + 1)
                pe.wait_ge(fw_ld["w1"], 32)
                HS = 12
                for m in range(KH):
                    pe.wait_ge(bk_free, b * (3 * KH) + (m + 3))
                    for n, nm in enumerate(("w1", "w2")):
                        for k in range(KT):
                            last = mm(B[2 + 2 * (m % 2) + n][:, :], FW[nm][:, k, m * 128:(m + 1) * 128],
                                      [f[:, k, :] for f in fT], k == 0, k == KT - 1)
                    last.then_inc(bk_ps, 1)
                if more:
                    mean(b + 1, 1 - q)
                for layer, nm, src in ((1, "h1", hA), (2, "h2", hB)):
                    pe.wait_ge(fw_ld[nm], 16)
                    for m in range(KH):
                        pe.wait_ge(bk_free, b * (3 * KH) + (KH + 3 + m // 2 if layer == 1 and m < 4 else layer * KH + m + 1))
                        for k in range(KH):
                            if m == 0 and k % 2 == 0:
                                pe.wait_ge(h_spl, b * HS + ((layer - 1) * 4 + k // 2 + 1))
                            last = mm(B[2 + m % 4][:, :], FW[nm][:, k, m * 128:(m + 1) * 128],
                                      [h[:, k, :] for h in src], k == 0, k == KH - 1)
                        last.then_inc(bk_ps, 1)
                        if more and layer == 1 and m == 3:
                            variance(b + 1, 1 - q)
                pe.wait_ge(fw_ld["w3"], 16)
                for k in range(KH):
                    if k % 2 == 0:
                        pe.wait_ge(h_spl, b * HS + (8 + k // 2 + 1))
                    for m in range(KT):
                        last = mm(B[6 + m][:, :], FW["w3"][:, k, m * 128:(m + 1) * 128],
                                  [h[:, k, :] for h in hA], k == 0, k == KH - 1)
                last.then_inc(o_ps, 1)

            def blocks(exact):
                with pe.Fori(0, NB // 2 - 1) as t:
                    for q in range(2):
                        block_of(t * 2 + q, q, exact, True)
                for q in range(2):
                    block_of(NB - 2 + q, q, exact, q == 0)

            mean(0, 0)
            variance(0, 0)
            with pe.If_eq(flag, 0):
                blocks(True)
            with pe.Else():
                blocks(False)

        pblk.close()
        pe_.close()


def layout(I):
    import numpy as np
    g = lambda n: np.asarray(I[n])
    t = lambda n: np.ascontiguousarray(g(n).T)
    out = {
        "x": g("L0_attn_x"),
        "wcatT": np.ascontiguousarray(np.concatenate([g("L0_attn_Wk"), g("L0_attn_Wv"), g("L0_attn_Wq"), g("L0_attn_pw")], 0).T),
        "wvT": t("L0_attn_Wv"), "ir1T": t("L0_attn_ir_w1"), "ir2T": t("L0_attn_ir_w2"),
        "nm1T": t("L0_attn_nm_w1"), "nm2T": t("L0_attn_nm_w2"), "woT": t("L0_attn_Wo"), "wroT": g("L0_ffn_w_router"),
        "ir_b1": g("L0_attn_ir_b1"), "ir_b2": g("L0_attn_ir_b2"), "nm_b1": g("L0_attn_nm_b1"), "nm_b2": g("L0_attn_nm_b2"),
        "norm_w": g("L0_attn_norm_w"),
        "fast_alpha": g("L0_attn_fast_alpha").reshape(1), "slow_alpha": g("L0_attn_slow_alpha").reshape(1),
    }
    out.update({"w1": g("L0_ffn_w1"), "w2": g("L0_ffn_w2"), "b1T": np.ascontiguousarray(g("L0_ffn_b1").reshape(NE * HID // 128, 128).T), "b2": g("L0_ffn_b2")})
    vk = lambda n: np.ascontiguousarray(g("L1_attn_" + n).reshape(KT, 128).T)
    for n in ("time_decay", "time_first", "tmk", "tmv", "tmr", "g1", "g2", "cmk", "cmr"):
        out[n] = vk(n)
    out["b1v"], out["b2v"] = vk("b1"), vk("b2")
    for n in ("W_tm", "W_cm", "W_cp"):
        out[n] = g("L1_attn_" + n)
    col = lambda n: g("L1_ffn_" + n).reshape(-1, 128).T
    out["scales"] = np.ascontiguousarray(np.concatenate([col(n) for n in ("w1_s", "w2_s", "h1_s", "h2_s", "w3_s")], 1))
    for n in ("w1", "w2", "h1", "h2", "w3"):
        out["ffn_" + n] = t("L1_ffn_" + n + "_w")
    return out


def kernel(**inputs):
    import numpy as np
    import concourse.bacc as _bacc
    from concourse import mybir as _mybir
    from concourse.bass_utils import run_bass_kernel_spmd as _run

    nc = _bacc.Bacc("TRN2", target_bir_lowering=False, num_devices=1)
    arrays, A = {}, {}
    for name, a in layout(inputs).items():
        arrays[f"in_{name}_dram"] = a
        A[name] = nc.dram_tensor(f"in_{name}_dram", a.shape, _mybir.dt.from_np(a.dtype), kind="ExternalInput").ap()
    A["out"] = nc.dram_tensor("out_0_dram", (D, S), _mybir.dt.float32, kind="ExternalOutput").ap()
    build(nc, A)
    r = _run(nc, [arrays], core_ids=[0])
    return np.ascontiguousarray(np.asarray(r.results[0]["out_0_dram"]).T).reshape(1, S, D)
```
